# Optimizing a Trainium2 kernel written in Bass

```python
import numpy as np
import jax
import jax.numpy as jnp

def _softmax(x, axis=-1):
    return jax.nn.softmax(x, axis=axis)

def _gelu(x):
    return jax.nn.gelu(x, approximate=True)

def _silu(x):
    return jax.nn.silu(x)

def _sigmoid(x):
    return jax.nn.sigmoid(x)

def _layernorm(x, axis=-1, eps=1e-05):
    m = jnp.mean(x, axis=axis, keepdims=True)
    v = jnp.var(x, axis=axis, keepdims=True)
    return (x - m) / jnp.sqrt(v + eps)

def _scatter_add(tgt, idx, src, axis=0):
    return tgt.at[idx].add(src)

def _segment_sum(src, seg, n):
    return jax.ops.segment_sum(src, seg, n)
kernel_name = 'mk_vit_tower_postln_d4_tok_img768_r4_96759a'

def setup_inputs(seed: int=0):
    np.random.seed(seed)
    _w = jnp.asarray

    def _rec_inputs():
        import jax
        import jax.numpy as jnp
        _rk = jax.random.key(seed)
        x = -0.00040386 + 0.999972 * jax.random.normal(jax.random.fold_in(_rk, 1), (64, 64, 64, 3), jnp.float32)
        return x
    x = _rec_inputs()

    def _L0_tok_setup():
        import jax, jax.numpy as jnp
        import numpy as np
        IMG = 64
        PATCH = 16
        C = 3
        D = 192
        NP_ = (IMG // PATCH) ** 2
        B = 64

        def _patchify(x):
            Bn, H, Wd, Cn = x.shape
            hp, wp = (H // PATCH, Wd // PATCH)
            x = x.reshape(Bn, hp, PATCH, wp, PATCH, Cn)
            x = x.transpose(0, 1, 3, 2, 4, 5)
            return x.reshape(Bn, hp * wp, PATCH * PATCH * Cn)
        key = jax.random.key(seed)
        k1, k2, k3 = jax.random.split(key, 3)
        x = jax.random.normal(k1, (B, IMG, IMG, C), dtype=jnp.float32)
        patch_dim = C * PATCH * PATCH
        W = jax.random.normal(k2, (patch_dim, D), dtype=jnp.float32) / np.sqrt(patch_dim)
        b = jnp.zeros((D,), dtype=jnp.float32)
        pos_emb = jax.random.normal(k3, (NP_, D), dtype=jnp.float32) * 0.02
        return {'x': x, 'W': W, 'b': b, 'pos_emb': pos_emb}
    _L0_tok_all = _L0_tok_setup()
    _L0_tok_in = {k: v for k, v in _L0_tok_all.items() if k in ('W', 'b', 'pos_emb')}
    del _L0_tok_all

    def _L0_attn_setup():
        import jax, jax.numpy as jnp
        import numpy as np
        N_HEAD = 12
        key = jax.random.key(seed)
        ks = jax.random.split(key, 6)
        B, T, C = (8, 256, 192)
        x = jax.random.normal(ks[0], (B, T, C), dtype=jnp.float32)
        w_attn = jax.random.normal(ks[1], (C, 3 * C), dtype=jnp.float32) * 0.02
        b_attn = jnp.zeros((3 * C,), dtype=jnp.float32)
        w_proj = jax.random.normal(ks[2], (C, C), dtype=jnp.float32) * 0.02
        b_proj = jnp.zeros((C,), dtype=jnp.float32)
        rel_emb = jax.random.normal(ks[3], (2 * 256 - 1, C // N_HEAD), dtype=jnp.float32) * 0.02
        return {'x': x, 'w_attn': w_attn, 'b_attn': b_attn, 'w_proj': w_proj, 'b_proj': b_proj, 'rel_emb': rel_emb}
    _L0_attn_all = _L0_attn_setup()
    _L0_attn_in = {k: v for k, v in _L0_attn_all.items() if k in ('w_attn', 'b_attn', 'w_proj', 'b_proj', 'rel_emb')}
    del _L0_attn_all

    def _L0_ffn_setup():
        import jax, jax.numpy as jnp
        import numpy as np

        def _fq(x, scale, qmin, qmax):
            q = jnp.clip(jnp.round(x / scale), qmin, qmax) * scale
            return x + jax.lax.stop_gradient(q - x)

        def _quant_weight(W):
            scale = jnp.max(jnp.abs(W)) / 127.0
            return _fq(W, scale, -127.0, 127.0)
        key = jax.random.key(seed)
        ks = jax.random.split(key, 5)
        B, S, D, H = (64, 196, 192, 768)
        x = jax.random.normal(ks[0], (B, S, D), dtype=jnp.float32)
        W1 = jax.random.normal(ks[1], (H, D), dtype=jnp.float32) * D ** (-0.5)
        b1 = jax.random.normal(ks[2], (H,), dtype=jnp.float32) * 0.01
        W2 = jax.random.normal(ks[3], (D, H), dtype=jnp.float32) * H ** (-0.5)
        b2 = jax.random.normal(ks[4], (D,), dtype=jnp.float32) * 0.01
        s_gelu = jnp.float32(0.05)
        s_out = jnp.float32(0.02)
        return {'x': x, 'W1': W1, 'b1': b1, 'W2': W2, 'b2': b2, 's_gelu': s_gelu, 's_out': s_out}
    _L0_ffn_all = _L0_ffn_setup()
    _L0_ffn_in = {k: v for k, v in _L0_ffn_all.items() if k in ('W1', 'b1', 'W2', 'b2', 's_gelu', 's_out')}
    del _L0_ffn_all

    def _L1_attn_setup():
        import jax, jax.numpy as jnp
        import numpy as np
        B, N, C = (8, 256, 192)
        H = 12
        D = C // H
        SCALE = D ** (-0.5)
        EPS = 1e-05

        def _layer_norm(x):
            mean = x.mean(-1, keepdims=True)
            var = ((x - mean) ** 2).mean(-1, keepdims=True)
            return (x - mean) / jnp.sqrt(var + EPS)
        key = jax.random.key(seed)
        k1, k2, k3 = jax.random.split(key, 3)
        x = jax.random.normal(k1, (B, N, C), dtype=jnp.float32)
        qkv_weight = jax.random.normal(k2, (3 * C, C), dtype=jnp.float32) * C ** (-0.5)
        proj_weight = jax.random.normal(k3, (C, C), dtype=jnp.float32) * C ** (-0.5)
        return {'x': x, 'qkv_weight': qkv_weight, 'proj_weight': proj_weight}
    _L1_attn_all = _L1_attn_setup()
    _L1_attn_in = {k: v for k, v in _L1_attn_all.items() if k in ('qkv_weight', 'proj_weight')}
    del _L1_attn_all

    def _L1_ffn_setup():
        import jax, jax.numpy as jnp
        import numpy as np
        DIM = 192
        H = 12
        HD = 64
        SHARED = 2
        ROUTED = 2
        E_ROUTED = H - SHARED
        LN_EPS = 1e-05

        def _layernorm(x, w, b):
            m = x.mean(-1, keepdims=True)
            v = ((x - m) ** 2).mean(-1, keepdims=True)
            return (x - m) * jax.lax.rsqrt(v + LN_EPS) * w + b
        key = jax.random.key(seed)
        ks = jax.random.split(key, 12)
        B, N = (4, 512)
        s = 0.02
        return {'x': jax.random.normal(ks[0], (B, N, DIM), jnp.float32), 'qkv_w': jax.random.normal(ks[1], (DIM, 3 * H * HD), jnp.float32) * s, 'qkv_b': jnp.zeros((3 * H * HD,), jnp.float32), 'q_norm_w': jnp.ones((HD,), jnp.float32), 'q_norm_b': jnp.zeros((HD,), jnp.float32), 'k_norm_w': jnp.ones((HD,), jnp.float32), 'k_norm_b': jnp.zeros((HD,), jnp.float32), 'wg_w': jax.random.normal(ks[2], (DIM, E_ROUTED), jnp.float32) * s, 'wg0_w': jax.random.normal(ks[3], (DIM, 2), jnp.float32) * s, 'wg1_w': jax.random.normal(ks[4], (DIM, SHARED), jnp.float32) * s, 'proj_w': jax.random.normal(ks[5], (H * HD, DIM), jnp.float32) * s, 'proj_b': jnp.zeros((DIM,), jnp.float32)}
    _L1_ffn_all = _L1_ffn_setup()
    _L1_ffn_in = {k: v for k, v in _L1_ffn_all.items() if k in ('qkv_w', 'qkv_b', 'q_norm_w', 'q_norm_b', 'k_norm_w', 'k_norm_b', 'wg_w', 'wg0_w', 'wg1_w', 'proj_w', 'proj_b')}
    del _L1_ffn_all

    def _L2_attn_setup():
        import jax, jax.numpy as jnp
        import numpy as np
        NUM_HEADS = 12
        DIM = 192
        HEAD_DIM = DIM // NUM_HEADS
        B, N = (32, 64)
        key = jax.random.key(seed)
        ks = jax.random.split(key, 8)
        s = 0.02
        return {'x': jax.random.normal(ks[0], (B, N, DIM), dtype=jnp.float32), 'qkv_w': jax.random.normal(ks[1], (3 * DIM, DIM), dtype=jnp.float32) * s, 'qkv_b': jnp.zeros((3 * DIM,), dtype=jnp.float32), 'grassman_scale': jnp.asarray(HEAD_DIM ** (-0.5), dtype=jnp.float32), 'conv_w': jax.random.normal(ks[2], (NUM_HEADS, 2 * NUM_HEADS), dtype=jnp.float32) * s, 'conv_b': jnp.zeros((NUM_HEADS,), dtype=jnp.float32), 'proj_w': jax.random.normal(ks[3], (DIM, DIM), dtype=jnp.float32) * s, 'proj_b': jnp.zeros((DIM,), dtype=jnp.float32)}
    _L2_attn_all = _L2_attn_setup()
    _L2_attn_in = {k: v for k, v in _L2_attn_all.items() if k in ('qkv_w', 'qkv_b', 'grassman_scale', 'conv_w', 'conv_b', 'proj_w', 'proj_b')}
    del _L2_attn_all

    def _L2_ffn_setup():
        import jax, jax.numpy as jnp
        import numpy as np
        B, T, D = (4, 512, 192)
        E, F, K = (8, 4 * 192, 2)
        key = jax.random.key(seed)
        ks = jax.random.split(key, 5)
        s = 0.02
        return {'x': jax.random.normal(ks[0], (B, T, D), dtype=jnp.float32), 'Wg': jax.random.normal(ks[1], (D, E), dtype=jnp.float32) * s, 'bg': jnp.zeros((E,), dtype=jnp.float32), 'W1': jax.random.normal(ks[2], (E, D, F), dtype=jnp.float32) * s, 'b1': jnp.zeros((E, F), dtype=jnp.float32), 'W2': jax.random.normal(ks[3], (E, F, D), dtype=jnp.float32) * s, 'b2': jnp.zeros((E, D), dtype=jnp.float32)}
    _L2_ffn_all = _L2_ffn_setup()
    _L2_ffn_in = {k: v for k, v in _L2_ffn_all.items() if k in ('Wg', 'bg', 'W1', 'b1', 'W2', 'b2')}
    del _L2_ffn_all

    def _L3_attn_setup():
        import jax, jax.numpy as jnp
        import numpy as np
        N_QUBITS = 8
        N_HEADS = 12
        EPS = 1e-08
        key = jax.random.key(seed)
        ks = jax.random.split(key, 8)
        B, S, D = (4, 512, 192)
        scale = 0.02
        return {'x': jax.random.normal(ks[0], (B, S, D), jnp.float32), 'sp_w': jax.random.normal(ks[1], (2 * N_QUBITS, D), jnp.float32) * scale, 'sp_b': jax.random.normal(ks[2], (2 * N_QUBITS,), jnp.float32) * scale, 'in_w': jax.random.normal(ks[3], (3 * D, D), jnp.float32) * scale, 'in_b': jax.random.normal(ks[4], (3 * D,), jnp.float32) * scale, 'out_w': jax.random.normal(ks[5], (D, D), jnp.float32) * scale, 'out_b': jax.random.normal(ks[6], (D,), jnp.float32) * scale, 'qw': jnp.array(0.5, jnp.float32)}
    _L3_attn_all = _L3_attn_setup()
    _L3_attn_in = {k: v for k, v in _L3_attn_all.items() if k in ('sp_w', 'sp_b', 'in_w', 'in_b', 'out_w', 'out_b', 'qw')}
    del _L3_attn_all

    def _L3_ffn_setup():
        import jax, jax.numpy as jnp
        import numpy as np
        B, S, D = (4, 256, 192)
        E = 8
        H = 192
        HS = 768
        TOPK_ROUTED = 2
        key = jax.random.key(seed)
        ks = jax.random.split(key, 10)
        w = lambda k, shape: jax.random.normal(k, shape, dtype=jnp.float32) * 0.02
        return {'x': jax.random.normal(ks[0], (B, S, D), dtype=jnp.float32), 'router_w': w(ks[1], (D, E)), 'w_gate': w(ks[2], (E, D, H)), 'w_up': w(ks[3], (E, D, H)), 'w_down': w(ks[4], (E, H, D)), 'ws_gate': w(ks[5], (D, HS)), 'ws_up': w(ks[6], (D, HS)), 'ws_down': w(ks[7], (HS, D)), 'sg_w': w(ks[8], (D, 1)), 'sg_b': jnp.zeros((1,), jnp.float32)}
    _L3_ffn_all = _L3_ffn_setup()
    _L3_ffn_in = {k: v for k, v in _L3_ffn_all.items() if k in ('router_w', 'w_gate', 'w_up', 'w_down', 'ws_gate', 'ws_up', 'ws_down', 'sg_w', 'sg_b')}
    del _L3_ffn_all
    return {'x': x, 'L0_tok_W': _L0_tok_in['W'], 'L0_tok_b': _L0_tok_in['b'], 'L0_tok_pos_emb': _L0_tok_in['pos_emb'], 'L0_attn_w_attn': _L0_attn_in['w_attn'], 'L0_attn_b_attn': _L0_attn_in['b_attn'], 'L0_attn_w_proj': _L0_attn_in['w_proj'], 'L0_attn_b_proj': _L0_attn_in['b_proj'], 'L0_attn_rel_emb': _L0_attn_in['rel_emb'], 'L0_ffn_W1': _L0_ffn_in['W1'], 'L0_ffn_b1': _L0_ffn_in['b1'], 'L0_ffn_W2': _L0_ffn_in['W2'], 'L0_ffn_b2': _L0_ffn_in['b2'], 'L0_ffn_s_gelu': _L0_ffn_in['s_gelu'], 'L0_ffn_s_out': _L0_ffn_in['s_out'], 'L1_attn_qkv_weight': _L1_attn_in['qkv_weight'], 'L1_attn_proj_weight': _L1_attn_in['proj_weight'], 'L1_ffn_qkv_w': _L1_ffn_in['qkv_w'], 'L1_ffn_qkv_b': _L1_ffn_in['qkv_b'], 'L1_ffn_q_norm_w': _L1_ffn_in['q_norm_w'], 'L1_ffn_q_norm_b': _L1_ffn_in['q_norm_b'], 'L1_ffn_k_norm_w': _L1_ffn_in['k_norm_w'], 'L1_ffn_k_norm_b': _L1_ffn_in['k_norm_b'], 'L1_ffn_wg_w': _L1_ffn_in['wg_w'], 'L1_ffn_wg0_w': _L1_ffn_in['wg0_w'], 'L1_ffn_wg1_w': _L1_ffn_in['wg1_w'], 'L1_ffn_proj_w': _L1_ffn_in['proj_w'], 'L1_ffn_proj_b': _L1_ffn_in['proj_b'], 'L2_attn_qkv_w': _L2_attn_in['qkv_w'], 'L2_attn_qkv_b': _L2_attn_in['qkv_b'], 'L2_attn_grassman_scale': _L2_attn_in['grassman_scale'], 'L2_attn_conv_w': _L2_attn_in['conv_w'], 'L2_attn_conv_b': _L2_attn_in['conv_b'], 'L2_attn_proj_w': _L2_attn_in['proj_w'], 'L2_attn_proj_b': _L2_attn_in['proj_b'], 'L2_ffn_Wg': _L2_ffn_in['Wg'], 'L2_ffn_bg': _L2_ffn_in['bg'], 'L2_ffn_W1': _L2_ffn_in['W1'], 'L2_ffn_b1': _L2_ffn_in['b1'], 'L2_ffn_W2': _L2_ffn_in['W2'], 'L2_ffn_b2': _L2_ffn_in['b2'], 'L3_attn_sp_w': _L3_attn_in['sp_w'], 'L3_attn_sp_b': _L3_attn_in['sp_b'], 'L3_attn_in_w': _L3_attn_in['in_w'], 'L3_attn_in_b': _L3_attn_in['in_b'], 'L3_attn_out_w': _L3_attn_in['out_w'], 'L3_attn_out_b': _L3_attn_in['out_b'], 'L3_attn_qw': _L3_attn_in['qw'], 'L3_ffn_router_w': _L3_ffn_in['router_w'], 'L3_ffn_w_gate': _L3_ffn_in['w_gate'], 'L3_ffn_w_up': _L3_ffn_in['w_up'], 'L3_ffn_w_down': _L3_ffn_in['w_down'], 'L3_ffn_ws_gate': _L3_ffn_in['ws_gate'], 'L3_ffn_ws_up': _L3_ffn_in['ws_up'], 'L3_ffn_ws_down': _L3_ffn_in['ws_down'], 'L3_ffn_sg_w': _L3_ffn_in['sg_w'], 'L3_ffn_sg_b': _L3_ffn_in['sg_b']}

def reference(x, L0_tok_W, L0_tok_b, L0_tok_pos_emb, L0_attn_w_attn, L0_attn_b_attn, L0_attn_w_proj, L0_attn_b_proj, L0_attn_rel_emb, L0_ffn_W1, L0_ffn_b1, L0_ffn_W2, L0_ffn_b2, L0_ffn_s_gelu, L0_ffn_s_out, L1_attn_qkv_weight, L1_attn_proj_weight, L1_ffn_qkv_w, L1_ffn_qkv_b, L1_ffn_q_norm_w, L1_ffn_q_norm_b, L1_ffn_k_norm_w, L1_ffn_k_norm_b, L1_ffn_wg_w, L1_ffn_wg0_w, L1_ffn_wg1_w, L1_ffn_proj_w, L1_ffn_proj_b, L2_attn_qkv_w, L2_attn_qkv_b, L2_attn_grassman_scale, L2_attn_conv_w, L2_attn_conv_b, L2_attn_proj_w, L2_attn_proj_b, L2_ffn_Wg, L2_ffn_bg, L2_ffn_W1, L2_ffn_b1, L2_ffn_W2, L2_ffn_b2, L3_attn_sp_w, L3_attn_sp_b, L3_attn_in_w, L3_attn_in_b, L3_attn_out_w, L3_attn_out_b, L3_attn_qw, L3_ffn_router_w, L3_ffn_w_gate, L3_ffn_w_up, L3_ffn_w_down, L3_ffn_ws_gate, L3_ffn_ws_up, L3_ffn_ws_down, L3_ffn_sg_w, L3_ffn_sg_b):
    import jax
    import jax.numpy as jnp

    def _L0_tok_ref(x, W, b, pos_emb):
        import jax, jax.numpy as jnp
        import numpy as np
        IMG = 64
        PATCH = 16
        C = 3
        D = 192
        NP_ = (IMG // PATCH) ** 2
        B = 64

        def _patchify(x):
            Bn, H, Wd, Cn = x.shape
            hp, wp = (H // PATCH, Wd // PATCH)
            x = x.reshape(Bn, hp, PATCH, wp, PATCH, Cn)
            x = x.transpose(0, 1, 3, 2, 4, 5)
            return x.reshape(Bn, hp * wp, PATCH * PATCH * Cn)
        patches = _patchify(x)
        proj = jnp.einsum('bnd,de->bne', patches, W) + b
        return proj + pos_emb[None, :, :]

    def _L0_attn_ref(x, w_attn, b_attn, w_proj, b_proj, rel_emb):
        import jax, jax.numpy as jnp
        import numpy as np
        N_HEAD = 12
        b, t, c = x.shape
        h = N_HEAD
        d = c // h
        scale = d ** (-0.5)
        qkv = x @ w_attn + b_attn
        q, k, v = jnp.split(qkv, 3, axis=-1)
        split_heads = lambda z: z.reshape(b, t, h, d).transpose(0, 2, 1, 3)
        q, k, v = map(split_heads, (q, k, v))
        q = q * scale
        scores = jnp.einsum('bhid,bhjd->bhij', q, k)
        rel = rel_emb[:t]
        rel = jnp.concatenate([jnp.zeros_like(rel[:1]), rel], axis=0)[:-1]
        scores = scores + jnp.einsum('bhid,jd->bhij', q, rel)
        causal = jnp.tril(jnp.ones((t, t), dtype=bool))
        scores = jnp.where(causal, scores, -jnp.inf)
        probs = jax.nn.softmax(scores, axis=-1)
        y = jnp.einsum('bhij,bhjd->bhid', probs, v)
        y = y.transpose(0, 2, 1, 3).reshape(b, t, c)
        return y @ w_proj + b_proj

    def _L0_ffn_ref(x, W1, b1, W2, b2, s_gelu, s_out):
        import jax, jax.numpy as jnp
        import numpy as np

        def _fq(x, scale, qmin, qmax):
            q = jnp.clip(jnp.round(x / scale), qmin, qmax) * scale
            return x + jax.lax.stop_gradient(q - x)

        def _quant_weight(W):
            scale = jnp.max(jnp.abs(W)) / 127.0
            return _fq(W, scale, -127.0, 127.0)
        h = jnp.einsum('bsd,hd->bsh', x, _quant_weight(W1)) + b1
        h = jax.nn.gelu(h, approximate=False)
        h = _fq(h, s_gelu, -128.0, 127.0)
        y = jnp.einsum('bsh,dh->bsd', h, _quant_weight(W2)) + b2
        y = _fq(y, s_out, -128.0, 127.0)
        return y

    def _L1_attn_ref(x, qkv_weight, proj_weight):
        import jax, jax.numpy as jnp
        import numpy as np
        B, N, C = (8, 256, 192)
        H = 12
        D = C // H
        SCALE = D ** (-0.5)
        EPS = 1e-05

        def _layer_norm(x):
            mean = x.mean(-1, keepdims=True)
            var = ((x - mean) ** 2).mean(-1, keepdims=True)
            return (x - mean) / jnp.sqrt(var + EPS)
        Bx, Nx, Cx = x.shape
        qkv = x @ qkv_weight.T
        qkv = qkv.reshape(Bx, Nx, 3, H, D).transpose(2, 0, 3, 1, 4)
        q, k, v = (qkv[0], qkv[1], qkv[2])
        q = _layer_norm(q) * SCALE
        k = _layer_norm(k)
        attn = jnp.einsum('bhnd,bhmd->bhnm', q, k)
        attn = jax.nn.softmax(attn, axis=-1)
        out = jnp.einsum('bhnm,bhmd->bhnd', attn, v)
        out = out.transpose(0, 2, 1, 3).reshape(Bx, Nx, Cx)
        return out @ proj_weight.T

    def _L1_ffn_ref(x, qkv_w, qkv_b, q_norm_w, q_norm_b, k_norm_w, k_norm_b, wg_w, wg0_w, wg1_w, proj_w, proj_b):
        import jax, jax.numpy as jnp
        import numpy as np
        DIM = 192
        H = 12
        HD = 64
        SHARED = 2
        ROUTED = 2
        E_ROUTED = H - SHARED
        LN_EPS = 1e-05

        def _layernorm(x, w, b):
            m = x.mean(-1, keepdims=True)
            v = ((x - m) ** 2).mean(-1, keepdims=True)
            return (x - m) * jax.lax.rsqrt(v + LN_EPS) * w + b
        B, N, C = x.shape
        scale = HD ** (-0.5)
        gates = jax.nn.softmax(x @ wg_w, axis=-1)
        _, idx = jax.lax.top_k(gates, ROUTED)
        mask = jax.nn.one_hot(idx, E_ROUTED, dtype=gates.dtype).sum(-2)
        rg = gates * mask
        denom = jnp.clip(rg.sum(-1, keepdims=True), jnp.finfo(rg.dtype).eps, None)
        routed_gates = rg / denom * ROUTED
        qkv = (x @ qkv_w + qkv_b).reshape(B, N, 3, H, HD)
        qkv = jnp.transpose(qkv, (2, 0, 3, 1, 4))
        q, k, v = (qkv[0], qkv[1], qkv[2])
        q = _layernorm(q, q_norm_w, q_norm_b)
        k = _layernorm(k, k_norm_w, k_norm_b)
        attn = jax.nn.softmax(jnp.einsum('bhqd,bhkd->bhqk', q * scale, k), axis=-1)
        o = jnp.einsum('bhqk,bhkd->bhqd', attn, v)
        o = jnp.transpose(o, (0, 2, 1, 3))
        shared_gates = jax.nn.softmax(x @ wg1_w, axis=-1) * SHARED
        w0 = jax.nn.softmax(x @ wg0_w, axis=-1) * 2.0
        shared_gates = w0[..., 0:1] * shared_gates
        routed_gates = w0[..., 1:2] * routed_gates
        masked_gates = jnp.concatenate([shared_gates, routed_gates], axis=-1)
        o = (masked_gates[..., None] * o).reshape(B, N, H * HD)
        return o @ proj_w + proj_b

    def _L2_attn_ref(x, qkv_w, qkv_b, grassman_scale, conv_w, conv_b, proj_w, proj_b):
        import jax, jax.numpy as jnp
        import numpy as np
        NUM_HEADS = 12
        DIM = 192
        HEAD_DIM = DIM // NUM_HEADS
        B, N = (32, 64)
        Bs, Ns, C = x.shape
        H, d = (NUM_HEADS, C // NUM_HEADS)
        qkv = (x @ qkv_w.T + qkv_b).reshape(Bs, Ns, 3, H, d).transpose(2, 0, 3, 1, 4)
        q, k, v = (qkv[0], qkv[1], qkv[2])
        qgr = jnp.linalg.qr(q, mode='reduced')[0]
        kgr = jnp.linalg.qr(k, mode='reduced')[0]
        dots = jnp.einsum('bhnd,bhmd->bhnm', qgr, kgr)
        attn_g = dots * dots * grassman_scale
        cat = jnp.concatenate([attn_g, attn_g], axis=1)
        mixed = jnp.einsum('oc,bcnm->bonm', conv_w, cat) + conv_b[None, :, None, None]
        attn = jax.nn.softmax(mixed, axis=-1)
        out = jnp.einsum('bhnm,bhmd->bhnd', attn, v)
        out = out.transpose(0, 2, 1, 3).reshape(Bs, Ns, C)
        return out @ proj_w.T + proj_b

    def _L2_ffn_ref(x, Wg, bg, W1, b1, W2, b2):
        import jax, jax.numpy as jnp
        import numpy as np
        B, T, D = (4, 512, 192)
        E, F, K = (8, 4 * 192, 2)
        b, t, d = x.shape
        x_flat = x.reshape(-1, d)
        n = x_flat.shape[0]
        gates = jax.nn.softmax(x_flat @ Wg + bg, axis=-1)
        topk_g, topk_i = jax.lax.top_k(gates, K)
        combine = jnp.zeros((n, W1.shape[0]), dtype=gates.dtype)
        combine = combine.at[jnp.arange(n)[:, None], topk_i].add(topk_g)
        h = jnp.einsum('nd,edf->enf', x_flat, W1) + b1[:, None, :]
        h = jax.nn.gelu(h, approximate=False)
        y = jnp.einsum('enf,efd->end', h, W2) + b2[:, None, :]
        out = jnp.einsum('ne,end->nd', combine, y)
        return out.reshape(b, t, d)

    def _L3_attn_ref(x, sp_w, sp_b, in_w, in_b, out_w, out_b, qw):
        import jax, jax.numpy as jnp
        import numpy as np
        N_QUBITS = 8
        N_HEADS = 12
        EPS = 1e-08
        B, S, D = x.shape
        Q = N_QUBITS
        sp = x @ sp_w.T + sp_b
        re, im = (sp[..., :Q], sp[..., Q:])
        norm = jnp.sqrt(jnp.sum(re * re + im * im, axis=-1, keepdims=True))
        re = re / (norm + EPS)
        im = im / (norm + EPS)
        ov_re = jnp.einsum('bid,bjd->bij', re, re) + jnp.einsum('bid,bjd->bij', im, im)
        ov_im = jnp.einsum('bid,bjd->bij', re, im) - jnp.einsum('bid,bjd->bij', im, re)
        fid = ov_re * ov_re + ov_im * ov_im
        qa = jax.nn.softmax(fid, axis=-1)
        quantum_out = jnp.einsum('bij,bjd->bid', qa, x)
        H, Dh = (N_HEADS, D // N_HEADS)
        qkv = x @ in_w.T + in_b
        q, k, v = jnp.split(qkv, 3, axis=-1)
        q = q.reshape(B, S, H, Dh).transpose(0, 2, 1, 3)
        k = k.reshape(B, S, H, Dh).transpose(0, 2, 1, 3)
        v = v.reshape(B, S, H, Dh).transpose(0, 2, 1, 3)
        scores = jnp.einsum('bhid,bhjd->bhij', q, k) / jnp.sqrt(jnp.asarray(Dh, x.dtype))
        attn = jax.nn.softmax(scores, axis=-1)
        ctx = jnp.einsum('bhij,bhjd->bhid', attn, v)
        ctx = ctx.transpose(0, 2, 1, 3).reshape(B, S, D)
        classical_out = ctx @ out_w.T + out_b
        w = jax.nn.sigmoid(qw)
        return w * quantum_out + (1.0 - w) * classical_out

    def _L3_ffn_ref(x, router_w, w_gate, w_up, w_down, ws_gate, ws_up, ws_down, sg_w, sg_b):
        import jax, jax.numpy as jnp
        import numpy as np
        B, S, D = (4, 256, 192)
        E = 8
        H = 192
        HS = 768
        TOPK_ROUTED = 2
        probs = jax.nn.softmax(x @ router_w, axis=-1)
        gates, idx = jax.lax.top_k(probs, TOPK_ROUTED)
        gates = gates / jnp.sum(gates, axis=-1, keepdims=True)
        n_exp = router_w.shape[1]
        dense_g = jnp.sum(jax.nn.one_hot(idx, n_exp, dtype=x.dtype) * gates[..., None], axis=-2)
        g = jax.nn.silu(jnp.einsum('bsd,edh->bseh', x, w_gate))
        u = jnp.einsum('bsd,edh->bseh', x, w_up)
        expert_out = jnp.einsum('bseh,ehd->bsed', g * u, w_down)
        routed = jnp.einsum('bse,bsed->bsd', dense_g, expert_out)
        shared = jax.nn.silu(x @ ws_gate) * (x @ ws_up) @ ws_down
        alpha = jax.nn.sigmoid(x @ sg_w + sg_b)
        return alpha * shared + (1.0 - alpha) * routed
    h = _L0_tok_ref(x, L0_tok_W, L0_tok_b, L0_tok_pos_emb)
    h = _layernorm(h + _L0_attn_ref(h, L0_attn_w_attn, L0_attn_b_attn, L0_attn_w_proj, L0_attn_b_proj, L0_attn_rel_emb), axis=-1)
    h = _layernorm(h + _L0_ffn_ref(h, L0_ffn_W1, L0_ffn_b1, L0_ffn_W2, L0_ffn_b2, L0_ffn_s_gelu, L0_ffn_s_out), axis=-1)
    h = _layernorm(h + _L1_attn_ref(h, L1_attn_qkv_weight, L1_attn_proj_weight), axis=-1)
    h = _layernorm(h + _L1_ffn_ref(h, L1_ffn_qkv_w, L1_ffn_qkv_b, L1_ffn_q_norm_w, L1_ffn_q_norm_b, L1_ffn_k_norm_w, L1_ffn_k_norm_b, L1_ffn_wg_w, L1_ffn_wg0_w, L1_ffn_wg1_w, L1_ffn_proj_w, L1_ffn_proj_b), axis=-1)
    h = _layernorm(h + _L2_attn_ref(h, L2_attn_qkv_w, L2_attn_qkv_b, L2_attn_grassman_scale, L2_attn_conv_w, L2_attn_conv_b, L2_attn_proj_w, L2_attn_proj_b), axis=-1)
    h = _layernorm(h + _L2_ffn_ref(h, L2_ffn_Wg, L2_ffn_bg, L2_ffn_W1, L2_ffn_b1, L2_ffn_W2, L2_ffn_b2), axis=-1)
    h = _layernorm(h + _L3_attn_ref(h, L3_attn_sp_w, L3_attn_sp_b, L3_attn_in_w, L3_attn_in_b, L3_attn_out_w, L3_attn_out_b, L3_attn_qw), axis=-1)
    h = _layernorm(h + _L3_ffn_ref(h, L3_ffn_router_w, L3_ffn_w_gate, L3_ffn_w_up, L3_ffn_w_down, L3_ffn_ws_gate, L3_ffn_ws_up, L3_ffn_ws_down, L3_ffn_sg_w, L3_ffn_sg_b), axis=-1)
    return h

_drawn_inputs = setup_inputs


def setup_inputs(seed=0):
    import zlib

    import numpy as np

    out = dict(_drawn_inputs(seed))
    spreads = {'L0_tok_b': (0.0, 0.1),
     'L0_attn_b_attn': (0.0, 0.1),
     'L0_attn_b_proj': (0.0, 0.1),
     'L1_ffn_qkv_b': (0.0, 0.1),
     'L1_ffn_q_norm_w': (1.0, 0.6),
     'L1_ffn_q_norm_b': (0.0, 0.8),
     'L1_ffn_k_norm_w': (1.0, 0.6),
     'L1_ffn_k_norm_b': (0.0, 2.0),
     'L1_ffn_proj_b': (0.0, 0.1),
     'L2_attn_qkv_b': (0.0, 0.1),
     'L2_attn_conv_b': (0.0, 2.0),
     'L2_attn_proj_b': (0.0, 0.1),
     'L2_ffn_bg': (0.0, 0.407),
     'L2_ffn_b1': (0.0, 0.8),
     'L2_ffn_b2': (0.0, 0.309)}
    factors = {'L0_attn_rel_emb': 8.0,
     'L0_ffn_b1': 4.481,
     'L0_ffn_b2': 3.811,
     'L1_ffn_wg0_w': 7.07,
     'L1_ffn_wg1_w': 7.231,
     'L2_attn_conv_w': 64.0,
     'L2_ffn_W1': 3.143,
     'L2_ffn_W2': 2.827,
     'L3_attn_sp_w': 4.163,
     'L3_attn_sp_b': 27.974,
     'L3_attn_in_w': 4.722,
     'L3_attn_in_b': 8.0,
     'L3_attn_out_w': 4.947,
     'L3_attn_out_b': 8.0,
     'L3_ffn_router_w': 8.0,
     'L3_ffn_w_gate': 8.0,
     'L3_ffn_w_up': 8.0,
     'L3_ffn_w_down': 8.0,
     'L3_ffn_ws_gate': 5.002,
     'L3_ffn_ws_up': 5.045,
     'L3_ffn_ws_down': 5.0,
     'L3_ffn_sg_w': 8.0}
    for name, (base, spread) in spreads.items():
        noise = np.random.default_rng([zlib.crc32(name.encode()), seed]).standard_normal(out[name].shape)
        drawn = base * np.exp(spread * noise) if base else spread * noise
        out[name] = jnp.asarray(drawn.astype(out[name].dtype))
    for name, factor in factors.items():
        out[name] = (out[name] * factor).astype(out[name].dtype)
    return out
```

```python
import concourse.bass as bass
from concourse import mybir
from concourse.alu_op_type import AluOpType as ALU
from contextlib import ExitStack
import numpy as np

FP32 = mybir.dt.float32
BF16 = mybir.dt.bfloat16
U32 = mybir.dt.uint32
ACT = mybir.ActivationFunctionType
AX = mybir.AxisListType

D = 192
SEQ = 16
IMAGES = 64
TOKENS = IMAGES * SEQ
P = 128
TILES = TOKENS // P
PAIRS = TILES // 2
H = 12
HD = D // H
WD = 64
KC = D // 2
KB = KC + 1
GROUP = 32
NG = P // GROUP
FF = 768
FC = FF // P
E = 8
LN_EPS = 1e-5
BANK = 512
MAGIC = 1.5 * 2.0 ** 23


class Steps:

    def __init__(self, eng, sem, per=0, index=None):
        self.eng, self.sem, self.per, self.index, self.n = eng, sem, per, index, 0

    def link(self, ins):
        self.n += 1
        ins.then_inc(self.sem, 1)
        self.eng.wait_ge(self.sem, self.n if self.index is None else self.index * self.per + self.n)

    def end(self):
        assert self.index is None or self.n == self.per, (self.n, self.per)


def spread(ap, n):
    return ap.unsqueeze(ap.ndim).to_broadcast(list(ap.shape) + [n])


def spread_mid(ap, n):
    return ap.unsqueeze(1).to_broadcast([ap.shape[0], n, ap.shape[1]])


def reflect(dve, st, dst, vs, prod, w, taus, j, first, nm):
    n, m = SEQ - j, SEQ - first
    if m == 0:
        return
    d = dst[:, j:SEQ, :, first:SEQ]
    v = vs[:, j:SEQ, :, j]
    t = prod[:, 0:n, :, 0:m]
    wm = w[:, :, 0:m]
    st.link(dve.tensor_tensor(t, d, spread(v, m), ALU.mult))
    st.link(dve.tensor_reduce(wm, t.rearrange("p n c d -> p c d n"), AX.X, ALU.add))
    st.link(dve.tensor_tensor(wm, wm, spread(taus[:, j, :], m), ALU.mult))
    wide = wm.unsqueeze(1).to_broadcast([P, n, nm, m])
    st.link(dve.tensor_tensor(t, wide, spread(v, m), ALU.mult))
    st.link(dve.tensor_tensor(d, d, t, ALU.subtract))


def vit_tower(nc, I, out, stop=99):
    ctx = ExitStack()
    with ctx:
        def sb(name, shape, dt=FP32):
            return ctx.enter_context(nc.sbuf_tensor(name, shape, dt))

        scratch = ExitStack()

        def local(name, shape, dt=FP32):
            return scratch.enter_context(nc.sbuf_tensor(name, shape, dt))

        of_phase = []

        def sem(name):
            of_phase.append(nc.alloc_semaphore(name))
            return of_phase[-1]

        def lasting(name):
            return ctx.enter_context(nc.semaphore(name))

        def end_phase():
            nc.clear_and_free_semaphores(list(of_phase))
            of_phase.clear()
            scratch.close()
            nc.all_engine_barrier()

        PS = ctx.enter_context(nc.psum_tensor("PS", [P, 8, BANK], FP32))
        X = sb("X", [P, TILES, D])
        XT = sb("XT", [KB, 2, TOKENS])
        ones = sb("ones", [1, P])
        big = sb("big", [P, FC, TOKENS])
        stats = sb("stats", [P, TILES, 6])
        mv = sb("mv", [P, TILES, 2])
        rstd = sb("rstd", [P, TILES])
        newton = sb("newton", [P, TILES])
        order = lasting("order")

        loaded = {}
        plan = []

        def keep(name):
            src = I[name]
            loaded[name] = (sb("w_" + name, src.shape, src.dtype), lasting("in_" + name))
            plan.append(name)
            return loaded[name][0]

        in_patches = lasting("in_patches")
        tok_w, pos, tok_b = keep("tok_w"), keep("pos"), keep("tok_b")
        ident = keep("ident")
        keys_causal, keys_block = keep("keys_causal"), keep("keys_block")
        rel, l0_qkv, l0_proj = keep("rel"), keep("l0_qkv"), keep("l0_proj")
        ff_w1, ff_b1, ff_w2, ff_b2 = keep("ff_w1"), keep("ff_b1"), keep("ff_w2"), keep("ff_b2")
        ff_s = keep("ff_s")
        l1_qkv, l1_proj = keep("l1_qkv"), keep("l1_proj")
        w_qkv, w_proj, w_projb = keep("w_qkv"), keep("w_proj"), keep("w_projb")
        w_gates, w_affine, iota10 = keep("w_gates"), keep("w_affine"), keep("iota10")
        l2_qkv, l2_proj, l2_scale = keep("l2_qkv"), keep("l2_proj"), keep("l2_scale")
        mix_a, mix_b, half01 = keep("mix_a"), keep("mix_b"), keep("half01")
        moe_g, moe_b2 = keep("moe_g"), keep("moe_b2")
        l3_qkv, l3_proj, l3_qw, block01 = keep("l3_qkv"), keep("l3_proj"), keep("l3_qw"), keep("block01")
        l3_gates = keep("l3_gates")

        def landed(eng, *names):
            for n in names:
                eng.wait_ge(loaded[n][1], 16)

        def own(eng, s, value):
            eng.wait_ge(s, value)
            eng.sem_inc(order, 1)

        emb_done, emb_added, xt_ones, pos_ready = sem("emb_done"), sem("emb_added"), sem("xt_ones"), sem("pos_ready")
        with nc.Block() as block:
            @block.sync
            def _(sp):
                for n in plan[:3]:
                    sp.dma_start(loaded[n][0][:], I[n]).then_inc(loaded[n][1], 16)
                sp.dma_start(big[:], I["patches"]).then_inc(in_patches, 16)
                for n in plan[3:]:
                    sp.dma_start(loaded[n][0][:], I[n]).then_inc(loaded[n][1], 16)

            @block.gpsimd
            def _(pool):
                pool.memset(XT[KC:KB, :, :], 1.0).then_inc(xt_ones, 1)
                pool.wait_ge(xt_ones, 1)
                pool.memset(ones[:], 1.0).then_inc(xt_ones, 1)
                pool.wait_ge(xt_ones, 2)

            @block.tensor
            def _(pe):
                landed(pe, "tok_w")
                pe.wait_ge(in_patches, 16)
                for t in range(TILES):
                    for c in range(FC):
                        last = pe.matmul(PS[:, t // 2, (t % 2) * D:(t % 2 + 1) * D], big[:, c, t * P:(t + 1) * P],
                                         tok_w[:, c, :], start=(c == 0), stop=(c == FC - 1))
                    last.then_inc(emb_done, 1)

            @block.vector
            def _(dve):
                landed(dve, "pos", "tok_b")
                dve.tensor_tensor(pos[:], pos[:], tok_b[:], ALU.add).then_inc(pos_ready, 1)
                dve.wait_ge(pos_ready, 1)
                for m in range(PAIRS):
                    dve.wait_ge(emb_done, 2 * m + 2)
                    dve.tensor_tensor(X[:, 2 * m:2 * m + 2, :], PS[:, m, 0:2 * D].rearrange("p (t d) -> p t d", t=2),
                                      spread_mid(pos[:], 2), ALU.add).then_inc(emb_added, 1)
                dve.wait_ge(emb_added, PAIRS)

        def norm_and_transpose(name, norm=True, transpose=True):
            dve_step, var_ready = sem(name + "_dve"), sem(name + "_var")
            log_done, start_done = sem(name + "_log"), sem(name + "_start")
            normed, turned, copied = sem(name + "_normed"), sem(name + "_turned"), sem(name + "_copied")
            with nc.Block() as block:
                @block.vector
                def _(dve):
                    if not norm:
                        return
                    steps = Steps(dve, dve_step)
                    for t in range(TILES):
                        dve.bn_stats(stats[:, t, :], X[:, t, :]).then_inc(dve_step, 1)
                    steps.n = TILES
                    dve.wait_ge(dve_step, TILES)
                    for t in range(TILES):
                        dve.bn_aggr(mv[:, t, :], stats[:, t, :]).then_inc(dve_step, 1)
                    steps.n = 2 * TILES
                    dve.wait_ge(dve_step, 2 * TILES)
                    dve.tensor_scalar(mv[:, :, 1], mv[:, :, 1], LN_EPS, None, ALU.add).then_inc(var_ready, 1)
                    dve.wait_ge(start_done, 1)
                    steps.link(dve.tensor_tensor(newton[:], rstd[:], rstd[:], ALU.mult))
                    steps.link(dve.tensor_tensor(newton[:], newton[:], mv[:, :, 1], ALU.mult))
                    steps.link(dve.tensor_scalar(newton[:], newton[:], -0.5, 1.5, ALU.mult, ALU.add))
                    steps.link(dve.tensor_tensor(rstd[:], rstd[:], newton[:], ALU.mult))
                    for t in range(TILES):
                        dve.tensor_scalar(X[:, t, :], X[:, t, :], mv[:, t, 0:1], rstd[:, t:t + 1],
                                          ALU.subtract, ALU.mult).then_inc(normed, 1)
                    dve.wait_ge(normed, TILES)

                @block.scalar
                def _(act):
                    if norm:
                        act.wait_ge(var_ready, 1)
                        act.activation(rstd[:], mv[:, :, 1], ACT.Ln).then_inc(log_done, 1)
                        act.wait_ge(log_done, 1)
                        act.activation(rstd[:], rstd[:], ACT.Exp, scale=-0.5).then_inc(start_done, 1)
                    if transpose:
                        for m in range(PAIRS):
                            act.wait_ge(turned, m + 1)
                            act.activation(XT[0:KC, :, m * 2 * P:(m + 1) * 2 * P],
                                           PS[0:KC, m, :].rearrange("p (c n) -> p c n", c=2), ACT.Copy).then_inc(copied, 1)
                        act.wait_ge(copied, PAIRS)

                @block.tensor
                def _(pe):
                    if not transpose:
                        return
                    landed(pe, "ident")
                    for m in range(PAIRS):
                        if norm:
                            pe.wait_ge(normed, 2 * m + 2)
                        for t in range(2):
                            for c in range(2):
                                last = pe.transpose(PS[0:KC, m, c * 2 * P + t * P:c * 2 * P + (t + 1) * P],
                                                    X[:, 2 * m + t, c * KC:(c + 1) * KC], ident[:])
                        last.then_inc(turned, 1)

        end_phase()
        norm_and_transpose("tok", norm=False)
        end_phase()

        XTs = sb("XTs", [KB, 2, 2 * P])
        Xs = sb("Xs", [P, 2, D])
        NB = 28
        QK = sb("QK", [P, 2, NB, GROUP])
        QKT = sb("QKT", [P, 2, NB, GROUP])
        CN = sb("CN", [P, 2 * 2 * H, HD])
        SQ = sb("SQ", [P, 2 * 2 * H, HD])
        hm, hv, hr, ht = (sb(n, [P, 2 * 2 * H]) for n in ("hm", "hv", "hr", "ht"))
        V = sb("V", [P, 2 * D * 2])
        S = sb("S", [P, 2, H, GROUP])
        PT = sb("PT", [P, 2, H, GROUP])
        smax, rsum = sb("smax", [P, 2, H]), sb("rsum", [P, 2, H])
        Y = sb("Y", [P, 2, D])
        YT = sb("YT", [KB, 2, 2 * P])
        F = sb("F", [P, 2, 2, GROUP])
        QF, QFT = sb("QF", [P, 2, GROUP]), sb("QFT", [P, 2, GROUP])
        qs = sb("qs", [P, 2])
        sp2, spr, spt = sb("sp2", [P, 2]), sb("spr", [P, 2]), sb("spt", [P, 2])
        SP = sb("SP", [P, 2, HD])
        SPQ = sb("SPQ", [P, 2, HD])
        mixw = sb("mixw", [P, 2])

        identb = sb("identb", [P, P], BF16)
        mask_causal = sb("mask_causal", [P, H * GROUP], BF16)
        mask_block = sb("mask_block", [P, (H + 2) * GROUP], BF16)

        buf_zero = sem("buf_zero")
        with nc.Block() as block:
            @block.gpsimd
            def _(pool):
                pool.memset(QK[:], 0.0).then_inc(buf_zero, 1)
                pool.wait_ge(buf_zero, 1)
                pool.memset(YT[KC:KB, :, :], 1.0).then_inc(buf_zero, 1)
                pool.wait_ge(buf_zero, 2)
                pool.memset(mask_block[:], 0.0).then_inc(buf_zero, 1)
                pool.wait_ge(buf_zero, 3)
                landed(pool, "ident", "keys_causal", "keys_block")
                pool.tensor_copy(identb[:], ident[:]).then_inc(buf_zero, 1)
                pool.wait_ge(buf_zero, 4)
                for mask, keys in ((mask_causal, keys_causal), (mask_block, keys_block)):
                    pool.tensor_copy(mask[:, 0:H * GROUP].rearrange("p (h j) -> p h j", h=H),
                                     spread_mid(keys[:], H)).then_inc(buf_zero, 1)
                pool.wait_ge(buf_zero, 6)

        def attention(name, wqkv, wproj, w_names, mask, causal_rel=False, head_norm=False, quantum=False):
            s = {k: sem(f"{name}_{k}") for k in (
                "xts", "qkv", "vcopy", "qcopy", "var", "log", "start", "sqd", "qkt", "score", "expin", "expd",
                "pt", "pv", "yn", "yt", "ytc", "proj", "added", "dve", "fsq", "fin", "fexp", "qft", "qv", "spl", "sps", "qw")}
            nh = H + 2 if quantum else H
            nb = 2 * nh
            per = 5
            if head_norm:
                per = 11
            if quantum:
                per = 18

            with nc.Block() as block:
                @block.gpsimd
                def _(pool):
                    with pool.Fori(0, PAIRS) as i:
                        own(pool, s["qkv"], i + 1)
                        if quantum:
                            own(pool, s["qv"], i + 1)
                            pool.tensor_copy(Xs[:], X[:, bass.ds(i * 2, 2), :]).then_inc(s["xts"], 1)
                            own(pool, s["xts"], i * 2 + 1)
                        pool.tensor_copy(XTs[:], XT[:, :, bass.ds(i * (2 * P), 2 * P)]).then_inc(s["xts"], 1)

                nst = 2 if quantum else 1

                @block.tensor
                def _(pe):
                    landed(pe, "ident", *w_names)
                    wa = 2 * D + (SEQ if quantum else 0)
                    for k in ("qkv", "score", "pv", "qv"):
                        pe.sem_inc(s[k], 1)
                    with pe.Fori(0, PAIRS) as i:
                        pe.wait_ge(s["xts"], i * nst + nst)
                        own(pe, s["added"], i + 1)
                        for t in range(2):
                            for c in range(2):
                                pe.matmul(PS[:, t, 0:wa], XTs[:, c, t * P:(t + 1) * P], wqkv[:, c, 0:wa],
                                          start=(c == 0), stop=(c == 1))
                            for c in range(2):
                                last = pe.matmul(PS[:, 2, t * D:(t + 1) * D], XTs[:, c, t * P:(t + 1) * P],
                                                 wqkv[:, c, wa:wa + D], start=(c == 0), stop=(c == 1))
                        last.then_inc(s["qkv"], 1)
                        own(pe, s["qkt"], i + 1)
                        for t in range(2):
                            pe.matmul(PS[:, 4 + t, 0:nh * GROUP], identb[:],
                                      mask[:, 0:nh * GROUP], start=True, stop=False, skip_group_check=True)
                            for h in range(nh):
                                for g in range(NG):
                                    r = slice(g * GROUP, g * GROUP + HD)
                                    last = pe.matmul(PS[g * GROUP:(g + 1) * GROUP, 4 + t, h * GROUP:(h + 1) * GROUP],
                                                     QKT[r, t, h, :], QKT[r, t, nh + h, :], start=False,
                                                     stop=True, skip_group_check=True)
                        last.then_inc(s["score"], 1)
                        own(pe, s["pt"], i + 1)
                        own(pe, s["vcopy"], i + 1)
                        for t in range(2):
                            for h in range(H):
                                for g in range(NG):
                                    r = slice(g * GROUP, (g + 1) * GROUP)
                                    last = pe.matmul(PS[r, 6, t * D + h * HD:t * D + (h + 1) * HD], PT[r, t, h, :],
                                                     V[r, t * D + h * HD:t * D + (h + 1) * HD],
                                                     start=True, stop=True, skip_group_check=True)
                        last.then_inc(s["pv"], 1)
                        if quantum:
                            own(pe, s["qft"], i + 1)
                            for t in range(2):
                                for g in range(NG):
                                    r = slice(g * GROUP, (g + 1) * GROUP)
                                    last = pe.matmul(PS[r, 3, t * D:(t + 1) * D], QFT[r, t, :], Xs[r, t, :],
                                                     start=True, stop=True, skip_group_check=True)
                            last.then_inc(s["qv"], 1)
                        own(pe, s["yn"], i + 1)
                        for t in range(2):
                            for c in range(2):
                                last = pe.transpose(PS[0:KC, 7, c * 2 * P + t * P:c * 2 * P + (t + 1) * P],
                                                    Y[:, t, c * KC:(c + 1) * KC], ident[:])
                        last.then_inc(s["yt"], 1)
                        own(pe, s["ytc"], i + 1)
                        for t in range(2):
                            for c in range(2):
                                last = pe.matmul(PS[:, 2, t * D:(t + 1) * D], YT[:, c, t * P:(t + 1) * P],
                                                 wproj[:, c, :], start=(c == 0), stop=(c == 1))
                        last.then_inc(s["proj"], 1)

                @block.scalar
                def _(act):
                    if quantum:
                        landed(act, "l3_qw")
                        act.activation(mixw[:, 0:1], l3_qw[:], ACT.Exp, scale=-1.0).then_inc(s["qw"], 1)
                    with act.Fori(0, PAIRS) as i:
                        act.wait_ge(s["qkv"], i + 2)
                        act.wait_ge(s["pv"], i + 1)
                        act.activation(V[:, 0:2 * D], PS[:, 2, 0:2 * D], ACT.Copy).then_inc(s["vcopy"], 1)
                        if not head_norm:
                            n = H if causal_rel else 2 * H
                            act.wait_ge(s["score"], i + 1)
                            if not quantum:
                                act.activation(QK[:, :, 0:n, 0:HD], PS[:, 0:2, 0:n * HD].rearrange(
                                    "p t (h d) -> p t h d", d=HD), ACT.Copy).then_inc(s["qcopy"], 1)
                            else:
                                for j in range(2):
                                    act.activation(QK[:, :, j * nh:j * nh + H, 0:HD],
                                                   PS[:, 0:2, j * D:(j + 1) * D].rearrange(
                                                       "p t (h d) -> p t h d", d=HD), ACT.Copy).then_inc(s["qcopy"], 1)
                                act.wait_ge(s["spl"], i + 1)
                                act.activation(spr[:], sp2[:], ACT.Ln).then_inc(s["log"], 1)
                                act.wait_ge(s["log"], i + 1)
                                act.activation(spr[:], spr[:], ACT.Exp, scale=-0.5).then_inc(s["start"], 1)
                                act.wait_ge(s["score"], i + 2)
                                act.activation(F[:], PS[:, 4:6, H * GROUP:nh * GROUP].rearrange(
                                    "p t (h j) -> p t h j", j=GROUP), ACT.Square).then_inc(s["fsq"], 1)
                                act.wait_ge(s["fin"], i + 1)
                                act.activation(QF[:], QF[:], ACT.Exp).then_inc(s["fexp"], 1)
                        else:
                            act.wait_ge(s["var"], i * 2 + 1)
                            act.activation(SQ[:], CN[:], ACT.Square).then_inc(s["sqd"], 1)
                            act.wait_ge(s["var"], i * 2 + 2)
                            act.activation(hr[:], hv[:], ACT.Ln).then_inc(s["log"], 1)
                            act.wait_ge(s["log"], i + 1)
                            act.activation(hr[:], hr[:], ACT.Exp, scale=-0.5).then_inc(s["start"], 1)
                        act.wait_ge(s["expin"], i + 1)
                        act.activation(S[:], S[:], ACT.Exp, scale=HD ** -0.5).then_inc(s["expd"], 1)
                        act.wait_ge(s["yt"], i + 1)
                        act.activation(YT[0:KC, :, :], PS[0:KC, 7, :].rearrange("p (c n) -> p c n", c=2),
                                       ACT.Copy).then_inc(s["ytc"], 1)

                @block.vector
                def _(dve):
                    pre = Steps(dve, s["sps"])
                    if causal_rel:
                        landed(dve, "rel")
                    if quantum:
                        landed(dve, "block01")
                        dve.wait_ge(s["qw"], 1)
                        pre.link(dve.tensor_scalar(mixw[:, 1:2], mixw[:, 0:1], 1.0, None, ALU.add))
                        pre.link(dve.reciprocal(mixw[:, 0:1], mixw[:, 1:2]))
                        pre.link(dve.tensor_scalar(mixw[:, 1:2], mixw[:, 0:1], -1.0, 1.0, ALU.mult, ALU.add))
                    dve.sem_inc(s["added"], 1)
                    with dve.Fori(0, PAIRS) as i:
                        st = Steps(dve, s["dve"], per, i)
                        dve.wait_ge(s["qkv"], i + 2)
                        if not head_norm:
                            dve.wait_ge(s["qcopy"], i * (2 if quantum else 1) + (2 if quantum else 1))
                        if causal_rel:
                            for t in range(2):
                                st.link(dve.tensor_tensor(
                                    QK[:, t, H:2 * H, 0:HD],
                                    PS[:, t, D:2 * D].rearrange("p (h d) -> p h d", d=HD),
                                    spread_mid(rel[:], H), ALU.add))
                        if head_norm:
                            qk = PS[:, 0:2, 0:2 * D].rearrange("p t (h d) -> p t h d", d=HD)
                            cn = CN[:].rearrange("p (t h) d -> p t h d", t=2)
                            m2, r2 = (x[:].rearrange("p (t h) -> p t h", t=2) for x in (hm, hr))
                            st.link(dve.tensor_reduce(m2, qk, AX.X, ALU.add))
                            st.link(dve.tensor_scalar(hm[:], hm[:], 1.0 / HD, None, ALU.mult))
                            dve.tensor_tensor(cn, qk, spread(m2, HD), ALU.subtract).then_inc(s["var"], 1)
                            dve.wait_ge(s["sqd"], i + 1)
                            st.link(dve.tensor_reduce(hv[:], SQ[:], AX.X, ALU.add))
                            dve.tensor_scalar(hv[:], hv[:], 1.0 / HD, LN_EPS, ALU.mult, ALU.add).then_inc(s["var"], 1)
                            dve.wait_ge(s["start"], i + 1)
                            st.link(dve.tensor_tensor(ht[:], hr[:], hr[:], ALU.mult))
                            st.link(dve.tensor_tensor(ht[:], ht[:], hv[:], ALU.mult))
                            st.link(dve.tensor_scalar(ht[:], ht[:], -0.5, 1.5, ALU.mult, ALU.add))
                            st.link(dve.tensor_tensor(hr[:], hr[:], ht[:], ALU.mult))
                            st.link(dve.tensor_tensor(QK[:, :, 0:2 * H, 0:HD], cn, spread(r2, HD), ALU.mult))
                        if quantum:
                            sp_in = PS[:, 0:2, 2 * D:2 * D + HD]
                            st.link(dve.tensor_copy(SP[:], sp_in))
                            st.link(dve.tensor_tensor(SPQ[:], SP[:], SP[:], ALU.mult))
                            st.link(dve.tensor_reduce(sp2[:], SPQ[:], AX.X, ALU.add))
                            dve.tensor_scalar(sp2[:], sp2[:], 2.0 ** -64, None, ALU.max).then_inc(s["spl"], 1)
                            dve.wait_ge(s["start"], i + 1)
                            st.link(dve.tensor_tensor(spt[:], spr[:], spr[:], ALU.mult))
                            st.link(dve.tensor_tensor(spt[:], spt[:], sp2[:], ALU.mult))
                            st.link(dve.tensor_scalar(spt[:], spt[:], -0.5, 1.5, ALU.mult, ALU.add))
                            st.link(dve.tensor_tensor(spr[:], spr[:], spt[:], ALU.mult))
                            st.link(dve.tensor_tensor(spt[:], spr[:], sp2[:], ALU.mult))
                            st.link(dve.tensor_scalar(spt[:], spt[:], 1e-8, None, ALU.add))
                            st.link(dve.reciprocal(spr[:], spt[:]))
                            sc = spread(spr[:], HD)
                            half = HD // 2
                            dve.tensor_tensor(QK[:, :, H, 0:HD], SP[:], sc, ALU.mult)
                            dve.tensor_tensor(QK[:, :, H + 1, 0:HD], SP[:], sc, ALU.mult)
                            dve.tensor_tensor(QK[:, :, nh + H, 0:HD], SP[:], sc, ALU.mult)
                            dve.tensor_tensor(QK[:, :, nh + H + 1, 0:half], SP[:, :, half:HD], spread(spr[:], half), ALU.mult)
                            st.link(dve.scalar_tensor_tensor(QK[:, :, nh + H + 1, half:HD], SP[:, :, 0:half], -1.0,
                                                             spread(spr[:], half), ALU.mult, ALU.mult))
                        dve.transpose(QKT[:, :, 0:nb, :], QK[:, :, 0:nb, :]).then_inc(s["qkt"], 1)
                        dve.wait_ge(s["score"], i + 2)
                        sc_ps = PS[:, 4:6, 0:H * GROUP].rearrange("p t (h j) -> p t h j", j=GROUP)
                        if quantum:
                            dve.wait_ge(s["fsq"], i + 1)
                            dve.tensor_tensor(QF[:], F[:, :, 0, :], F[:, :, 1, :], ALU.add).then_inc(s["fin"], 1)
                        st.link(dve.tensor_reduce(smax[:], sc_ps, AX.X, ALU.max))
                        dve.tensor_tensor(S[:], sc_ps, spread(smax[:], GROUP), ALU.subtract).then_inc(s["expin"], 1)
                        if quantum:
                            dve.wait_ge(s["fexp"], i + 1)
                            st.link(dve.tensor_tensor(QF[:], QF[:], spread_mid(block01[:], 2), ALU.mult))
                            dve.transpose(QFT[:], QF[:]).then_inc(s["qft"], 1)
                            st.link(dve.tensor_reduce(qs[:], QF[:], AX.X, ALU.add))
                        dve.wait_ge(s["expd"], i + 1)
                        dve.transpose(PT[:], S[:]).then_inc(s["pt"], 1)
                        st.link(dve.tensor_reduce(rsum[:], S[:], AX.X, ALU.add))
                        st.link(dve.reciprocal(smax[:], rsum[:]))
                        dve.wait_ge(s["pv"], i + 2)
                        dve.tensor_tensor(Y[:].rearrange("p t (h d) -> p (t h) d", d=HD),
                                          PS[:, 6, 0:2 * D].rearrange("p (h d) -> p h d", d=HD),
                                          spread(smax[:].rearrange("p t h -> p (t h)"), HD), ALU.mult).then_inc(s["yn"], 1)
                        xi = X[:, bass.ds(i * 2, 2), :]
                        o = PS[:, 2, 0:2 * D].rearrange("p (t d) -> p t d", t=2)
                        if quantum:
                            st.link(dve.reciprocal(qs[:], qs[:]))
                            dve.tensor_tensor(qs[:], qs[:], mixw[:, 0:1].to_broadcast([P, 2]), ALU.mult).then_inc(s["sps"], 1)
                            dve.wait_ge(s["sps"], i + 4)
                            dve.wait_ge(s["qv"], i + 2)
                            for t in range(2):
                                xt_ = X[:, bass.ds(i * 2 + t, 1), :]
                                last = dve.scalar_tensor_tensor(xt_, PS[:, 3, t * D:(t + 1) * D].unsqueeze(1), qs[:, t:t + 1], xt_,
                                                                ALU.mult, ALU.add)
                            st.link(last)
                        dve.wait_ge(s["proj"], i + 1)
                        if quantum:
                            dve.scalar_tensor_tensor(xi, o, mixw[:, 1:2], xi, ALU.mult, ALU.add).then_inc(s["added"], 1)
                        else:
                            dve.tensor_tensor(xi, o, xi, ALU.add).then_inc(s["added"], 1)
                        dve.wait_ge(s["added"], i + 2)
                        st.end()

        def wide_attention():
            WB = 2 * H * 2
            CW = local("CW", [P, 2 * H, WD])
            SW = local("SW", [P, 2 * H * WD])
            QKW = local("QKW", [P, WB, GROUP])
            VW = local("VW", [P, H * WD])
            YTW = local("YTW", [P, 6, P])
            wr, wv, wt, wm = (local(n, [P, 2 * H]) for n in ("wr", "wv", "wt", "wm"))
            k = {n: sem("wide_" + n) for n in ("xts", "qkv", "vcopy", "var", "sq", "log", "start", "turned", "affine",
                                               "score", "expin", "expd", "pt", "pv", "yn", "yt", "ytc", "proj", "added",
                                               "dve")}
            HB = H * WD // 2
            with nc.Block() as block:
                @block.gpsimd
                def _(pool):
                    with pool.Fori(0, TILES) as i:
                        own(pool, k["qkv"], i + 1)
                        pool.tensor_copy(XTs[:, :, 0:P], XT[:, :, bass.ds(i * P, P)]).then_inc(k["xts"], 1)

                @block.tensor
                def _(pe):
                    landed(pe, "w_qkv", "w_proj", "w_projb")
                    for n in ("qkv", "pv"):
                        pe.sem_inc(k[n], 1)
                    with pe.Fori(0, TILES) as i:
                        pe.wait_ge(k["xts"], i + 1)
                        own(pe, k["added"], i + 1)
                        for b in range(6):
                            for c in range(2):
                                last = pe.matmul(PS[:, b, 0:HB], XTs[:, c, 0:P], w_qkv[:, c, b * HB:(b + 1) * HB],
                                                 start=(c == 0), stop=(c == 1))
                        last.then_inc(k["qkv"], 1)
                        own(pe, k["affine"], i * 4 + 4)
                        pe.matmul(PS[:, 6, 0:H * GROUP], identb[:], mask_block[:, 0:H * GROUP], start=True, stop=False,
                                  skip_group_check=True)
                        for h in range(H):
                            for g in range(NG):
                                r = slice(g * GROUP, (g + 1) * GROUP)
                                for d in range(2):
                                    last = pe.matmul(PS[r, 6, h * GROUP:(h + 1) * GROUP],
                                                     SW[r, (2 * h + d) * GROUP:(2 * h + d + 1) * GROUP],
                                                     SW[r, (2 * H + 2 * h + d) * GROUP:(2 * H + 2 * h + d + 1) * GROUP],
                                                     start=False, stop=True, skip_group_check=True)
                        last.then_inc(k["score"], 1)
                        own(pe, k["pt"], i + 1)
                        own(pe, k["vcopy"], i + 1)
                        for h in range(H):
                            for g in range(NG):
                                r = slice(g * GROUP, (g + 1) * GROUP)
                                last = pe.matmul(PS[r, h // 6, (h % 6) * WD:(h % 6 + 1) * WD], PT[r, 0, h, :],
                                                 VW[r, h * WD:(h + 1) * WD], start=True, stop=True, skip_group_check=True)
                        last.then_inc(k["pv"], 1)
                        own(pe, k["yn"], i + 1)
                        for j in range(6):
                            last = pe.transpose(PS[:, 2 + j // 3, (j % 3) * P:(j % 3 + 1) * P],
                                                CW[:].rearrange("p h d -> p (h d)")[:, j * P:(j + 1) * P], ident[:])
                        last.then_inc(k["yt"], 1)
                        own(pe, k["ytc"], i + 1)
                        for j in range(6):
                            pe.matmul(PS[:, 7, 0:D], YTW[:, j, :], w_proj[:, j, :], start=(j == 0), stop=False)
                        pe.matmul(PS[:, 7, 0:D], ones[:], w_projb[:], start=False, stop=True).then_inc(k["proj"], 1)

                @block.scalar
                def _(act):
                    landed(act, "w_affine")
                    with act.Fori(0, TILES) as i:
                        act.wait_ge(k["qkv"], i + 2)
                        own(act, k["pv"], i + 1)
                        act.activation(VW[:].rearrange("p (b n) -> p b n", b=2), PS[:, 4:6, 0:HB], ACT.Copy).then_inc(k["vcopy"], 1)
                        act.wait_ge(k["var"], i * 2 + 1)
                        act.activation(SW[:], CW[:].rearrange("p h d -> p (h d)"), ACT.Square).then_inc(k["sq"], 1)
                        act.wait_ge(k["var"], i * 2 + 2)
                        act.activation(wr[:], wv[:], ACT.Ln).then_inc(k["log"], 1)
                        act.wait_ge(k["log"], i + 1)
                        act.activation(wr[:], wr[:], ACT.Exp, scale=-0.5).then_inc(k["start"], 1)
                        act.wait_ge(k["turned"], i + 1)
                        for j in range(2):
                            for d in range(2):
                                v = SW[:].rearrange("p (j h d n) -> p j h d n", j=2, d=2, n=GROUP)[:, j, :, d, :]
                                act.activation(v, v, ACT.Identity, scale=w_affine[:, 4 * j + d:4 * j + d + 1],
                                               bias=w_affine[:, 4 * j + 2 + d:4 * j + 3 + d]).then_inc(k["affine"], 1)
                        act.wait_ge(k["expin"], i + 1)
                        act.activation(S[:, 0], S[:, 0], ACT.Exp, scale=WD ** -0.5).then_inc(k["expd"], 1)
                        act.wait_ge(k["yt"], i + 1)
                        act.activation(YTW[:].rearrange("p (b j) n -> p b (j n)", b=2), PS[:, 2:4, 0:3 * P],
                                       ACT.Copy).then_inc(k["ytc"], 1)

                @block.vector
                def _(dve):
                    dve.sem_inc(k["added"], 1)
                    with dve.Fori(0, TILES) as i:
                        st = Steps(dve, k["dve"], 12, i)
                        dve.wait_ge(k["qkv"], i + 2)
                        qk = PS[:, 0:4, 0:HB].rearrange("p b (h d) -> p b h d", d=WD)
                        cw = CW[:].rearrange("p (b h) d -> p b h d", b=4)
                        w3 = [x[:].rearrange("p (b h) -> p b h", b=4) for x in (wm, wr)]
                        st.link(dve.tensor_reduce(w3[0], qk, AX.X, ALU.add))
                        st.link(dve.tensor_scalar(wm[:], wm[:], 1.0 / WD, None, ALU.mult))
                        dve.tensor_tensor(cw, qk, spread(w3[0], WD), ALU.subtract).then_inc(k["var"], 1)
                        dve.wait_ge(k["sq"], i + 1)
                        st.link(dve.tensor_reduce(wv[:], SW[:].rearrange("p (h d) -> p h d", d=WD), AX.X, ALU.add))
                        dve.tensor_scalar(wv[:], wv[:], 1.0 / WD, LN_EPS, ALU.mult, ALU.add).then_inc(k["var"], 1)
                        dve.wait_ge(k["start"], i + 1)
                        st.link(dve.tensor_tensor(wt[:], wr[:], wr[:], ALU.mult))
                        st.link(dve.tensor_tensor(wt[:], wt[:], wv[:], ALU.mult))
                        st.link(dve.tensor_scalar(wt[:], wt[:], -0.5, 1.5, ALU.mult, ALU.add))
                        st.link(dve.tensor_tensor(wr[:], wr[:], wt[:], ALU.mult))
                        st.link(dve.tensor_tensor(QKW[:].rearrange("p (h d) n -> p h (d n)", d=2), CW[:], spread(wr[:], WD), ALU.mult))
                        dve.transpose(SW[:].rearrange("p (b n) -> p b n", n=GROUP), QKW[:]).then_inc(k["turned"], 1)
                        dve.wait_ge(k["score"], i + 1)
                        sc_ps = PS[:, 6, 0:H * GROUP].rearrange("p (h j) -> p h j", j=GROUP)
                        st.link(dve.tensor_reduce(smax[:, 0], sc_ps, AX.X, ALU.max))
                        dve.tensor_tensor(S[:, 0], sc_ps, spread(smax[:, 0], GROUP), ALU.subtract).then_inc(k["expin"], 1)
                        dve.wait_ge(k["expd"], i + 1)
                        dve.transpose(PT[:, 0], S[:, 0]).then_inc(k["pt"], 1)
                        st.link(dve.tensor_reduce(rsum[:, 0], S[:, 0], AX.X, ALU.add))
                        st.link(dve.reciprocal(smax[:, 0], rsum[:, 0]))
                        st.link(dve.tensor_tensor(smax[:, 0], smax[:, 0], G[:, bass.ds(i, 1), :].rearrange("p a h -> p (a h)"), ALU.mult))
                        dve.wait_ge(k["pv"], i + 2)
                        dve.tensor_tensor(cw[:, 0:2], PS[:, 0:2, 0:HB].rearrange("p b (h d) -> p b h d", d=WD),
                                          spread(smax[:, 0].rearrange("p (b h) -> p b h", b=2), WD), ALU.mult).then_inc(k["yn"], 1)
                        dve.wait_ge(k["proj"], i + 1)
                        xi = X[:, bass.ds(i, 1), :]
                        dve.tensor_tensor(xi, PS[:, 7:8, 0:D], xi, ALU.add).then_inc(k["added"], 1)
                        dve.wait_ge(k["added"], i + 2)
                        st.end()

        def grassmann_attention():
            k = {n: sem("gr_" + n) for n in ("qk", "qkc", "v", "vc", "to", "back", "a", "q", "qo", "qb", "dve", "mixsum",
                                             "xts", "pad", "qkt", "score", "sq", "dc", "dt", "dtc", "mixed", "expin",
                                             "expd", "pt", "pv", "yn", "yt", "ytc", "proj", "added", "dve2", "sc2", "prep")}
            there = nc.dram_tensor("heads_there", (TOKENS, 2 * D), FP32).ap()
            back = nc.dram_tensor("heads_back", (TOKENS, 2 * D), FP32).ap()
            NM = 2 * (H // 2)
            M = SEQ
            VA = local("VA", [P, TILES, D])
            QT_ = big[:].rearrange("p a b -> p (a b)")
            tok = QT_[:, 0:TILES * 2 * D].rearrange("p (t n) -> p t n", t=TILES)
            A = QT_[:, 3072:6144].rearrange("p (n c d) -> p n c d", n=M, c=NM)
            Q = local("QM", [P, M, NM, M])
            T = QT_[:, 0:3072].rearrange("p (n c d) -> p n c d", n=M, c=NM)
            col = local("qr_col", [P, M, NM])
            w = local("qr_w", [P, NM, M])
            tail, nrm, v0, tau, tmp = (local("qr_" + n, [P, NM]) for n in ("tail", "nrm", "v0", "tau", "tmp"))
            taus = local("qr_taus", [P, M, NM])

            def half_rows(ap, half, which):
                o = which * D + half * KC
                return ap.rearrange("(b n) c -> b n c", n=SEQ)[:, :, o:o + KC]

            with nc.Block() as block:
                @block.tensor
                def _(pe):
                    landed(pe, "l2_qkv")
                    for t in range(TILES):
                        for c in range(2):
                            last = pe.matmul(PS[:, t, 0:2 * D], XT[:, c, t * P:(t + 1) * P], l2_qkv[:, c, 0:2 * D],
                                             start=(c == 0), stop=(c == 1))
                        last.then_inc(k["qk"], 1)
                    for t in range(TILES):
                        pe.wait_ge(k["qkc"], t + 1)
                        for c in range(2):
                            last = pe.matmul(PS[:, t, 0:D], XT[:, c, t * P:(t + 1) * P], l2_qkv[:, c, 2 * D:],
                                             start=(c == 0), stop=(c == 1))
                        last.then_inc(k["v"], 1)

                @block.scalar
                def _(act):
                    for t in range(TILES):
                        act.wait_ge(k["qk"], t + 1)
                        act.activation(tok[:, t, :], PS[:, t, 0:2 * D], ACT.Copy).then_inc(k["qkc"], 1)
                    for t in range(TILES):
                        act.wait_ge(k["v"], t + 1)
                        act.activation(VA[:, t, :], PS[:, t, 0:D], ACT.Copy).then_inc(k["vc"], 1)
                    act.wait_ge(k["vc"], TILES)

                @block.gpsimd
                def _(pool):
                    landed(pool, "mix_a", "mix_b", "half01", "l2_scale")
                    pool.tensor_tensor(mix_a[:], mix_a[:], mix_b[:], ALU.add).then_inc(k["mixsum"], 1)
                    pool.wait_ge(k["mixsum"], 1)
                    pool.tensor_tensor(l2_scale[:, 1:3], half01[:], l2_scale[:, 0:1].to_broadcast([P, 2]), ALU.mult).then_inc(k["mixsum"], 1)
                    pool.wait_ge(k["mixsum"], 2)

                @block.sync
                def _(sp):
                    sp.wait_ge(k["qkc"], TILES)
                    sp.dma_start(there.rearrange("(t p) c -> p t c", p=P), tok).then_inc(k["to"], 16)
                    sp.wait_ge(k["to"], 16)
                    for half in range(2):
                        for which in range(2):
                            sp.dma_start(A[half * 64:(half + 1) * 64, :, which * 6:(which + 1) * 6, :].rearrange("b n c d -> b n (c d)"),
                                         half_rows(there, half, which)).then_inc(k["a"], 16)
                    sp.wait_ge(k["q"], 1)
                    for half in range(2):
                        for which in range(2):
                            sp.dma_start(half_rows(back, half, which),
                                         Q[half * 64:(half + 1) * 64, :, which * 6:(which + 1) * 6, :].rearrange(
                                             "b n c d -> b n (c d)")).then_inc(k["qo"], 16)
                    sp.wait_ge(k["qo"], 64)
                    sp.dma_start(tok, back.rearrange("(t p) c -> p t c", p=P)).then_inc(k["qb"], 16)
                    sp.wait_ge(k["qb"], 16)

                @block.vector
                def _(dve):
                    st = Steps(dve, k["dve"])
                    st.link(dve.memset(Q[:], 0.0))
                    for n in range(M):
                        dve.memset(Q[:, n, :, n], 1.0).then_inc(k["dve"], 1)
                    st.n += M
                    dve.wait_ge(k["dve"], st.n)
                    dve.wait_ge(k["a"], 64)
                    for j in range(M - 1):
                        m = M - j
                        x = A[:, j:M, :, j]
                        cj = col[:, 0:m, :]
                        st.link(dve.tensor_tensor(cj, x, x, ALU.mult))
                        st.link(dve.tensor_reduce(tail[:], cj[:, 1:m, :].rearrange("p n c -> p c n"), AX.X, ALU.add))
                        st.link(dve.tensor_tensor(nrm[:], tail[:], cj[:, 0, :], ALU.add))
                        st.link(dve.tensor_scalar(nrm[:], nrm[:], 1e-37, None, ALU.max))
                        nb_, tb = nrm[:].bitcast(mybir.dt.int32), tmp[:].bitcast(mybir.dt.int32)
                        st.link(dve.tensor_scalar(tb, nb_, 1, None, ALU.arith_shift_right))
                        st.link(dve.tensor_scalar(tb, tb, -1.0, float(0x5F3759DF), ALU.mult, ALU.add))
                        for _ in range(3):
                            st.link(dve.tensor_tensor(v0[:], tmp[:], tmp[:], ALU.mult))
                            st.link(dve.tensor_tensor(v0[:], v0[:], nrm[:], ALU.mult))
                            st.link(dve.tensor_scalar(v0[:], v0[:], -0.5, 1.5, ALU.mult, ALU.add))
                            st.link(dve.tensor_tensor(tmp[:], tmp[:], v0[:], ALU.mult))
                        st.link(dve.tensor_tensor(nrm[:], nrm[:], tmp[:], ALU.mult))
                        st.link(dve.tensor_scalar(tmp[:], A[:, j, :, j], 0.0, 2.0, ALU.is_ge, ALU.mult))
                        st.link(dve.scalar_tensor_tensor(tmp[:], tmp[:], 1.0, nrm[:], ALU.subtract, ALU.mult))
                        st.link(dve.tensor_tensor(A[:, j, :, j], A[:, j, :, j], tmp[:], ALU.add))
                        st.link(dve.tensor_tensor(v0[:], A[:, j, :, j], A[:, j, :, j], ALU.mult))
                        st.link(dve.tensor_tensor(v0[:], v0[:], tail[:], ALU.add))
                        st.link(dve.tensor_scalar(v0[:], v0[:], 1e-37, None, ALU.max))
                        st.link(dve.reciprocal(tau[:], v0[:]))
                        st.link(dve.tensor_scalar(tmp[:], tail[:], 0.0, 2.0, ALU.is_gt, ALU.mult))
                        st.link(dve.tensor_tensor(taus[:, j, :], tau[:], tmp[:], ALU.mult))
                        reflect(dve, st, A, A, T, w, taus, j, j + 1, NM)
                    for j in reversed(range(M - 1)):
                        reflect(dve, st, Q, A, T, w, taus, j, j, NM)
                    dve.sem_inc(k["q"], 1)

            HS = slice(0, SEQ)
            with nc.Block() as block:
                @block.gpsimd
                def _(pool):
                    with pool.Fori(0, PAIRS) as i:
                        own(pool, k["qkt"], i + 1)
                        pool.tensor_copy(QK[:, :, 0:2 * H, 0:HD], tok[:, bass.ds(i * 2, 2), :].rearrange(
                            "p t (h d) -> p t h d", d=HD)).then_inc(k["pad"], 1)
                        own(pool, k["pad"], i * 2 + 1)
                        own(pool, k["pv"], i + 1)
                        pool.tensor_copy(V[:, 0:2 * D].rearrange("p (t d) -> p t d", t=2),
                                         VA[:, bass.ds(i * 2, 2), :]).then_inc(k["pad"], 1)

                @block.tensor
                def _(pe):
                    landed(pe, "l2_proj", "ident", "mix_a")
                    pe.sem_inc(k["pv"], 1)
                    with pe.Fori(0, PAIRS) as i:
                        own(pe, k["qkt"], i + 2)
                        for t in range(2):
                            for h in range(H):
                                for g in range(NG):
                                    r = slice(g * GROUP, g * GROUP + HD)
                                    last = pe.matmul(PS[g * GROUP:(g + 1) * GROUP, 4 + t, h * GROUP:(h + 1) * GROUP],
                                                     QKT[r, t, h, :], QKT[r, t, H + h, :], start=True, stop=True,
                                                     skip_group_check=True)
                        last.then_inc(k["score"], 1)
                        own(pe, k["dc"], i + 1)
                        for t in range(2):
                            for c in range(2):
                                last = pe.transpose(PS[0:KC, 7, c * 2 * P + t * P:c * 2 * P + (t + 1) * P],
                                                    Y[:, t, c * KC:(c + 1) * KC], ident[:])
                        last.then_inc(k["dt"], 1)
                        own(pe, k["dtc"], i + 1)
                        for t in range(2):
                            for c in range(2):
                                last = pe.matmul(PS[:, 2, t * D:(t + 1) * D], YT[:, c, t * P:(t + 1) * P], mix_a[:, c, :],
                                                 start=(c == 0), stop=(c == 1))
                        last.then_inc(k["mixed"], 1)
                        own(pe, k["pt"], i + 1)
                        own(pe, k["pad"], i * 2 + 2)
                        for t in range(2):
                            for h in range(H):
                                for g in range(NG):
                                    r = slice(g * GROUP, (g + 1) * GROUP)
                                    last = pe.matmul(PS[r, 6, t * D + h * HD:t * D + (h + 1) * HD], PT[r, t, h, :],
                                                     V[r, t * D + h * HD:t * D + (h + 1) * HD],
                                                     start=True, stop=True, skip_group_check=True)
                        last.then_inc(k["pv"], 1)
                        own(pe, k["yn"], i + 1)
                        for t in range(2):
                            for c in range(2):
                                last = pe.transpose(PS[0:KC, 7, c * 2 * P + t * P:c * 2 * P + (t + 1) * P],
                                                    Y[:, t, c * KC:(c + 1) * KC], ident[:])
                        last.then_inc(k["yt"], 1)
                        own(pe, k["ytc"], i + 1)
                        for t in range(2):
                            for c in range(2):
                                last = pe.matmul(PS[:, 2, t * D:(t + 1) * D], YT[:, c, t * P:(t + 1) * P],
                                                 l2_proj[:, c, :], start=(c == 0), stop=(c == 1))
                        last.then_inc(k["proj"], 1)

                @block.scalar
                def _(act):
                    with act.Fori(0, PAIRS) as i:
                        act.wait_ge(k["score"], i + 1)
                        act.activation(S[:], PS[:, 4:6, 0:H * GROUP].rearrange("p t (h j) -> p t h j", j=GROUP),
                                       ACT.Square).then_inc(k["sq"], 1)
                        act.wait_ge(k["dt"], i + 1)
                        act.activation(YT[0:KC, :, :], PS[0:KC, 7, :].rearrange("p (c n) -> p c n", c=2),
                                       ACT.Copy).then_inc(k["dtc"], 1)
                        act.wait_ge(k["expin"], i + 1)
                        act.activation(SQ[:, 0:2 * H, :], SQ[:, 0:2 * H, :], ACT.Exp).then_inc(k["expd"], 1)
                        act.wait_ge(k["yt"], i + 1)
                        act.activation(YT[0:KC, :, :], PS[0:KC, 7, :].rearrange("p (c n) -> p c n", c=2),
                                       ACT.Copy).then_inc(k["ytc"], 1)

                @block.vector
                def _(dve):
                    dve.sem_inc(k["qkt"], 1)
                    with dve.Fori(0, PAIRS) as i:
                        st = Steps(dve, k["dve2"], 6, i)
                        own(dve, k["pad"], i * 2 + 1)
                        dve.transpose(QKT[:, :, 0:2 * H, :], QK[:, :, 0:2 * H, :]).then_inc(k["qkt"], 1)
                        dve.wait_ge(k["sq"], i + 1)
                        yv = Y[:].rearrange("p t (h j) -> p (t h) j", j=SEQ)
                        sv = S[:].rearrange("p t h j -> p (t h) j")
                        st.link(dve.tensor_scalar(yv, sv[:, :, 0:SEQ], l2_scale[:, 1:2], None, ALU.mult))
                        dve.scalar_tensor_tensor(yv, sv[:, :, SEQ:GROUP], l2_scale[:, 2:3], yv, ALU.mult, ALU.add).then_inc(k["dc"], 1)
                        dve.wait_ge(k["mixed"], i + 1)
                        mx = PS[:, 2, 0:2 * D].rearrange("p (h j) -> p h j", j=SEQ)
                        m_ = SQ[:, 0:2 * H, :]
                        sm, rs = (x[:].rearrange("p t h -> p (t h)") for x in (smax, rsum))
                        st.link(dve.tensor_reduce(sm, mx, AX.X, ALU.max))
                        dve.tensor_tensor(m_, mx, spread(sm, SEQ), ALU.subtract).then_inc(k["expin"], 1)
                        dve.wait_ge(k["expd"], i + 1)
                        st.link(dve.tensor_scalar(sv[:, :, 0:SEQ], m_, half01[:, 0:1], None, ALU.mult))
                        st.link(dve.tensor_scalar(sv[:, :, SEQ:GROUP], m_, half01[:, 1:2], None, ALU.mult))
                        st.link(dve.tensor_reduce(rs, m_, AX.X, ALU.add))
                        dve.transpose(PT[:], S[:]).then_inc(k["pt"], 1)
                        st.link(dve.reciprocal(sm, rs))
                        dve.wait_ge(k["pv"], i + 2)
                        dve.tensor_tensor(yv, PS[:, 6, 0:2 * D].rearrange("p (h d) -> p h d", d=HD),
                                          spread(sm, HD), ALU.mult).then_inc(k["yn"], 1)
                        dve.wait_ge(k["proj"], i + 1)
                        xi = X[:, bass.ds(i * 2, 2), :]
                        dve.tensor_tensor(xi, PS[:, 2, 0:2 * D].rearrange("p (t d) -> p t d", t=2), xi, ALU.add).then_inc(k["added"], 1)
                        dve.wait_ge(k["added"], i + 1)
                        st.end()

        def quantised_ffn():
            am, amt, diag, sc = local("am", [P, 2]), local("amt", [2, 1]), local("diag", [2, 2]), local("wscale", [P, 4])
            inv = local("wscale_inv", [P, 4])
            ones2 = local("ones2", [2, P])
            fy = local("fy", [P, PAIRS, 2 * D])
            k = {n: sem("ff_" + n) for n in ("dve", "am", "amt", "diag", "scales", "w1q", "w2q", "hid", "gelu", "hq",
                                             "y", "zero", "done")}
            with nc.Block() as block:
                @block.gpsimd
                def _(pool):
                    pool.memset(am[:], 0.0).then_inc(k["zero"], 1)
                    pool.wait_ge(k["zero"], 1)
                    pool.memset(ones2[:], 1.0).then_inc(k["zero"], 1)
                    pool.wait_ge(k["zero"], 2)

                @block.tensor
                def _(pe):
                    landed(pe, "ident", "ff_b2")
                    pe.wait_ge(k["am"], 2)
                    pe.transpose(PS[0:2, 7, 0:P], am[:], ident[:]).then_inc(k["amt"], 1)
                    pe.wait_ge(k["diag"], 1)
                    pe.matmul(PS[:, 6, 0:2], ones2[:], diag[:], start=True, stop=True).then_inc(k["scales"], 1)
                    pe.wait_ge(k["w1q"], 1)
                    n = 0
                    for f in range(FC):
                        for half in range(2):
                            if n >= 4:
                                pe.wait_ge(k["gelu"], n - 3)
                            for c in range(2):
                                last = pe.matmul(PS[:, n % 4, :], ff_w1[:, c, f * P:(f + 1) * P],
                                                 XT[0:KC, c, half * BANK:(half + 1) * BANK],
                                                 start=(c == 0), stop=(c == 1))
                            last.then_inc(k["hid"], 1)
                            n += 1
                    pe.wait_ge(k["w2q"], 1)
                    pe.wait_ge(k["hq"], 2 * FC)
                    for m in range(PAIRS):
                        for t in range(2):
                            o = PS[:, 4 + m, t * D:(t + 1) * D]
                            for f in range(FC):
                                pe.matmul(o, big[:, f, (2 * m + t) * P:(2 * m + t + 1) * P], ff_w2[:, f, :],
                                          start=(f == 0), stop=False)
                            last = pe.matmul(o, ones[:], ff_b2[:], start=False, stop=True)
                        last.then_inc(k["y"], 1)

                @block.scalar
                def _(act):
                    landed(act, "ff_b1")
                    for n in range(2 * FC):
                        act.wait_ge(k["hid"], n + 1)
                        f, half = n // 2, n % 2
                        act.activation(big[:, f, half * BANK:(half + 1) * BANK], PS[:, n % 4, :], ACT.Gelu,
                                       bias=ff_b1[:, f:f + 1]).then_inc(k["gelu"], 1)

                @block.vector
                def _(dve):
                    st = Steps(dve, k["dve"])
                    landed(dve, "ff_w1", "ff_w2", "ff_s", "ident")
                    dve.wait_ge(k["zero"], 2)
                    dve.tensor_reduce(am[0:KC, 0:1], ff_w1[:], AX.XY, ALU.max, apply_absolute_value=True).then_inc(k["am"], 1)
                    dve.tensor_reduce(am[:, 1:2], ff_w2[:], AX.XY, ALU.max, apply_absolute_value=True).then_inc(k["am"], 1)
                    dve.wait_ge(k["amt"], 1)
                    st.link(dve.tensor_reduce(amt[:], PS[0:2, 7, 0:P], AX.X, ALU.max))
                    dve.tensor_scalar(diag[:], ident[0:2, 0:2], amt[:], None, ALU.mult).then_inc(k["diag"], 1)
                    dve.wait_ge(k["scales"], 1)
                    st.link(dve.tensor_scalar(sc[:, 0:2], PS[:, 6, 0:2], 1.0 / 127.0, None, ALU.mult))
                    st.link(dve.tensor_copy(sc[:, 2:4], ff_s[:]))
                    st.link(dve.reciprocal(inv[:], sc[:]))

                    def fake_quantise(dst, src, n, low, done):
                        rows_ = dst.shape[0]
                        scale = sc[0:rows_, n:n + 1]
                        st.link(dve.tensor_scalar(dst, src, inv[0:rows_, n:n + 1], MAGIC, ALU.mult, ALU.add))
                        st.link(dve.tensor_scalar(dst, dst, -MAGIC, 127.0, ALU.add, ALU.min))
                        ins = dve.tensor_scalar(dst, dst, low, scale, ALU.max, ALU.mult)
                        if done is None:
                            st.link(ins)
                        else:
                            ins.then_inc(done, 1)

                    fake_quantise(ff_w1[:], ff_w1[:], 0, -127.0, k["w1q"])
                    fake_quantise(ff_w2[:], ff_w2[:], 1, -127.0, k["w2q"])
                    for n in range(2 * FC):
                        dve.wait_ge(k["gelu"], n + 1)
                        f, half = n // 2, n % 2
                        h = big[:, f, half * BANK:(half + 1) * BANK]
                        fake_quantise(h, h, 2, -128.0, k["hq"])
                    for m in range(PAIRS):
                        dve.wait_ge(k["y"], m + 1)
                        fake_quantise(fy[:, m, :], PS[:, 4 + m, 0:2 * D], 3, -128.0, None)
                        xm = X[:, 2 * m:2 * m + 2, :]
                        dve.tensor_tensor(xm, xm, fy[:, m, :].rearrange("p (t d) -> p t d", t=2), ALU.add).then_inc(k["done"], 1)
                    dve.wait_ge(k["done"], PAIRS)

        GL, GA, GB = (sb(n, [P, TILES, 14]) for n in ("GL", "GA", "GB"))
        top8 = sb("top8", [P, TILES, 8])
        topi = sb("topi", [P, TILES, 8], U32)
        topf = sb("topf", [P, TILES, 8])
        G = sb("G", [P, TILES, H])
        gm, gs_ = sb("gm", [P, TILES, 1]), sb("gs", [P, TILES, 1])

        def gates(name, wg, wname, ncol, kind):
            k = {n: sem(f"{name}_{n}") for n in ("dve", "logits", "less", "exp")}
            soft = {"heads": ((0, 10), (10, 12), (12, 14)), "moe": ((0, E),), "shared": ((0, E),)}[kind]
            ne = soft[0][1]
            with nc.Block() as block:
                @block.tensor
                def _(pe):
                    landed(pe, wname)
                    for t in range(TILES):
                        for c in range(2):
                            last = pe.matmul(PS[:, 7, t * ncol:(t + 1) * ncol], XT[:, c, t * P:(t + 1) * P], wg[:, c, :],
                                             start=(c == 0), stop=(c == 1), skip_group_check=True)
                    last.then_inc(k["logits"], 1)

                @block.scalar
                def _(act):
                    act.wait_ge(k["less"], 1)
                    act.activation(GA[:, :, 0:ncol], GL[:, :, 0:ncol], ACT.Exp).then_inc(k["exp"], 1)

                @block.vector
                def _(dve):
                    landed(dve, "iota10")
                    st = Steps(dve, k["dve"])
                    dve.wait_ge(k["logits"], 1)
                    st.link(dve.tensor_copy(GL[:, :, 0:ncol], PS[:, 7, 0:TILES * ncol].rearrange("p (t e) -> p t e", t=TILES)))
                    for a, b in soft:
                        st.link(dve.tensor_reduce(gm[:, :, 0], GL[:, :, a:b], AX.X, ALU.max))
                        st.link(dve.tensor_tensor(GL[:, :, a:b], GL[:, :, a:b], spread(gm[:, :, 0], b - a), ALU.subtract))
                    if kind == "shared":
                        st.link(dve.tensor_scalar(GL[:, :, E], GL[:, :, E], -1.0, None, ALU.mult))
                    st.link(dve.tensor_scalar(GB[:, :, 0:1], GL[:, :, 0:1], 1.0, None, ALU.mult))
                    dve.sem_inc(k["less"], 1)
                    dve.wait_ge(k["exp"], 1)
                    for a, b in soft:
                        st.link(dve.tensor_reduce(gs_[:, :, 0], GA[:, :, a:b], AX.X, ALU.add))
                        st.link(dve.reciprocal(gm[:], gs_[:]))
                        st.link(dve.tensor_tensor(GA[:, :, a:b], GA[:, :, a:b], spread(gm[:, :, 0], b - a), ALU.mult))
                    for t in range(TILES):
                        dve.max(top8[:, t, :], GA[:, t, 0:ne]).then_inc(k["dve"], 1)
                    st.n += TILES
                    dve.wait_ge(k["dve"], st.n)
                    for t in range(TILES):
                        dve.max_index(topi[:, t, :], top8[:, t, :], GA[:, t, 0:ne]).then_inc(k["dve"], 1)
                    st.n += TILES
                    dve.wait_ge(k["dve"], st.n)
                    st.link(dve.tensor_copy(topf[:], topi[:]))
                    for t in range(TILES):
                        dve.scalar_tensor_tensor(GL[:, t, 0:ne], iota10[:, 0:ne], topf[:, t, 0:1], GA[:, t, 0:ne],
                                                 ALU.is_equal, ALU.mult).then_inc(k["dve"], 1)
                        dve.scalar_tensor_tensor(GB[:, t, 0:ne], iota10[:, 0:ne], topf[:, t, 1:2], GA[:, t, 0:ne],
                                                 ALU.is_equal, ALU.mult).then_inc(k["dve"], 1)
                    st.n += 2 * TILES
                    dve.wait_ge(k["dve"], st.n)
                    st.link(dve.tensor_tensor(GL[:, :, 0:ne], GL[:, :, 0:ne], GB[:, :, 0:ne], ALU.add))
                    if kind == "moe":
                        st.link(dve.tensor_copy(G[:, :, 0:E], GL[:, :, 0:E]))
                        return
                    st.link(dve.tensor_reduce(gs_[:, :, 0], GL[:, :, 0:ne], AX.X, ALU.add))
                    if kind == "heads":
                        eps = float(np.finfo(np.float32).eps)
                        st.link(dve.tensor_scalar(gs_[:], gs_[:], eps, None, ALU.max))
                    st.link(dve.reciprocal(gm[:], gs_[:]))
                    if kind == "heads":
                        st.link(dve.tensor_scalar(GA[:, :, 12:14], GA[:, :, 12:14], 4.0, None, ALU.mult))
                        st.link(dve.tensor_tensor(gm[:, :, 0], gm[:, :, 0], GA[:, :, 13], ALU.mult))
                        st.link(dve.tensor_tensor(G[:, :, 2:H], GL[:, :, 0:10], spread(gm[:, :, 0], 10), ALU.mult))
                        st.link(dve.tensor_tensor(G[:, :, 0:2], GA[:, :, 10:12], spread(GA[:, :, 12], 2), ALU.mult))
                    else:
                        st.link(dve.tensor_scalar(gs_[:, :, 0], GA[:, :, E], 1.0, None, ALU.add))
                        st.link(dve.reciprocal(GB[:, :, 0:1], gs_[:]))
                        st.link(dve.tensor_copy(G[:, :, E:H], spread(GB[:, :, 0], H - E)))
                        st.link(dve.tensor_scalar(GB[:, :, 1], GB[:, :, 0], -1.0, 1.0, ALU.mult, ALU.add))
                        st.link(dve.tensor_tensor(gm[:, :, 0], gm[:, :, 0], GB[:, :, 1], ALU.mult))
                        st.link(dve.tensor_tensor(G[:, :, 0:E], GL[:, :, 0:E], spread(gm[:, :, 0], E), ALU.mult))

        GT = sb("GT", [E, TOKENS])
        GX = sb("GX", [P, H, TILES])

        def expert_bias():
            k = {n: sem("eb_" + n) for n in ("gx", "gt", "gtc", "b", "done")}
            with nc.Block() as block:
                @block.tensor
                def _(pe):
                    landed(pe, "ident", "moe_b2")
                    for t in range(TILES):
                        last = pe.transpose(PS[0:E, t // 4, (t % 4) * P:(t % 4 + 1) * P], G[:, t, 0:E], ident[:])
                    last.then_inc(k["gt"], 1)
                    pe.wait_ge(k["gtc"], 2)
                    for t in range(TILES):
                        last = pe.matmul(PS[:, 2 + t // 2, (t % 2) * D:(t % 2 + 1) * D], GT[:, t * P:(t + 1) * P], moe_b2[:],
                                         start=True, stop=True)
                    last.then_inc(k["b"], 1)

                @block.scalar
                def _(act):
                    act.wait_ge(k["gt"], 1)
                    for b in range(2):
                        act.activation(GT[:, b * BANK:(b + 1) * BANK], PS[0:E, b, :], ACT.Copy).then_inc(k["gtc"], 1)
                    act.wait_ge(k["gtc"], 2)

                @block.vector
                def _(dve):
                    dve.tensor_copy(GX[:, 0:E, :].rearrange("p e t -> p t e"), G[:, :, 0:E]).then_inc(k["gx"], 1)
                    dve.wait_ge(k["b"], 1)
                    for m in range(PAIRS):
                        xm = X[:, 2 * m:2 * m + 2, :]
                        dve.tensor_tensor(xm, PS[:, 2 + m, 0:2 * D].rearrange("p (t d) -> p t d", t=2), xm,
                                          ALU.add).then_inc(k["done"], 1)
                    dve.wait_ge(k["done"], PAIRS)
                    dve.wait_ge(k["gx"], 1)

        HALF_TILES = TILES // 2

        def gelu_experts():
            k = {n: sem("moe_" + n) for n in ("w1a", "w1b", "w2a", "w2b", "hid", "gelu", "y", "sum")}
            w1 = [local(f"moe_w1_{j}", [KB, 2, FF]) for j in range(2)]
            w2 = [local(f"moe_w2_{j}", [P, FC, D]) for j in range(2)]
            hT = big[:].rearrange("p f (h n) -> p h f n", h=2)
            in1, in2 = (k["w1a"], k["w1b"]), (k["w2a"], k["w2b"])
            steps = [(j, half) for j in range(2) for half in range(2)]
            NS = len(steps)
            with nc.Block() as block:
                @block.sync
                def _(sp):
                    with sp.Fori(0, E // 2) as i:
                        for j in range(2):
                            sp.wait_ge(k["y"], i * NS + 2 * j + 1)
                            sp.dma_start(w1[j][:].unsqueeze(1), I["moe_w1"].rearrange("e p c n -> p e c n")[:, bass.ds(i * 2 + j, 1)]).then_inc(in1[j], 16)
                            sp.dma_start(w2[j][:].unsqueeze(1), I["moe_w2"].rearrange("e p c n -> p e c n")[:, bass.ds(i * 2 + j, 1)]).then_inc(in2[j], 16)

                @block.tensor
                def _(pe):
                    pe.sem_inc(k["y"], 3)
                    with pe.Fori(0, E // 2) as i:
                        def hidden(n):
                            j, half = steps[n]
                            if half == 0:
                                pe.wait_ge(in1[j], i * 16 + 16)
                            for f in range(FC):
                                pe.wait_ge(k["gelu"], i * (NS * FC) + n * FC + f + 1)
                                for c in range(2):
                                    last = pe.matmul(PS[:, (n * FC + f) % 4, :], w1[j][:, c, f * P:(f + 1) * P],
                                                     XT[:, c, half * BANK:(half + 1) * BANK], start=(c == 0), stop=(c == 1))
                                last.then_inc(k["hid"], 1)

                        def second(n):
                            j, half = steps[n]
                            if half == 0:
                                pe.wait_ge(in2[j], i * 16 + 16)
                            pe.wait_ge(k["gelu"], i * (NS * FC) + (n + 1) * FC + 4)
                            own(pe, k["sum"], i * (NS * HALF_TILES) + (n + 1) * HALF_TILES)
                            for t in range(HALF_TILES):
                                for f in range(FC):
                                    last = pe.matmul(PS[:, 4 + 2 * half + t // 2, (t % 2) * D:(t % 2 + 1) * D],
                                                     hT[:, half, f, t * P:(t + 1) * P], w2[j][:, f, :],
                                                     start=(f == 0), stop=(f == FC - 1))
                            last.then_inc(k["y"], 1)

                        hidden(0)
                        for n in range(1, NS):
                            hidden(n)
                            second(n - 1)
                        second(NS - 1)

                @block.scalar
                def _(act):
                    act.sem_inc(k["gelu"], 4)
                    with act.Fori(0, E // 2) as i:
                        for n, (j, half) in enumerate(steps):
                            own(act, k["y"], i * NS + n + 2)
                            for f in range(FC):
                                act.wait_ge(k["hid"], i * (NS * FC) + n * FC + f + 1)
                                act.activation(hT[:, half, f, :], PS[:, (n * FC + f) % 4, :], ACT.Gelu).then_inc(k["gelu"], 1)

                @block.vector
                def _(dve):
                    dve.sem_inc(k["sum"], 2 * HALF_TILES)
                    with dve.Fori(0, E // 2) as i:
                        for n, (j, half) in enumerate(steps):
                            dve.wait_ge(k["y"], i * NS + n + 4)
                            own(dve, k["sum"], i * (NS * HALF_TILES) + (n + 2) * HALF_TILES)
                            for t in range(HALF_TILES):
                                xt = X[:, half * HALF_TILES + t, :]
                                dve.scalar_tensor_tensor(xt, PS[:, 4 + 2 * half + t // 2, (t % 2) * D:(t % 2 + 1) * D],
                                                         GX[:, bass.ds(i * 2 + j, 1), half * HALF_TILES + t], xt, ALU.mult,
                                                         ALU.add).then_inc(k["sum"], 1)
                    dve.wait_ge(k["sum"], (E * 2 + 2) * HALF_TILES)

        def silu_experts():
            k = {n: sem("glu_" + n) for n in ("w1a", "w1b", "w2a", "w2b", "hid", "silu", "h", "y", "sum", "gx")}
            gu = [local(f"gu_{j}", [KC, 2, 2 * D]) for j in range(2)]
            dn = [local(f"dn_{j}", [KC, 2, D]) for j in range(2)]
            sg = local("sg", [KC, 2, BANK])
            hT = big[0:KC, 0:4, 0:BANK].rearrange("p (h c) n -> p h c n", h=2)
            in1, in2 = (k["w1a"], k["w1b"]), (k["w2a"], k["w2b"])
            steps = [(j, half) for j in range(2) for half in range(2)]
            NS = len(steps)
            TURNS = H // 2
            with nc.Block() as block:
                @block.sync
                def _(sp):
                    with sp.Fori(0, TURNS) as i:
                        for j in range(2):
                            sp.wait_ge(k["y"], i * NS + 2 * j + 1)
                            sp.dma_start(gu[j][:].unsqueeze(1), I["gu"].rearrange("e p c n -> p e c n")[:, bass.ds(i * 2 + j, 1)]).then_inc(in1[j], 16)
                            sp.dma_start(dn[j][:].unsqueeze(1), I["down"].rearrange("e p c n -> p e c n")[:, bass.ds(i * 2 + j, 1)]).then_inc(in2[j], 16)

                @block.tensor
                def _(pe):
                    pe.sem_inc(k["y"], 3)
                    with pe.Fori(0, TURNS) as i:
                        def hidden(n):
                            j, half = steps[n]
                            if half == 0:
                                pe.wait_ge(in1[j], i * 16 + 16)
                            for u in range(2):
                                pe.wait_ge(k["h"], i * (2 * NS) + 2 * n + u + 1)
                                for which in range(2):
                                    for c in range(2):
                                        last = pe.matmul(PS[0:KC, 2 * u + which, :],
                                                         gu[j][:, c, which * D + u * KC:which * D + (u + 1) * KC],
                                                         XT[0:KC, c, half * BANK:(half + 1) * BANK],
                                                         start=(c == 0), stop=(c == 1))
                                last.then_inc(k["hid"], 1)

                        def second(n):
                            j, half = steps[n]
                            if half == 0:
                                pe.wait_ge(in2[j], i * 16 + 16)
                            pe.wait_ge(k["h"], i * (2 * NS) + 2 * (n + 1) + 2)
                            own(pe, k["sum"], i * (NS * HALF_TILES) + (n + 1) * HALF_TILES)
                            for t in range(HALF_TILES):
                                for c in range(2):
                                    last = pe.matmul(PS[:, 4 + 2 * half + t // 2, (t % 2) * D:(t % 2 + 1) * D],
                                                     hT[:, half, c, t * P:(t + 1) * P], dn[j][:, c, :],
                                                     start=(c == 0), stop=(c == 1))
                            last.then_inc(k["y"], 1)

                        hidden(0)
                        for n in range(1, NS):
                            hidden(n)
                            second(n - 1)
                        second(NS - 1)

                @block.scalar
                def _(act):
                    with act.Fori(0, TURNS) as i:
                        for n in range(NS):
                            for u in range(2):
                                act.wait_ge(k["hid"], i * (2 * NS) + 2 * n + u + 1)
                                act.activation(sg[:, u, :], PS[0:KC, 2 * u, :], ACT.Silu).then_inc(k["silu"], 1)

                @block.vector
                def _(dve):
                    dve.tensor_copy(GX[:].rearrange("p e t -> p t e"), G[:]).then_inc(k["gx"], 1)
                    dve.wait_ge(k["gx"], 1)
                    dve.sem_inc(k["h"], 2)
                    dve.sem_inc(k["sum"], 2 * HALF_TILES)
                    with dve.Fori(0, TURNS) as i:
                        def product(n):
                            j, half = steps[n]
                            dve.wait_ge(k["y"], i * NS + n + 2)
                            for u in range(2):
                                dve.wait_ge(k["silu"], i * (2 * NS) + 2 * n + u + 1)
                                dve.tensor_tensor(hT[:, half, u, :], PS[0:KC, 2 * u + 1, :], sg[:, u, :], ALU.mult).then_inc(k["h"], 1)

                        def add(n):
                            j, half = steps[n]
                            dve.wait_ge(k["y"], i * NS + n + 4)
                            own(dve, k["sum"], i * (NS * HALF_TILES) + (n + 2) * HALF_TILES)
                            for t in range(HALF_TILES):
                                xt = X[:, half * HALF_TILES + t, :]
                                dve.scalar_tensor_tensor(xt, PS[:, 4 + 2 * half + t // 2, (t % 2) * D:(t % 2 + 1) * D],
                                                         GX[:, bass.ds(i * 2 + j, 1), half * HALF_TILES + t], xt, ALU.mult,
                                                         ALU.add).then_inc(k["sum"], 1)

                        product(0)
                        for n in range(1, NS):
                            product(n)
                            add(n - 1)
                        add(NS - 1)
                    dve.wait_ge(k["sum"], (TURNS * NS + 2) * HALF_TILES)

        def store():
            stored = sem("stored")
            with nc.Block() as block:
                @block.sync
                def _(sp):
                    landed(sp, *plan)
                    sp.dma_start(out.rearrange("(t p) d -> p t d", p=P), X[:]).then_inc(stored, 16)
                    sp.wait_ge(stored, 16)

        if stop == 0:
            return store()
        attention("l0", l0_qkv, l0_proj, ("l0_qkv", "l0_proj"), mask_causal, causal_rel=True)
        end_phase()
        norm_and_transpose("n0")
        end_phase()
        if stop == 1:
            return store()
        quantised_ffn()
        end_phase()
        norm_and_transpose("n1")
        end_phase()
        if stop == 2:
            return store()
        attention("l1", l1_qkv, l1_proj, ("l1_qkv", "l1_proj"), mask_block, head_norm=True)
        end_phase()
        norm_and_transpose("n2")
        end_phase()
        if stop == 3:
            return store()
        gates("heads", w_gates, "w_gates", 14, "heads")
        end_phase()
        wide_attention()
        end_phase()
        norm_and_transpose("n3")
        end_phase()
        if stop == 4:
            return store()
        grassmann_attention()
        end_phase()
        norm_and_transpose("n4")
        end_phase()
        if stop == 5:
            return store()
        gates("moe", moe_g, "moe_g", E, "moe")
        end_phase()
        expert_bias()
        end_phase()
        gelu_experts()
        end_phase()
        norm_and_transpose("n5")
        end_phase()
        if stop == 6:
            return store()
        attention("l3", l3_qkv, l3_proj, ("l3_qkv", "l3_proj"), mask_block, quantum=True)
        end_phase()
        norm_and_transpose("n6")
        end_phase()
        if stop == 7:
            return store()
        gates("shared", l3_gates, "l3_gates", E + 1, "shared")
        end_phase()
        silu_experts()
        end_phase()
        norm_and_transpose("n7", transpose=False)
        end_phase()
        return store()


def lay_out(a):
    f = np.float32

    def chunks(w, b=None):
        m = w.shape[1]
        r = np.zeros((KB, 2, m), f)
        r[:KC, 0], r[:KC, 1] = w[:KC], w[KC:]
        if b is not None:
            r[KC, 0] = b
        return r

    def rows(w):
        return np.ascontiguousarray(w.reshape(-1, P, w.shape[1]).transpose(1, 0, 2))

    def every(v):
        return np.ascontiguousarray(np.broadcast_to(np.reshape(v, (1, -1)), (P, np.size(v))))

    x = a["x"].reshape(IMAGES, 4, 16, 4, 16, 3).transpose(0, 1, 3, 2, 4, 5).reshape(TOKENS, FF)
    o = {"patches": rows(np.ascontiguousarray(x.T))}
    o["tok_w"] = rows(a["L0_tok_W"])
    o["pos"] = np.tile(a["L0_tok_pos_emb"], (P // SEQ, 1))
    o["tok_b"] = every(a["L0_tok_b"])
    o["ident"] = np.eye(P, dtype=f)
    n = np.arange(P)[:, None]
    j = np.arange(GROUP)[None, :]
    same = (n % GROUP) // SEQ == j // SEQ
    off = -30000.0
    block = np.where(same, 0.0, off)
    causal = np.where(same & (j % SEQ <= n % SEQ), 0.0, off)
    o["keys_causal"] = causal.astype(f)
    o["keys_block"] = block.astype(f)
    o["block01"] = same.astype(f)
    o["half01"] = np.concatenate([(n % GROUP < SEQ), (n % GROUP >= SEQ)], 1).astype(f)
    o["rel"] = np.tile(np.concatenate([np.zeros((1, HD), f), a["L0_attn_rel_emb"][:SEQ - 1]]), (P // SEQ, 1))
    o["l0_qkv"] = chunks(a["L0_attn_w_attn"], a["L0_attn_b_attn"])
    o["l0_proj"] = chunks(a["L0_attn_w_proj"], a["L0_attn_b_proj"])
    o["ff_w1"] = np.ascontiguousarray(a["L0_ffn_W1"].T.reshape(2, KC, FF).transpose(1, 0, 2))
    o["ff_b1"] = np.ascontiguousarray(a["L0_ffn_b1"].reshape(FC, P).T)
    o["ff_w2"] = rows(np.ascontiguousarray(a["L0_ffn_W2"].T))
    o["ff_b2"] = a["L0_ffn_b2"].reshape(1, D)
    o["ff_s"] = every(np.stack([np.reshape(a["L0_ffn_s_gelu"], ()), np.reshape(a["L0_ffn_s_out"], ())]))
    o["l1_qkv"] = chunks(a["L1_attn_qkv_weight"].T)
    o["l1_proj"] = chunks(a["L1_attn_proj_weight"].T)
    o["w_qkv"] = chunks(a["L1_ffn_qkv_w"], a["L1_ffn_qkv_b"])
    o["w_proj"] = rows(a["L1_ffn_proj_w"])
    o["w_projb"] = a["L1_ffn_proj_b"].reshape(1, D)
    o["w_gates"] = chunks(np.concatenate([a["L1_ffn_wg_w"], a["L1_ffn_wg1_w"], a["L1_ffn_wg0_w"]], 1))
    o["w_affine"] = np.stack([np.tile(a[k].reshape(2, GROUP)[d], NG) for k in (
        "L1_ffn_q_norm_w", "L1_ffn_q_norm_b", "L1_ffn_k_norm_w", "L1_ffn_k_norm_b") for d in range(2)], 1)
    o["iota10"] = np.broadcast_to(np.arange(10, dtype=f), (P, 10))
    o["l2_qkv"] = chunks(a["L2_attn_qkv_w"].T, a["L2_attn_qkv_b"])
    o["l2_proj"] = chunks(a["L2_attn_proj_w"].T, a["L2_attn_proj_b"])
    o["l2_scale"] = np.concatenate([every(a["L2_attn_grassman_scale"]), np.zeros((P, 2), f)], 1)

    def mixing(w, b):
        m = np.zeros((H, SEQ, H, SEQ), f)
        for key in range(SEQ):
            m[:, key, :, key] = w.T
        return chunks(m.reshape(D, D), b)

    o["mix_a"] = mixing(a["L2_attn_conv_w"][:, :H], np.repeat(a["L2_attn_conv_b"], SEQ))
    o["mix_b"] = mixing(a["L2_attn_conv_w"][:, H:], None)
    o["moe_g"] = chunks(a["L2_ffn_Wg"], a["L2_ffn_bg"])
    o["moe_b2"] = a["L2_ffn_b2"]
    o["moe_w1"] = np.stack([chunks(a["L2_ffn_W1"][e], a["L2_ffn_b1"][e]) for e in range(E)])
    o["moe_w2"] = np.stack([rows(a["L2_ffn_W2"][e]) for e in range(E)])
    o["l3_qkv"] = chunks(np.concatenate([a["L3_attn_in_w"].T[:, :2 * D], a["L3_attn_sp_w"].T, a["L3_attn_in_w"].T[:, 2 * D:]], 1),
                         np.concatenate([a["L3_attn_in_b"][:2 * D], a["L3_attn_sp_b"], a["L3_attn_in_b"][2 * D:]]))
    o["l3_proj"] = chunks(a["L3_attn_out_w"].T, a["L3_attn_out_b"])
    o["l3_qw"] = every(a["L3_attn_qw"])
    o["l3_gates"] = chunks(np.concatenate([a["L3_ffn_router_w"], a["L3_ffn_sg_w"]], 1),
                           np.concatenate([np.zeros(E, f), a["L3_ffn_sg_b"]]))
    gate = np.concatenate([a["L3_ffn_w_gate"], a["L3_ffn_ws_gate"].reshape(D, 4, D).transpose(1, 0, 2)])
    up = np.concatenate([a["L3_ffn_w_up"], a["L3_ffn_ws_up"].reshape(D, 4, D).transpose(1, 0, 2)])
    down = np.concatenate([a["L3_ffn_w_down"], a["L3_ffn_ws_down"].reshape(4, D, D)])
    o["gu"] = np.stack([chunks(np.concatenate([gate[e], up[e]], 1))[:KC] for e in range(12)])
    o["down"] = np.stack([chunks(down[e])[:KC] for e in range(12)])
    return {k: np.ascontiguousarray(v) for k, v in o.items()}


STOP = 99


def kernel(**inputs):
    import concourse.bacc as bacc
    from concourse.bass_utils import run_bass_kernel_spmd as run

    nc = bacc.Bacc("TRN2", target_bir_lowering=False, num_devices=1)
    laid = lay_out({k: np.asarray(v) for k, v in inputs.items()})
    arrays = {f"in_{k}": v for k, v in laid.items()}
    aps = {k: nc.dram_tensor(f"in_{k}", v.shape, mybir.dt.from_np(v.dtype), kind="ExternalInput").ap()
           for k, v in laid.items()}
    out = nc.dram_tensor("out_0", (TOKENS, D), FP32, kind="ExternalOutput").ap()
    vit_tower(nc, aps, out, STOP)
    r = run(nc, [arrays], core_ids=[0])
    return r.results[0]["out_0"].reshape(IMAGES, SEQ, D)
```

```python
import concourse.bass as bass
from concourse import mybir
from concourse.alu_op_type import AluOpType as ALU
from contextlib import ExitStack
import numpy as np

FP32 = mybir.dt.float32
BF16 = mybir.dt.bfloat16
U32 = mybir.dt.uint32
ACT = mybir.ActivationFunctionType
AX = mybir.AxisListType

D = 192
SEQ = 16
IMAGES = 64
TOKENS = IMAGES * SEQ
P = 128
TILES = TOKENS // P
PAIRS = TILES // 2
H = 12
HD = D // H
WD = 64
KC = D // 2
KB = KC + 1
GROUP = 32
NG = P // GROUP
FF = 768
FC = FF // P
E = 8
LN_EPS = 1e-5
BANK = 512
MAGIC = 1.5 * 2.0 ** 23


class Steps:

    def __init__(self, eng, sem, per=0, index=None, before=0):
        self.eng, self.sem, self.per, self.index, self.n, self.before = eng, sem, per, index, 0, before

    def link(self, ins):
        self.n += 1
        ins.then_inc(self.sem, 1)
        self.eng.wait_ge(self.sem, (0 if self.index is None else self.index * self.per) + self.n + self.before)

    def end(self):
        assert self.index is None or self.n == self.per, (self.n, self.per)


def spread(ap, n):
    return ap.unsqueeze(ap.ndim).to_broadcast(list(ap.shape) + [n])


def spread_mid(ap, n):
    return ap.unsqueeze(1).to_broadcast([ap.shape[0], n, ap.shape[1]])


ROOT_BITS = float(0x5F3759DF)
ROOT_STEPS = 11


def rsqrt(dve, st, r, v, t):
    ri, vi = r.bitcast(mybir.dt.int32), v.bitcast(mybir.dt.int32)
    st.link(dve.tensor_scalar(ri, vi, 1, None, ALU.arith_shift_right))
    st.link(dve.tensor_scalar(ri, ri, -1.0, ROOT_BITS, ALU.mult, ALU.add))
    for _ in range(3):
        st.link(dve.tensor_tensor(t, r, r, ALU.mult))
        st.link(dve.scalar_tensor_tensor(t, t, -0.5, v, ALU.mult, ALU.mult))
        st.link(dve.scalar_tensor_tensor(r, t, 1.5, r, ALU.add, ALU.mult))


def at_least(eng, s, value):
    if not (isinstance(value, int) and value <= 0):
        eng.wait_ge(s, value)


def pipelined(eng, before, turn, after):
    before()
    turn(0, True, False)
    with eng.Fori(1, TILES - 1) as i:
        turn(i, False, False)
    turn(TILES - 1, False, True)
    after()


def reflect(dve, st, dst, vs, tvs, prod, w, j, first, nm):
    n, m = SEQ - j, SEQ - first
    if m == 0:
        return
    d = dst[:, j:SEQ, :, first:SEQ]
    t = prod[:, 0:n, :, 0:m]
    wm = w[:, :, 0:m]
    st.link(dve.tensor_tensor(t, d, spread(vs[:, j:SEQ, :, j], m), ALU.mult))
    st.link(dve.tensor_reduce(wm, t.rearrange("p n c d -> p c d n"), AX.X, ALU.add))
    st.link(dve.tensor_tensor(t, wm.unsqueeze(1).to_broadcast([P, n, nm, m]), spread(tvs[:, j:SEQ, :, j], m), ALU.mult))
    st.link(dve.tensor_tensor(d, d, t, ALU.subtract))


def vit_tower(nc, I, out, stop=99):
    ctx = ExitStack()
    with ctx:
        def sb(name, shape, dt=FP32):
            return ctx.enter_context(nc.sbuf_tensor(name, shape, dt))

        scratch = ExitStack()

        def local(name, shape, dt=FP32):
            return scratch.enter_context(nc.sbuf_tensor(name, shape, dt))

        of_phase = []

        def sem(name):
            of_phase.append(nc.alloc_semaphore(name))
            return of_phase[-1]

        def lasting(name):
            return ctx.enter_context(nc.semaphore(name))

        def end_phase():
            nc.clear_and_free_semaphores(list(of_phase))
            of_phase.clear()
            scratch.close()
            nc.all_engine_barrier()

        PS = ctx.enter_context(nc.psum_tensor("PS", [P, 8, BANK], FP32))
        X = sb("X", [P, TILES, D])
        XT = sb("XT", [KB, 2, TOKENS])
        ones = sb("ones", [1, P])
        big = sb("big", [P, FC, TOKENS])
        stats = sb("stats", [P, TILES, 6])
        mv = sb("mv", [P, TILES, 2])
        rstd = sb("rstd", [P, TILES])
        newton = sb("newton", [P, TILES])
        order = lasting("order")

        loaded = {}
        plan = []

        def keep(name):
            src = I[name]
            loaded[name] = (sb("w_" + name, src.shape, src.dtype), lasting("in_" + name))
            plan.append(name)
            return loaded[name][0]

        in_patches = lasting("in_patches")
        tok_w, pos, tok_b = keep("tok_w"), keep("pos"), keep("tok_b")
        ident = keep("ident")
        keys_causal, keys_block = keep("keys_causal"), keep("keys_block")
        rel, l0_qkv, l0_proj = keep("rel"), keep("l0_qkv"), keep("l0_proj")
        ff_w1, ff_b1, ff_w2, ff_b2 = keep("ff_w1"), keep("ff_b1"), keep("ff_w2"), keep("ff_b2")
        ff_s = keep("ff_s")
        l1_qkv, l1_proj = keep("l1_qkv"), keep("l1_proj")
        w_qkv, w_proj, w_projb = keep("w_qkv"), keep("w_proj"), keep("w_projb")
        w_gates, w_affine, iota10 = keep("w_gates"), keep("w_affine"), keep("iota10")
        l2_qkv, l2_proj, l2_scale = keep("l2_qkv"), keep("l2_proj"), keep("l2_scale")
        mix_a, mix_b, half01 = keep("mix_a"), keep("mix_b"), keep("half01")
        moe_g, moe_b2 = keep("moe_g"), keep("moe_b2")
        l3_qkv, l3_proj, l3_qw, block01 = keep("l3_qkv"), keep("l3_proj"), keep("l3_qw"), keep("block01")
        l3_gates = keep("l3_gates")

        def landed(eng, *names):
            for n in names:
                eng.wait_ge(loaded[n][1], 16)

        def own(eng, s, value):
            if isinstance(value, int):
                at_least(eng, s, value)
                return
            eng.wait_ge(s, value)
            eng.sem_inc(order, 1)

        emb_done, emb_added, xt_ones, pos_ready = sem("emb_done"), sem("emb_added"), sem("xt_ones"), sem("pos_ready")
        with nc.Block() as block:
            @block.sync
            def _(sp):
                for n in plan[:3]:
                    sp.dma_start(loaded[n][0][:], I[n]).then_inc(loaded[n][1], 16)
                sp.dma_start(big[:], I["patches"]).then_inc(in_patches, 16)
                for n in plan[3:]:
                    sp.dma_start(loaded[n][0][:], I[n]).then_inc(loaded[n][1], 16)

            @block.gpsimd
            def _(pool):
                pool.memset(XT[KC:KB, :, :], 1.0).then_inc(xt_ones, 1)
                pool.wait_ge(xt_ones, 1)
                pool.memset(ones[:], 1.0).then_inc(xt_ones, 1)
                pool.wait_ge(xt_ones, 2)

            @block.tensor
            def _(pe):
                landed(pe, "tok_w")
                pe.wait_ge(in_patches, 16)
                for t in range(TILES):
                    for c in range(FC):
                        last = pe.matmul(PS[:, t // 2, (t % 2) * D:(t % 2 + 1) * D], big[:, c, t * P:(t + 1) * P],
                                         tok_w[:, c, :], start=(c == 0), stop=(c == FC - 1))
                    last.then_inc(emb_done, 1)

            @block.vector
            def _(dve):
                landed(dve, "pos", "tok_b")
                dve.tensor_tensor(pos[:], pos[:], tok_b[:], ALU.add).then_inc(pos_ready, 1)
                dve.wait_ge(pos_ready, 1)
                for m in range(PAIRS):
                    dve.wait_ge(emb_done, 2 * m + 2)
                    dve.tensor_tensor(X[:, 2 * m:2 * m + 2, :], PS[:, m, 0:2 * D].rearrange("p (t d) -> p t d", t=2),
                                      spread_mid(pos[:], 2), ALU.add).then_inc(emb_added, 1)
                dve.wait_ge(emb_added, PAIRS)

        def norm_and_transpose(name, norm=True, transpose=True):
            dve_step = sem(name + "_dve")
            normed, turned, copied = sem(name + "_normed"), sem(name + "_turned"), sem(name + "_copied")
            with nc.Block() as block:
                @block.vector
                def _(dve):
                    if not norm:
                        return
                    steps = Steps(dve, dve_step)
                    for t in range(TILES):
                        dve.bn_stats(stats[:, t, :], X[:, t, :]).then_inc(dve_step, 1)
                    steps.n = TILES
                    dve.wait_ge(dve_step, TILES)
                    for t in range(TILES):
                        dve.bn_aggr(mv[:, t, :], stats[:, t, :]).then_inc(dve_step, 1)
                    steps.n = 2 * TILES
                    dve.wait_ge(dve_step, 2 * TILES)
                    steps.link(dve.tensor_scalar(mv[:, :, 1], mv[:, :, 1], LN_EPS, None, ALU.add))
                    rsqrt(dve, steps, rstd[:], mv[:, :, 1], newton[:])
                    for t in range(TILES):
                        dve.tensor_scalar(X[:, t, :], X[:, t, :], mv[:, t, 0:1], rstd[:, t:t + 1],
                                          ALU.subtract, ALU.mult).then_inc(normed, 1)
                    dve.wait_ge(normed, TILES)

                @block.scalar
                def _(act):
                    if transpose:
                        for m in range(PAIRS):
                            act.wait_ge(turned, m + 1)
                            act.activation(XT[0:KC, :, m * 2 * P:(m + 1) * 2 * P],
                                           PS[0:KC, m, :].rearrange("p (c n) -> p c n", c=2), ACT.Copy).then_inc(copied, 1)
                        act.wait_ge(copied, PAIRS)

                @block.tensor
                def _(pe):
                    if not transpose:
                        return
                    landed(pe, "ident")
                    for m in range(PAIRS):
                        if norm:
                            pe.wait_ge(normed, 2 * m + 2)
                        for t in range(2):
                            for c in range(2):
                                last = pe.transpose(PS[0:KC, m, c * 2 * P + t * P:c * 2 * P + (t + 1) * P],
                                                    X[:, 2 * m + t, c * KC:(c + 1) * KC], ident[:])
                        last.then_inc(turned, 1)

        end_phase()
        norm_and_transpose("tok", norm=False)
        end_phase()

        XTs = sb("XTs", [KB, 2, P])
        Xs = sb("Xs", [P, D])
        NB = 28
        QK = sb("QK", [P, NB, GROUP])
        QKT = sb("QKT", [P, NB, GROUP])
        CN, SQ = sb("CN", [P, 2 * H, HD]), sb("SQ", [P, 2 * H, HD])
        hm, hv, hr, ht = (sb(n, [P, 2 * H]) for n in ("hm", "hv", "hr", "ht"))
        V = sb("V", [P, D])
        S, PT = sb("S", [P, H, GROUP]), sb("PT", [P, H, GROUP])
        smax, rsum, rinv = sb("smax", [P, H]), sb("rsum", [P, H]), sb("rinv", [P, H])
        Y = sb("Y", [P, D])
        YT = sb("YT", [KB, 2, P])
        F = sb("F", [P, 2, GROUP])
        QF, QFT = sb("QF", [P, GROUP]), sb("QFT", [P, GROUP])
        qs = sb("qs", [P, 1])
        sp2, spr, spt = sb("sp2", [P, 1]), sb("spr", [P, 1]), sb("spt", [P, 1])
        SP, SPQ = sb("SP", [P, HD]), sb("SPQ", [P, HD])
        mixw = sb("mixw", [P, 2])

        identb = sb("identb", [P, P], BF16)
        mask_causal = sb("mask_causal", [P, H * GROUP], BF16)
        mask_block = sb("mask_block", [P, (H + 2) * GROUP], BF16)

        buf_zero = sem("buf_zero")
        with nc.Block() as block:
            @block.gpsimd
            def _(pool):
                pool.memset(QK[:], 0.0).then_inc(buf_zero, 1)
                pool.wait_ge(buf_zero, 1)
                pool.memset(YT[KC:KB, :, :], 1.0).then_inc(buf_zero, 1)
                pool.wait_ge(buf_zero, 2)
                pool.memset(mask_block[:], 0.0).then_inc(buf_zero, 1)
                pool.wait_ge(buf_zero, 3)
                landed(pool, "ident", "keys_causal", "keys_block")
                pool.tensor_copy(identb[:], ident[:]).then_inc(buf_zero, 1)
                pool.wait_ge(buf_zero, 4)
                for mask, keys in ((mask_causal, keys_causal), (mask_block, keys_block)):
                    pool.tensor_copy(mask[:, 0:H * GROUP].rearrange("p (h j) -> p h j", h=H),
                                     spread_mid(keys[:], H)).then_inc(buf_zero, 1)
                pool.wait_ge(buf_zero, 6)

        def attention(name, wqkv, wproj, w_names, mask, causal_rel=False, head_norm=False, quantum=False):
            s = {k: sem(f"{name}_{k}") for k in (
                "xts", "xs", "qkv", "vcopy", "qcopy", "cent", "sqd", "qkt", "score", "expin", "expd",
                "pt", "pv", "yn", "yt", "ytc", "proj", "added", "prep", "soft", "fsq", "fin", "fexp", "qft", "qv",
                "qw", "qadd", "left", "take")}
            nh = H + 2 if quantum else H
            nb = 2 * nh
            wa = 2 * D + (HD if quantum else 0)
            QKV, VB, SB, QVB, YB, TB, OB = range(7)
            nq = 0 if head_norm else (2 if quantum else 1)

            with nc.Block() as block:
                @block.gpsimd
                def _(pool):
                    def stage(i, wait=True):
                        if wait:
                            own(pool, s["qkv"], i)
                        pool.tensor_copy(XTs[:], XT[:, :, bass.ds(i * P, P)]).then_inc(s["xts"], 1)
                        if quantum:
                            own(pool, s["xts"], i + 1)
                            if wait:
                                own(pool, s["qv"], i)
                            pool.tensor_copy(Xs[:].unsqueeze(1), X[:, bass.ds(i, 1), :]).then_inc(s["xs"], 1)
                            own(pool, s["xs"], i + 1)

                    stage(0, False)
                    with pool.Fori(1, TILES) as i:
                        stage(i)

                @block.tensor
                def _(pe):
                    landed(pe, "ident", *w_names)

                    def project(i):
                        pe.wait_ge(s["xts"], i + 1)
                        own(pe, s["left"], i)
                        for c in range(2):
                            pe.matmul(PS[:, QKV, 0:wa], XTs[:, c, :], wqkv[:, c, 0:wa], start=(c == 0), stop=(c == 1))
                        own(pe, s["vcopy"], i)
                        for c in range(2):
                            last = pe.matmul(PS[:, VB, 0:D], XTs[:, c, :], wqkv[:, c, wa:wa + D], start=(c == 0), stop=(c == 1))
                        last.then_inc(s["qkv"], 1)

                    def turn_output(i):
                        own(pe, s["yn"], i + 1)
                        for c in range(2):
                            last = pe.transpose(PS[0:KC, TB, c * P:(c + 1) * P], Y[:, c * KC:(c + 1) * KC], ident[:])
                        last.then_inc(s["yt"], 1)

                    def project_output(i):
                        own(pe, s["ytc"], i + 1)
                        own(pe, s["added"], i)
                        for c in range(2):
                            last = pe.matmul(PS[:, OB, 0:D], YT[:, c, :], wproj[:, c, :], start=(c == 0), stop=(c == 1))
                        last.then_inc(s["proj"], 1)

                    def turn(i, first, last_turn):
                        own(pe, s["qkt"], i + 1)
                        own(pe, s["expin"], i)
                        pe.matmul(PS[:, SB, 0:nh * GROUP], identb[:], mask[:, 0:nh * GROUP], start=True, stop=False,
                                  skip_group_check=True)
                        for h in range(nh):
                            for g in range(NG):
                                r = slice(g * GROUP, g * GROUP + HD)
                                last = pe.matmul(PS[g * GROUP:(g + 1) * GROUP, SB, h * GROUP:(h + 1) * GROUP],
                                                 QKT[r, h, :], QKT[r, nh + h, :], start=False, stop=True,
                                                 skip_group_check=True)
                        last.then_inc(s["score"], 1)
                        if not first:
                            turn_output(i - 1)
                        if not last_turn:
                            project(i + 1)
                        if not first:
                            project_output(i - 1)
                        own(pe, s["pt"], i + 1)
                        own(pe, s["vcopy"], i + 1)
                        for h in range(H):
                            for g in range(NG):
                                r = slice(g * GROUP, (g + 1) * GROUP)
                                last = pe.matmul(PS[r, YB, h * HD:(h + 1) * HD], PT[r, h, :], V[r, h * HD:(h + 1) * HD],
                                                 start=True, stop=True, skip_group_check=True)
                        last.then_inc(s["pv"], 1)
                        if quantum:
                            own(pe, s["qft"], i + 1)
                            own(pe, s["xs"], i + 1)
                            own(pe, s["qadd"], i)
                            for g in range(NG):
                                r = slice(g * GROUP, (g + 1) * GROUP)
                                last = pe.matmul(PS[r, QVB, 0:D], QFT[r, :], Xs[r, :], start=True, stop=True,
                                                 skip_group_check=True)
                            last.then_inc(s["qv"], 1)

                    def after():
                        turn_output(TILES - 1)
                        project_output(TILES - 1)

                    pipelined(pe, lambda: project(0), turn, after)

                @block.scalar
                def _(act):
                    if quantum:
                        landed(act, "l3_qw")
                        act.activation(mixw[:, 0:1], l3_qw[:], ACT.Exp, scale=-1.0).then_inc(s["qw"], 1)

                    def heads_out(i):
                        act.wait_ge(s["qkv"], i + 1)
                        if head_norm:
                            act.wait_ge(s["cent"], i + 1)
                            act.activation(SQ[:], CN[:], ACT.Square).then_inc(s["sqd"], 1)
                            return
                        at_least(act, s["qkt"], i)
                        if not quantum:
                            n = H if causal_rel else 2 * H
                            act.activation(QK[:, 0:n, 0:HD], PS[:, QKV, 0:n * HD].rearrange(
                                "p (h d) -> p h d", d=HD), ACT.Copy).then_inc(s["qcopy"], 1)
                            return
                        for j in range(2):
                            act.activation(QK[:, j * nh:j * nh + H, 0:HD],
                                           PS[:, QKV, j * D:(j + 1) * D].rearrange("p (h d) -> p h d", d=HD),
                                           ACT.Copy).then_inc(s["qcopy"], 1)

                    def values_out(i):
                        at_least(act, s["qkv"], i + 1)
                        at_least(act, s["pv"], i)
                        act.activation(V[:], PS[:, VB, 0:D], ACT.Copy).then_inc(s["vcopy"], 1)

                    def output_out(i):
                        act.wait_ge(s["yt"], i + 1)
                        at_least(act, s["proj"], i)
                        act.activation(YT[0:KC, :, :], PS[0:KC, TB, 0:2 * P].rearrange("p (c n) -> p c n", c=2),
                                       ACT.Copy).then_inc(s["ytc"], 1)

                    def turn(i, first, last_turn):
                        if quantum:
                            act.wait_ge(s["score"], i + 1)
                            act.activation(F[:], PS[:, SB, H * GROUP:nh * GROUP].rearrange(
                                "p (h j) -> p h j", j=GROUP), ACT.Square).then_inc(s["fsq"], 1)
                            act.wait_ge(s["fin"], i + 1)
                            act.activation(QF[:], QF[:], ACT.Exp).then_inc(s["fexp"], 1)
                        act.wait_ge(s["expin"], i + 1)
                        act.activation(S[:], S[:], ACT.Exp, scale=HD ** -0.5).then_inc(s["expd"], 1)
                        if not first:
                            output_out(i - 1)
                        if not last_turn:
                            heads_out(i + 1)
                            values_out(i + 1)

                    def before():
                        heads_out(0)
                        values_out(0)

                    pipelined(act, before, turn, lambda: output_out(TILES - 1))

                @block.vector
                def _(dve):
                    pre = Steps(dve, s["soft"])
                    if causal_rel:
                        landed(dve, "rel")
                    if quantum:
                        landed(dve, "block01")
                        dve.wait_ge(s["qw"], 1)
                        pre.link(dve.tensor_scalar(mixw[:, 1:2], mixw[:, 0:1], 1.0, None, ALU.add))
                        pre.link(dve.reciprocal(mixw[:, 0:1], mixw[:, 1:2]))
                        pre.link(dve.tensor_scalar(mixw[:, 1:2], mixw[:, 0:1], -1.0, 1.0, ALU.mult, ALU.add))

                    def take(i):
                        st = Steps(dve, s["take"], 1 if causal_rel else 2 if head_norm else 0, i)
                        dve.wait_ge(s["qkv"], i + 1)
                        if nq:
                            dve.wait_ge(s["qcopy"], i * nq + nq)
                        if causal_rel:
                            st.link(dve.tensor_tensor(QK[:, H:2 * H, 0:HD],
                                                      PS[:, QKV, D:2 * D].rearrange("p (h d) -> p h d", d=HD),
                                                      spread_mid(rel[:], H), ALU.add))
                            dve.sem_inc(s["left"], 1)
                        if head_norm:
                            qk = PS[:, QKV, 0:2 * D].rearrange("p (h d) -> p h d", d=HD)
                            st.link(dve.tensor_reduce(hm[:], qk, AX.X, ALU.add))
                            st.link(dve.tensor_scalar(hm[:], hm[:], 1.0 / HD, None, ALU.mult))
                            dve.tensor_tensor(CN[:], qk, spread(hm[:], HD), ALU.subtract).then_inc(s["cent"], 1)
                            dve.wait_ge(s["cent"], i + 1)
                            dve.sem_inc(s["left"], 1)
                        if quantum:
                            dve.tensor_copy(SP[:], PS[:, QKV, 2 * D:2 * D + HD]).then_inc(s["left"], 1)
                            dve.wait_ge(s["left"], i + 1)
                        st.end()

                    def prepare(i):
                        st = Steps(dve, s["prep"], 2 + ROOT_STEPS + 1 if head_norm else
                                   3 + ROOT_STEPS + 3 + 5 if quantum else 0, i)
                        if head_norm:
                            dve.wait_ge(s["sqd"], i + 1)
                            st.link(dve.tensor_reduce(hv[:], SQ[:], AX.X, ALU.add))
                            st.link(dve.tensor_scalar(hv[:], hv[:], 1.0 / HD, LN_EPS, ALU.mult, ALU.add))
                            rsqrt(dve, st, hr[:], hv[:], ht[:])
                            st.link(dve.tensor_tensor(QK[:, 0:2 * H, 0:HD], CN[:], spread(hr[:], HD), ALU.mult))
                        if quantum:
                            st.link(dve.tensor_tensor(SPQ[:], SP[:], SP[:], ALU.mult))
                            st.link(dve.tensor_reduce(sp2[:], SPQ[:], AX.X, ALU.add))
                            st.link(dve.tensor_scalar(sp2[:], sp2[:], 2.0 ** -64, None, ALU.max))
                            rsqrt(dve, st, spr[:], sp2[:], spt[:])
                            st.link(dve.tensor_tensor(spt[:], spr[:], sp2[:], ALU.mult))
                            st.link(dve.tensor_scalar(spt[:], spt[:], 1e-8, None, ALU.add))
                            st.link(dve.reciprocal(spr[:], spt[:]))
                            half = HD // 2
                            st.link(dve.tensor_scalar(SP[:], SP[:], spr[:], None, ALU.mult))
                            st.link(dve.tensor_copy(QK[:, H:H + 2, 0:HD], spread_mid(SP[:], 2)))
                            st.link(dve.tensor_copy(QK[:, nh + H, 0:HD], SP[:]))
                            st.link(dve.tensor_copy(QK[:, nh + H + 1, 0:half], SP[:, half:HD]))
                            st.link(dve.tensor_scalar(QK[:, nh + H + 1, half:HD], SP[:, 0:half], -1.0, None, ALU.mult))
                        st.end()
                        at_least(dve, s["score"], i)
                        dve.transpose(QKT[:, 0:nb, :], QK[:, 0:nb, :]).then_inc(s["qkt"], 1)

                    def add_output(i):
                        dve.wait_ge(s["proj"], i + 1)
                        xi, o = X[:, bass.ds(i, 1), :], PS[:, OB:OB + 1, 0:D]
                        if quantum:
                            dve.scalar_tensor_tensor(xi, o, mixw[:, 1:2], xi, ALU.mult, ALU.add).then_inc(s["added"], 1)
                        else:
                            dve.tensor_tensor(xi, o, xi, ALU.add).then_inc(s["added"], 1)

                    def turn(i, first, last_turn):
                        st = Steps(dve, s["soft"], 7 if quantum else 3, i, before=3 if quantum else 0)
                        sc_ps = PS[:, SB, 0:H * GROUP].rearrange("p (h j) -> p h j", j=GROUP)
                        dve.wait_ge(s["score"], i + 1)
                        if quantum:
                            dve.wait_ge(s["fsq"], i + 1)
                            dve.tensor_tensor(QF[:], F[:, 0, :], F[:, 1, :], ALU.add).then_inc(s["fin"], 1)
                        st.link(dve.tensor_reduce(smax[:], sc_ps, AX.X, ALU.max))
                        at_least(dve, s["pt"], i)
                        dve.tensor_tensor(S[:], sc_ps, spread(smax[:], GROUP), ALU.subtract).then_inc(s["expin"], 1)
                        if quantum:
                            dve.wait_ge(s["fexp"], i + 1)
                            st.link(dve.tensor_tensor(QF[:], QF[:], block01[:], ALU.mult))
                            dve.transpose(QFT[:], QF[:]).then_inc(s["qft"], 1)
                            st.link(dve.tensor_reduce(qs[:], QF[:], AX.X, ALU.add))
                            st.link(dve.reciprocal(qs[:], qs[:]))
                            st.link(dve.tensor_tensor(qs[:], qs[:], mixw[:, 0:1], ALU.mult))
                        dve.wait_ge(s["expd"], i + 1)
                        dve.transpose(PT[:], S[:]).then_inc(s["pt"], 1)
                        st.link(dve.tensor_reduce(rsum[:], S[:], AX.X, ALU.add))
                        st.link(dve.reciprocal(rinv[:], rsum[:]))
                        st.end()
                        if not last_turn:
                            take(i + 1)
                            prepare(i + 1)
                        if not first:
                            add_output(i - 1)
                        dve.wait_ge(s["pv"], i + 1)
                        at_least(dve, s["yt"], i)
                        dve.tensor_tensor(Y[:].rearrange("p (h d) -> p h d", d=HD),
                                          PS[:, YB, 0:D].rearrange("p (h d) -> p h d", d=HD),
                                          spread(rinv[:], HD), ALU.mult).then_inc(s["yn"], 1)
                        if quantum:
                            dve.wait_ge(s["qv"], i + 1)
                            xi = X[:, bass.ds(i, 1), :]
                            dve.scalar_tensor_tensor(xi, PS[:, QVB:QVB + 1, 0:D], qs[:], xi, ALU.mult, ALU.add).then_inc(s["qadd"], 1)
                            dve.wait_ge(s["qadd"], i + 1)

                    def after():
                        add_output(TILES - 1)
                        dve.wait_ge(s["added"], TILES)

                    def before():
                        take(0)
                        prepare(0)

                    pipelined(dve, before, turn, after)

        def wide_attention():
            WB = 2 * H * 2
            CW = local("CW", [P, 2 * H, WD])
            SW = local("SW", [P, 2 * H * WD])
            QKW = local("QKW", [P, WB, GROUP])
            KW = local("KW", [P, WB, GROUP])
            VW = local("VW", [P, H * WD])
            YW = local("YW", [P, H * WD])
            YTW = local("YTW", [P, 6, P])
            wr, wv, wt, wm, wi = (local(n, [P, 2 * H]) for n in ("wr", "wv", "wt", "wm", "wi"))
            k = {n: sem("wide_" + n) for n in ("xts", "qk", "v", "vcopy", "cent", "sq", "turned", "affine", "score",
                                               "expin", "expd", "pt", "pv", "yn", "yt", "ytc", "proj", "added",
                                               "prep", "soft", "take")}
            HB = H * WD // 2

            with nc.Block() as block:
                @block.gpsimd
                def _(pool):
                    pool.tensor_copy(XTs[:], XT[:, :, 0:P]).then_inc(k["xts"], 1)
                    with pool.Fori(1, TILES) as i:
                        own(pool, k["v"], i)
                        pool.tensor_copy(XTs[:], XT[:, :, bass.ds(i * P, P)]).then_inc(k["xts"], 1)

                @block.tensor
                def _(pe):
                    landed(pe, "w_qkv", "w_proj", "w_projb")

                    def project(i):
                        pe.wait_ge(k["xts"], i + 1)
                        own(pe, k["cent"], i)
                        for b in range(4):
                            for c in range(2):
                                last = pe.matmul(PS[:, b, 0:HB], XTs[:, c, :], w_qkv[:, c, b * HB:(b + 1) * HB],
                                                 start=(c == 0), stop=(c == 1))
                        last.then_inc(k["qk"], 1)

                    def project_values(i):
                        own(pe, k["expin"], i)
                        own(pe, k["added"], i - 1)
                        for b in range(2):
                            for c in range(2):
                                last = pe.matmul(PS[:, 6 + b, 0:HB], XTs[:, c, :], w_qkv[:, c, (4 + b) * HB:(5 + b) * HB],
                                                 start=(c == 0), stop=(c == 1))
                        last.then_inc(k["v"], 1)

                    def turn_output(i):
                        own(pe, k["yn"], i + 1)
                        for j in range(6):
                            last = pe.transpose(PS[:, 4 + j // 3, (j % 3) * P:(j % 3 + 1) * P], YW[:, j * P:(j + 1) * P], ident[:])
                        last.then_inc(k["yt"], 1)

                    def project_output(i):
                        own(pe, k["ytc"], i + 1)
                        own(pe, k["vcopy"], i + 1)
                        for j in range(6):
                            pe.matmul(PS[:, 7, 0:D], YTW[:, j, :], w_proj[:, j, :], start=(j == 0), stop=False)
                        pe.matmul(PS[:, 7, 0:D], ones[:], w_projb[:], start=False, stop=True).then_inc(k["proj"], 1)

                    def turn(i, first, last_turn):
                        if not last_turn:
                            project(i + 1)
                        own(pe, k["affine"], i * 4 + 4)
                        own(pe, k["vcopy"], i + 1)
                        pe.matmul(PS[:, 6, 0:H * GROUP], identb[:], mask_block[:, 0:H * GROUP], start=True, stop=False,
                                  skip_group_check=True)
                        for h in range(H):
                            for g in range(NG):
                                r = slice(g * GROUP, (g + 1) * GROUP)
                                for d in range(2):
                                    last = pe.matmul(PS[r, 6, h * GROUP:(h + 1) * GROUP], KW[r, 2 * h + d, :],
                                                     KW[r, 2 * H + 2 * h + d, :], start=False, stop=True,
                                                     skip_group_check=True)
                        last.then_inc(k["score"], 1)
                        if not first:
                            turn_output(i - 1)
                            project_output(i - 1)
                        own(pe, k["pt"], i + 1)
                        for h in range(H):
                            for g in range(NG):
                                r = slice(g * GROUP, (g + 1) * GROUP)
                                last = pe.matmul(PS[r, 4 + h // 6, (h % 6) * WD:(h % 6 + 1) * WD], PT[r, h, :],
                                                 VW[r, h * WD:(h + 1) * WD], start=True, stop=True, skip_group_check=True)
                        last.then_inc(k["pv"], 1)
                        if not last_turn:
                            project_values(i + 1)

                    def before():
                        project(0)
                        project_values(0)

                    def after():
                        turn_output(TILES - 1)
                        project_output(TILES - 1)

                    pipelined(pe, before, turn, after)

                @block.scalar
                def _(act):
                    landed(act, "w_affine")

                    def square(i):
                        act.wait_ge(k["cent"], i + 1)
                        act.activation(SW[:], CW[:].rearrange("p h d -> p (h d)"), ACT.Square).then_inc(k["sq"], 1)

                    def affine(i):
                        at_least(act, k["score"], i)
                        act.wait_ge(k["turned"], i + 1)
                        for j in range(2):
                            for d in range(2):
                                v = KW[:].rearrange("p (j h d) n -> p j h d n", j=2, d=2)[:, j, :, d, :]
                                act.activation(v, v, ACT.Identity, scale=w_affine[:, 4 * j + d:4 * j + d + 1],
                                               bias=w_affine[:, 4 * j + 2 + d:4 * j + 3 + d]).then_inc(k["affine"], 1)

                    def values_out(i):
                        act.wait_ge(k["v"], i + 1)
                        at_least(act, k["pv"], i)
                        act.activation(VW[:].rearrange("p (b n) -> p b n", b=2), PS[:, 6:8, 0:HB], ACT.Copy).then_inc(k["vcopy"], 1)

                    def output_out(i):
                        act.wait_ge(k["yt"], i + 1)
                        at_least(act, k["proj"], i)
                        act.activation(YTW[:].rearrange("p (b j) n -> p b (j n)", b=2), PS[:, 4:6, 0:3 * P],
                                       ACT.Copy).then_inc(k["ytc"], 1)

                    def turn(i, first, last_turn):
                        if not last_turn:
                            square(i + 1)
                        act.wait_ge(k["expin"], i + 1)
                        act.activation(S[:], S[:], ACT.Exp, scale=WD ** -0.5).then_inc(k["expd"], 1)
                        if not first:
                            output_out(i - 1)
                        if not last_turn:
                            affine(i + 1)
                            values_out(i + 1)

                    def before():
                        square(0)
                        affine(0)
                        values_out(0)

                    pipelined(act, before, turn, lambda: output_out(TILES - 1))

                @block.vector
                def _(dve):
                    def take(i):
                        st = Steps(dve, k["take"], 2, i)
                        dve.wait_ge(k["qk"], i + 1)
                        qk = PS[:, 0:4, 0:HB].rearrange("p b (h d) -> p b h d", d=WD)
                        cw = CW[:].rearrange("p (b h) d -> p b h d", b=4)
                        mean = wm[:].rearrange("p (b h) -> p b h", b=4)
                        st.link(dve.tensor_reduce(mean, qk, AX.X, ALU.add))
                        st.link(dve.tensor_scalar(wm[:], wm[:], 1.0 / WD, None, ALU.mult))
                        dve.tensor_tensor(cw, qk, spread(mean, WD), ALU.subtract).then_inc(k["cent"], 1)
                        st.end()

                    def prepare(i):
                        st = Steps(dve, k["prep"], 3 + ROOT_STEPS, i)
                        dve.wait_ge(k["sq"], i + 1)
                        st.link(dve.tensor_reduce(wv[:], SW[:].rearrange("p (h d) -> p h d", d=WD), AX.X, ALU.add))
                        st.link(dve.tensor_scalar(wv[:], wv[:], 1.0 / WD, LN_EPS, ALU.mult, ALU.add))
                        rsqrt(dve, st, wr[:], wv[:], wt[:])
                        st.link(dve.tensor_tensor(QKW[:].rearrange("p (h d) n -> p h (d n)", d=2), CW[:], spread(wr[:], WD), ALU.mult))
                        at_least(dve, k["score"], i)
                        dve.transpose(KW[:], QKW[:]).then_inc(k["turned"], 1)
                        st.end()

                    def add_output(i):
                        dve.wait_ge(k["proj"], i + 1)
                        xi = X[:, bass.ds(i, 1), :]
                        dve.tensor_tensor(xi, PS[:, 7:8, 0:D], xi, ALU.add).then_inc(k["added"], 1)

                    def turn(i, first, last_turn):
                        if not last_turn:
                            take(i + 1)
                        st = Steps(dve, k["soft"], 4, i)
                        dve.wait_ge(k["score"], i + 1)
                        sc_ps = PS[:, 6, 0:H * GROUP].rearrange("p (h j) -> p h j", j=GROUP)
                        st.link(dve.tensor_reduce(smax[:], sc_ps, AX.X, ALU.max))
                        at_least(dve, k["pt"], i)
                        dve.tensor_tensor(S[:], sc_ps, spread(smax[:], GROUP), ALU.subtract).then_inc(k["expin"], 1)
                        dve.wait_ge(k["expd"], i + 1)
                        dve.transpose(PT[:], S[:]).then_inc(k["pt"], 1)
                        st.link(dve.tensor_reduce(rsum[:], S[:], AX.X, ALU.add))
                        st.link(dve.reciprocal(rinv[:], rsum[:]))
                        st.link(dve.tensor_tensor(wi[:, 0:H].unsqueeze(1), rinv[:].unsqueeze(1), G[:, bass.ds(i, 1), :], ALU.mult))
                        st.end()
                        if not last_turn:
                            prepare(i + 1)
                        if not first:
                            add_output(i - 1)
                        dve.wait_ge(k["pv"], i + 1)
                        at_least(dve, k["yt"], i)
                        dve.tensor_tensor(YW[:].rearrange("p (b h d) -> p b h d", b=2, d=WD),
                                          PS[:, 4:6, 0:HB].rearrange("p b (h d) -> p b h d", d=WD),
                                          spread(wi[:, 0:H].rearrange("p (b h) -> p b h", b=2), WD), ALU.mult).then_inc(k["yn"], 1)

                    def after():
                        add_output(TILES - 1)
                        dve.wait_ge(k["added"], TILES)

                    def before():
                        take(0)
                        prepare(0)

                    pipelined(dve, before, turn, after)

        def grassmann_attention():
            k = {n: sem("gr_" + n) for n in ("qk", "qkc", "v", "vc", "to", "back", "a", "q", "qo", "qb", "dve", "mixsum",
                                             "xts", "pad", "qkt", "score", "sq", "dc", "dt", "dtc", "mixed", "expin",
                                             "expd", "pt", "pv", "yn", "yt", "ytc", "proj", "added", "dve2", "sc2", "prep", "ss", "root")}
            there = nc.dram_tensor("heads_there", (TOKENS, 2 * D), FP32).ap()
            back = nc.dram_tensor("heads_back", (TOKENS, 2 * D), FP32).ap()
            NM = 2 * (H // 2)
            M = SEQ
            VA = local("VA", [P, TILES, D])
            QT_ = big[:].rearrange("p a b -> p (a b)")
            tok = QT_[:, 0:TILES * 2 * D].rearrange("p (t n) -> p t n", t=TILES)
            A = QT_[:, 3072:6144].rearrange("p (n c d) -> p n c d", n=M, c=NM)
            Q = local("QM", [P, M, NM, M])
            T = QT_[:, 0:3072].rearrange("p (n c d) -> p n c d", n=M, c=NM)
            col = local("qr_col", [P, M, NM])
            w = local("qr_w", [P, NM, M])
            tail, nrm, v0, tau, tmp = (local("qr_" + n, [P, NM]) for n in ("tail", "nrm", "v0", "tau", "tmp"))
            TV = local("qr_tv", [P, M, NM, M])

            def half_rows(ap, half, which):
                o = which * D + half * KC
                return ap.rearrange("(b n) c -> b n c", n=SEQ)[:, :, o:o + KC]

            with nc.Block() as block:
                @block.tensor
                def _(pe):
                    landed(pe, "l2_qkv")
                    for t in range(TILES):
                        for c in range(2):
                            last = pe.matmul(PS[:, t, 0:2 * D], XT[:, c, t * P:(t + 1) * P], l2_qkv[:, c, 0:2 * D],
                                             start=(c == 0), stop=(c == 1))
                        last.then_inc(k["qk"], 1)
                    for t in range(TILES):
                        pe.wait_ge(k["qkc"], t + 1)
                        for c in range(2):
                            last = pe.matmul(PS[:, t, 0:D], XT[:, c, t * P:(t + 1) * P], l2_qkv[:, c, 2 * D:],
                                             start=(c == 0), stop=(c == 1))
                        last.then_inc(k["v"], 1)

                @block.scalar
                def _(act):
                    for t in range(TILES):
                        act.wait_ge(k["qk"], t + 1)
                        act.activation(tok[:, t, :], PS[:, t, 0:2 * D], ACT.Copy).then_inc(k["qkc"], 1)
                    for t in range(TILES):
                        act.wait_ge(k["v"], t + 1)
                        act.activation(VA[:, t, :], PS[:, t, 0:D], ACT.Copy).then_inc(k["vc"], 1)
                    act.wait_ge(k["vc"], TILES)
                    for j in range(M - 1):
                        act.wait_ge(k["ss"], j + 1)
                        act.activation(tmp[:], nrm[:], ACT.Sqrt).then_inc(k["root"], 1)

                @block.gpsimd
                def _(pool):
                    landed(pool, "mix_a", "mix_b", "half01", "l2_scale")
                    pool.tensor_tensor(mix_a[:], mix_a[:], mix_b[:], ALU.add).then_inc(k["mixsum"], 1)
                    pool.wait_ge(k["mixsum"], 1)
                    pool.tensor_tensor(l2_scale[:, 1:3], half01[:], l2_scale[:, 0:1].to_broadcast([P, 2]), ALU.mult).then_inc(k["mixsum"], 1)
                    pool.wait_ge(k["mixsum"], 2)

                @block.sync
                def _(sp):
                    sp.wait_ge(k["qkc"], TILES)
                    sp.dma_start(there.rearrange("(t p) c -> p t c", p=P), tok).then_inc(k["to"], 16)
                    sp.wait_ge(k["to"], 16)
                    for half in range(2):
                        for which in range(2):
                            sp.dma_start(A[half * 64:(half + 1) * 64, :, which * 6:(which + 1) * 6, :].rearrange("b n c d -> b n (c d)"),
                                         half_rows(there, half, which)).then_inc(k["a"], 16)
                    sp.wait_ge(k["q"], 1)
                    for half in range(2):
                        for which in range(2):
                            sp.dma_start(half_rows(back, half, which),
                                         Q[half * 64:(half + 1) * 64, :, which * 6:(which + 1) * 6, :].rearrange(
                                             "b n c d -> b n (c d)")).then_inc(k["qo"], 16)
                    sp.wait_ge(k["qo"], 64)
                    sp.dma_start(tok, back.rearrange("(t p) c -> p t c", p=P)).then_inc(k["qb"], 16)
                    sp.wait_ge(k["qb"], 16)

                @block.vector
                def _(dve):
                    st = Steps(dve, k["dve"])
                    st.link(dve.memset(Q[:], 0.0))
                    for n in range(M):
                        dve.memset(Q[:, n, :, n], 1.0).then_inc(k["dve"], 1)
                    st.n += M
                    dve.wait_ge(k["dve"], st.n)
                    dve.wait_ge(k["a"], 64)
                    for j in range(M - 1):
                        m = M - j
                        x = A[:, j:M, :, j]
                        cj = col[:, 0:m, :]
                        st.link(dve.tensor_tensor(cj, x, x, ALU.mult))
                        st.link(dve.tensor_reduce(tail[:], cj[:, 1:m, :].rearrange("p n c -> p c n"), AX.X, ALU.add))
                        st.link(dve.tensor_tensor(nrm[:], tail[:], cj[:, 0, :], ALU.add))
                        dve.tensor_scalar(nrm[:], nrm[:], 1e-37, None, ALU.max).then_inc(k["ss"], 1)
                        st.link(dve.tensor_scalar(v0[:], A[:, j, :, j], 0.0, 2.0, ALU.is_ge, ALU.mult))
                        st.link(dve.tensor_scalar(tail[:], tail[:], 0.0, None, ALU.is_gt))
                        dve.wait_ge(k["root"], j + 1)
                        st.link(dve.reciprocal(tau[:], tmp[:]))
                        st.link(dve.tensor_tensor(tau[:], tau[:], nrm[:], ALU.mult))
                        st.link(dve.tensor_tensor(tau[:], tau[:], tmp[:], ALU.add))
                        st.link(dve.tensor_scalar(nrm[:], tau[:], 0.5, None, ALU.mult))
                        st.link(dve.scalar_tensor_tensor(v0[:], v0[:], 1.0, nrm[:], ALU.subtract, ALU.mult))
                        st.link(dve.tensor_tensor(A[:, j, :, j], A[:, j, :, j], v0[:], ALU.add))
                        st.link(dve.tensor_tensor(v0[:], v0[:], A[:, j, :, j], ALU.mult))
                        st.link(dve.reciprocal(tau[:], v0[:]))
                        st.link(dve.tensor_tensor(tau[:], tau[:], tail[:], ALU.mult))
                        st.link(dve.tensor_tensor(TV[:, j:M, :, j], A[:, j:M, :, j], tau[:].unsqueeze(1).to_broadcast([P, m, NM]), ALU.mult))
                        reflect(dve, st, A, A, TV, T, w, j, j + 1, NM)
                    for j in reversed(range(M - 1)):
                        reflect(dve, st, Q, A, TV, T, w, j, j, NM)
                    dve.sem_inc(k["q"], 1)

            SB, DB, MB, YB, TB, OB = range(6)
            DC = local("DC", [P, D])
            DT = local("DT", [KB, 2, P])
            MX = local("MX", [P, H, SEQ])
            with nc.Block() as block:
                @block.gpsimd
                def _(pool):
                    def stage(i):
                        own(pool, k["qkt"], i)
                        pool.tensor_copy(QK[:, 0:2 * H, 0:HD].unsqueeze(1), tok[:, bass.ds(i, 1), :].rearrange(
                            "p t (h d) -> p t h d", d=HD)).then_inc(k["pad"], 1)
                        own(pool, k["pad"], i + 1)
                        own(pool, k["pv"], i)
                        pool.tensor_copy(V[:].unsqueeze(1), VA[:, bass.ds(i, 1), :]).then_inc(k["xts"], 1)
                        own(pool, k["xts"], i + 1)

                    pool.memset(DT[KC:KB, :, :], 1.0).then_inc(k["prep"], 1)
                    pool.wait_ge(k["prep"], 1)
                    stage(0)
                    with pool.Fori(1, TILES) as i:
                        stage(i)

                @block.tensor
                def _(pe):
                    landed(pe, "l2_proj", "ident", "mix_a")

                    def score(i):
                        own(pe, k["qkt"], i + 1)
                        own(pe, k["sq"], i)
                        for h in range(H):
                            for g in range(NG):
                                r = slice(g * GROUP, g * GROUP + HD)
                                last = pe.matmul(PS[g * GROUP:(g + 1) * GROUP, SB, h * GROUP:(h + 1) * GROUP],
                                                 QKT[r, h, :], QKT[r, H + h, :], start=True, stop=True,
                                                 skip_group_check=True)
                        last.then_inc(k["score"], 1)

                    def turn_scores(i):
                        own(pe, k["dc"], i + 1)
                        for c in range(2):
                            last = pe.transpose(PS[0:KC, DB, c * P:(c + 1) * P], DC[:, c * KC:(c + 1) * KC], ident[:])
                        last.then_inc(k["dt"], 1)

                    def mix(i):
                        own(pe, k["dtc"], i + 1)
                        own(pe, k["expin"], i)
                        for c in range(2):
                            last = pe.matmul(PS[:, MB, 0:D], DT[:, c, :], mix_a[:, c, :], start=(c == 0), stop=(c == 1))
                        last.then_inc(k["mixed"], 1)

                    def turn_output(i):
                        own(pe, k["yn"], i + 1)
                        for c in range(2):
                            last = pe.transpose(PS[0:KC, TB, c * P:(c + 1) * P], Y[:, c * KC:(c + 1) * KC], ident[:])
                        last.then_inc(k["yt"], 1)

                    def project_output(i):
                        own(pe, k["ytc"], i + 1)
                        own(pe, k["added"], i)
                        for c in range(2):
                            last = pe.matmul(PS[:, OB, 0:D], YT[:, c, :], l2_proj[:, c, :], start=(c == 0), stop=(c == 1))
                        last.then_inc(k["proj"], 1)

                    def turn(i, first, last_turn):
                        if not first:
                            turn_output(i - 1)
                        if not last_turn:
                            score(i + 1)
                        if not first:
                            project_output(i - 1)
                        if not last_turn:
                            turn_scores(i + 1)
                            mix(i + 1)
                        own(pe, k["pt"], i + 1)
                        own(pe, k["xts"], i + 1)
                        for h in range(H):
                            for g in range(NG):
                                r = slice(g * GROUP, (g + 1) * GROUP)
                                last = pe.matmul(PS[r, YB, h * HD:(h + 1) * HD], PT[r, h, :], V[r, h * HD:(h + 1) * HD],
                                                 start=True, stop=True, skip_group_check=True)
                        last.then_inc(k["pv"], 1)

                    def before():
                        score(0)
                        turn_scores(0)
                        mix(0)

                    def after():
                        turn_output(TILES - 1)
                        project_output(TILES - 1)

                    pipelined(pe, before, turn, after)

                @block.scalar
                def _(act):
                    def square(i):
                        act.wait_ge(k["score"], i + 1)
                        at_least(act, k["dc"], i)
                        act.activation(SQ[:].rearrange("p (h a) j -> p h (a j)", a=2), PS[:, SB, 0:H * GROUP].rearrange(
                            "p (h j) -> p h j", j=GROUP), ACT.Square).then_inc(k["sq"], 1)

                    def scores_out(i):
                        act.wait_ge(k["dt"], i + 1)
                        act.activation(DT[0:KC, :, :], PS[0:KC, DB, 0:2 * P].rearrange("p (c n) -> p c n", c=2),
                                       ACT.Copy).then_inc(k["dtc"], 1)

                    def output_out(i):
                        act.wait_ge(k["yt"], i + 1)
                        act.activation(YT[0:KC, :, :], PS[0:KC, TB, 0:2 * P].rearrange("p (c n) -> p c n", c=2),
                                       ACT.Copy).then_inc(k["ytc"], 1)

                    def turn(i, first, last_turn):
                        act.wait_ge(k["expin"], i + 1)
                        act.activation(MX[:], MX[:], ACT.Exp).then_inc(k["expd"], 1)
                        if not first:
                            output_out(i - 1)
                        if not last_turn:
                            square(i + 1)
                            scores_out(i + 1)

                    def before():
                        square(0)
                        scores_out(0)

                    pipelined(act, before, turn, lambda: output_out(TILES - 1))

                @block.vector
                def _(dve):
                    def turn_heads(i):
                        dve.wait_ge(k["pad"], i + 1)
                        at_least(dve, k["score"], i)
                        dve.transpose(QKT[:, 0:2 * H, :], QK[:, 0:2 * H, :]).then_inc(k["qkt"], 1)

                    def compact(i):
                        st = Steps(dve, k["sc2"], 1, i)
                        dve.wait_ge(k["sq"], i + 1)
                        at_least(dve, k["dt"], i)
                        dc = DC[:].rearrange("p (h j) -> p h j", j=SEQ)
                        sq = SQ[:].rearrange("p (h a) j -> p h a j", a=2)
                        st.link(dve.tensor_scalar(dc, sq[:, :, 0, :], l2_scale[:, 1:2], None, ALU.mult))
                        dve.scalar_tensor_tensor(dc, sq[:, :, 1, :], l2_scale[:, 2:3], dc, ALU.mult, ALU.add).then_inc(k["dc"], 1)
                        st.end()

                    def add_output(i):
                        dve.wait_ge(k["proj"], i + 1)
                        xi = X[:, bass.ds(i, 1), :]
                        dve.tensor_tensor(xi, PS[:, OB:OB + 1, 0:D], xi, ALU.add).then_inc(k["added"], 1)

                    def turn(i, first, last_turn):
                        if not last_turn:
                            turn_heads(i + 1)
                        st = Steps(dve, k["dve2"], 5, i)
                        dve.wait_ge(k["mixed"], i + 1)
                        mx = PS[:, MB, 0:D].rearrange("p (h j) -> p h j", j=SEQ)
                        st.link(dve.tensor_reduce(smax[:], mx, AX.X, ALU.max))
                        dve.tensor_tensor(MX[:], mx, spread(smax[:], SEQ), ALU.subtract).then_inc(k["expin"], 1)
                        dve.wait_ge(k["expd"], i + 1)
                        at_least(dve, k["pt"], i)
                        st.link(dve.tensor_scalar(S[:, :, 0:SEQ], MX[:], half01[:, 0:1], None, ALU.mult))
                        st.link(dve.tensor_scalar(S[:, :, SEQ:GROUP], MX[:], half01[:, 1:2], None, ALU.mult))
                        dve.transpose(PT[:], S[:]).then_inc(k["pt"], 1)
                        if not last_turn:
                            compact(i + 1)
                        st.link(dve.tensor_reduce(rsum[:], MX[:], AX.X, ALU.add))
                        st.link(dve.reciprocal(rinv[:], rsum[:]))
                        if not first:
                            add_output(i - 1)
                        dve.wait_ge(k["pv"], i + 1)
                        at_least(dve, k["yt"], i)
                        dve.tensor_tensor(Y[:].rearrange("p (h d) -> p h d", d=HD),
                                          PS[:, YB, 0:D].rearrange("p (h d) -> p h d", d=HD),
                                          spread(rinv[:], HD), ALU.mult).then_inc(k["yn"], 1)
                        st.end()

                    def before():
                        turn_heads(0)
                        compact(0)

                    def after():
                        add_output(TILES - 1)
                        dve.wait_ge(k["added"], TILES)

                    pipelined(dve, before, turn, after)

        def quantised_ffn():
            am, amt, diag, sc = local("am", [P, 2]), local("amt", [2, 1]), local("diag", [2, 2]), local("wscale", [P, 4])
            inv = local("wscale_inv", [P, 4])
            ones2 = local("ones2", [2, P])
            fy = local("fy", [P, PAIRS, 2 * D])
            k = {n: sem("ff_" + n) for n in ("dve", "am", "amt", "diag", "scales", "w1q", "w2q", "hid", "gelu", "hq",
                                             "y", "zero", "done")}
            with nc.Block() as block:
                @block.gpsimd
                def _(pool):
                    pool.memset(am[:], 0.0).then_inc(k["zero"], 1)
                    pool.wait_ge(k["zero"], 1)
                    pool.memset(ones2[:], 1.0).then_inc(k["zero"], 1)
                    pool.wait_ge(k["zero"], 2)

                @block.tensor
                def _(pe):
                    landed(pe, "ident", "ff_b2")
                    pe.wait_ge(k["am"], 2)
                    pe.transpose(PS[0:2, 7, 0:P], am[:], ident[:]).then_inc(k["amt"], 1)
                    pe.wait_ge(k["diag"], 1)
                    pe.matmul(PS[:, 6, 0:2], ones2[:], diag[:], start=True, stop=True).then_inc(k["scales"], 1)
                    pe.wait_ge(k["w1q"], 1)
                    n = 0
                    for f in range(FC):
                        for half in range(2):
                            if n >= 4:
                                pe.wait_ge(k["gelu"], n - 3)
                            for c in range(2):
                                last = pe.matmul(PS[:, n % 4, :], ff_w1[:, c, f * P:(f + 1) * P],
                                                 XT[0:KC, c, half * BANK:(half + 1) * BANK],
                                                 start=(c == 0), stop=(c == 1))
                            last.then_inc(k["hid"], 1)
                            n += 1
                    pe.wait_ge(k["w2q"], 1)
                    pe.wait_ge(k["hq"], 2 * FC)
                    for m in range(PAIRS):
                        for t in range(2):
                            o = PS[:, 4 + m, t * D:(t + 1) * D]
                            for f in range(FC):
                                pe.matmul(o, big[:, f, (2 * m + t) * P:(2 * m + t + 1) * P], ff_w2[:, f, :],
                                          start=(f == 0), stop=False)
                            last = pe.matmul(o, ones[:], ff_b2[:], start=False, stop=True)
                        last.then_inc(k["y"], 1)

                @block.scalar
                def _(act):
                    landed(act, "ff_b1")
                    for n in range(2 * FC):
                        act.wait_ge(k["hid"], n + 1)
                        f, half = n // 2, n % 2
                        act.activation(big[:, f, half * BANK:(half + 1) * BANK], PS[:, n % 4, :], ACT.Gelu,
                                       bias=ff_b1[:, f:f + 1]).then_inc(k["gelu"], 1)

                @block.vector
                def _(dve):
                    st = Steps(dve, k["dve"])
                    landed(dve, "ff_w1", "ff_w2", "ff_s", "ident")
                    dve.wait_ge(k["zero"], 2)
                    dve.tensor_reduce(am[0:KC, 0:1], ff_w1[:], AX.XY, ALU.max, apply_absolute_value=True).then_inc(k["am"], 1)
                    dve.tensor_reduce(am[:, 1:2], ff_w2[:], AX.XY, ALU.max, apply_absolute_value=True).then_inc(k["am"], 1)
                    dve.wait_ge(k["amt"], 1)
                    st.link(dve.tensor_reduce(amt[:], PS[0:2, 7, 0:P], AX.X, ALU.max))
                    dve.tensor_scalar(diag[:], ident[0:2, 0:2], amt[:], None, ALU.mult).then_inc(k["diag"], 1)
                    dve.wait_ge(k["scales"], 1)
                    st.link(dve.tensor_scalar(sc[:, 0:2], PS[:, 6, 0:2], 1.0 / 127.0, None, ALU.mult))
                    st.link(dve.tensor_copy(sc[:, 2:4], ff_s[:]))
                    st.link(dve.reciprocal(inv[:], sc[:]))

                    def fake_quantise(dst, src, n, low, done):
                        rows_ = dst.shape[0]
                        scale = sc[0:rows_, n:n + 1]
                        st.link(dve.tensor_scalar(dst, src, inv[0:rows_, n:n + 1], MAGIC, ALU.mult, ALU.add))
                        st.link(dve.tensor_scalar(dst, dst, -MAGIC, 127.0, ALU.add, ALU.min))
                        ins = dve.tensor_scalar(dst, dst, low, scale, ALU.max, ALU.mult)
                        if done is None:
                            st.link(ins)
                        else:
                            ins.then_inc(done, 1)

                    fake_quantise(ff_w1[:], ff_w1[:], 0, -127.0, k["w1q"])
                    fake_quantise(ff_w2[:], ff_w2[:], 1, -127.0, k["w2q"])
                    for n in range(2 * FC):
                        dve.wait_ge(k["gelu"], n + 1)
                        f, half = n // 2, n % 2
                        h = big[:, f, half * BANK:(half + 1) * BANK]
                        fake_quantise(h, h, 2, -128.0, k["hq"])
                    for m in range(PAIRS):
                        dve.wait_ge(k["y"], m + 1)
                        fake_quantise(fy[:, m, :], PS[:, 4 + m, 0:2 * D], 3, -128.0, None)
                        xm = X[:, 2 * m:2 * m + 2, :]
                        dve.tensor_tensor(xm, xm, fy[:, m, :].rearrange("p (t d) -> p t d", t=2), ALU.add).then_inc(k["done"], 1)
                    dve.wait_ge(k["done"], PAIRS)

        GL, GA, GB = (sb(n, [P, TILES, 14]) for n in ("GL", "GA", "GB"))
        top8 = sb("top8", [P, TILES, 8])
        topi = sb("topi", [P, TILES, 8], U32)
        topf = sb("topf", [P, TILES, 8])
        G = sb("G", [P, TILES, H])
        gm, gs_ = sb("gm", [P, TILES, 1]), sb("gs", [P, TILES, 1])

        def gates(name, wg, wname, ncol, kind):
            k = {n: sem(f"{name}_{n}") for n in ("dve", "logits", "less", "exp")}
            soft = {"heads": ((0, 10), (10, 12), (12, 14)), "moe": ((0, E),), "shared": ((0, E),)}[kind]
            ne = soft[0][1]
            with nc.Block() as block:
                @block.tensor
                def _(pe):
                    landed(pe, wname)
                    for t in range(TILES):
                        for c in range(2):
                            last = pe.matmul(PS[:, 7, t * ncol:(t + 1) * ncol], XT[:, c, t * P:(t + 1) * P], wg[:, c, :],
                                             start=(c == 0), stop=(c == 1), skip_group_check=True)
                    last.then_inc(k["logits"], 1)

                @block.scalar
                def _(act):
                    act.wait_ge(k["less"], 1)
                    act.activation(GA[:, :, 0:ncol], GL[:, :, 0:ncol], ACT.Exp).then_inc(k["exp"], 1)

                @block.vector
                def _(dve):
                    landed(dve, "iota10")
                    st = Steps(dve, k["dve"])
                    dve.wait_ge(k["logits"], 1)
                    st.link(dve.tensor_copy(GL[:, :, 0:ncol], PS[:, 7, 0:TILES * ncol].rearrange("p (t e) -> p t e", t=TILES)))
                    for a, b in soft:
                        st.link(dve.tensor_reduce(gm[:, :, 0], GL[:, :, a:b], AX.X, ALU.max))
                        st.link(dve.tensor_tensor(GL[:, :, a:b], GL[:, :, a:b], spread(gm[:, :, 0], b - a), ALU.subtract))
                    if kind == "shared":
                        st.link(dve.tensor_scalar(GL[:, :, E], GL[:, :, E], -1.0, None, ALU.mult))
                    st.link(dve.tensor_scalar(GB[:, :, 0:1], GL[:, :, 0:1], 1.0, None, ALU.mult))
                    dve.sem_inc(k["less"], 1)
                    dve.wait_ge(k["exp"], 1)
                    for a, b in soft:
                        st.link(dve.tensor_reduce(gs_[:, :, 0], GA[:, :, a:b], AX.X, ALU.add))
                        st.link(dve.reciprocal(gm[:], gs_[:]))
                        st.link(dve.tensor_tensor(GA[:, :, a:b], GA[:, :, a:b], spread(gm[:, :, 0], b - a), ALU.mult))
                    for t in range(TILES):
                        dve.max(top8[:, t, :], GA[:, t, 0:ne]).then_inc(k["dve"], 1)
                    st.n += TILES
                    dve.wait_ge(k["dve"], st.n)
                    for t in range(TILES):
                        dve.max_index(topi[:, t, :], top8[:, t, :], GA[:, t, 0:ne]).then_inc(k["dve"], 1)
                    st.n += TILES
                    dve.wait_ge(k["dve"], st.n)
                    st.link(dve.tensor_copy(topf[:], topi[:]))
                    for t in range(TILES):
                        dve.scalar_tensor_tensor(GL[:, t, 0:ne], iota10[:, 0:ne], topf[:, t, 0:1], GA[:, t, 0:ne],
                                                 ALU.is_equal, ALU.mult).then_inc(k["dve"], 1)
                        dve.scalar_tensor_tensor(GB[:, t, 0:ne], iota10[:, 0:ne], topf[:, t, 1:2], GA[:, t, 0:ne],
                                                 ALU.is_equal, ALU.mult).then_inc(k["dve"], 1)
                    st.n += 2 * TILES
                    dve.wait_ge(k["dve"], st.n)
                    st.link(dve.tensor_tensor(GL[:, :, 0:ne], GL[:, :, 0:ne], GB[:, :, 0:ne], ALU.add))
                    if kind == "moe":
                        st.link(dve.tensor_copy(G[:, :, 0:E], GL[:, :, 0:E]))
                        return
                    st.link(dve.tensor_reduce(gs_[:, :, 0], GL[:, :, 0:ne], AX.X, ALU.add))
                    if kind == "heads":
                        eps = float(np.finfo(np.float32).eps)
                        st.link(dve.tensor_scalar(gs_[:], gs_[:], eps, None, ALU.max))
                    st.link(dve.reciprocal(gm[:], gs_[:]))
                    if kind == "heads":
                        st.link(dve.tensor_scalar(GA[:, :, 12:14], GA[:, :, 12:14], 4.0, None, ALU.mult))
                        st.link(dve.tensor_tensor(gm[:, :, 0], gm[:, :, 0], GA[:, :, 13], ALU.mult))
                        st.link(dve.tensor_tensor(G[:, :, 2:H], GL[:, :, 0:10], spread(gm[:, :, 0], 10), ALU.mult))
                        st.link(dve.tensor_tensor(G[:, :, 0:2], GA[:, :, 10:12], spread(GA[:, :, 12], 2), ALU.mult))
                    else:
                        st.link(dve.tensor_scalar(gs_[:, :, 0], GA[:, :, E], 1.0, None, ALU.add))
                        st.link(dve.reciprocal(GB[:, :, 0:1], gs_[:]))
                        st.link(dve.tensor_copy(G[:, :, E:H], spread(GB[:, :, 0], H - E)))
                        st.link(dve.tensor_scalar(GB[:, :, 1], GB[:, :, 0], -1.0, 1.0, ALU.mult, ALU.add))
                        st.link(dve.tensor_tensor(gm[:, :, 0], gm[:, :, 0], GB[:, :, 1], ALU.mult))
                        st.link(dve.tensor_tensor(G[:, :, 0:E], GL[:, :, 0:E], spread(gm[:, :, 0], E), ALU.mult))

        GT = sb("GT", [E, TOKENS])
        GX = sb("GX", [P, H, TILES])

        def expert_bias():
            k = {n: sem("eb_" + n) for n in ("gx", "gt", "gtc", "b", "done")}
            with nc.Block() as block:
                @block.tensor
                def _(pe):
                    landed(pe, "ident", "moe_b2")
                    for t in range(TILES):
                        last = pe.transpose(PS[0:E, t // 4, (t % 4) * P:(t % 4 + 1) * P], G[:, t, 0:E], ident[:])
                    last.then_inc(k["gt"], 1)
                    pe.wait_ge(k["gtc"], 2)
                    for t in range(TILES):
                        last = pe.matmul(PS[:, 2 + t // 2, (t % 2) * D:(t % 2 + 1) * D], GT[:, t * P:(t + 1) * P], moe_b2[:],
                                         start=True, stop=True)
                    last.then_inc(k["b"], 1)

                @block.scalar
                def _(act):
                    act.wait_ge(k["gt"], 1)
                    for b in range(2):
                        act.activation(GT[:, b * BANK:(b + 1) * BANK], PS[0:E, b, :], ACT.Copy).then_inc(k["gtc"], 1)
                    act.wait_ge(k["gtc"], 2)

                @block.vector
                def _(dve):
                    dve.tensor_copy(GX[:, 0:E, :].rearrange("p e t -> p t e"), G[:, :, 0:E]).then_inc(k["gx"], 1)
                    dve.wait_ge(k["b"], 1)
                    for m in range(PAIRS):
                        xm = X[:, 2 * m:2 * m + 2, :]
                        dve.tensor_tensor(xm, PS[:, 2 + m, 0:2 * D].rearrange("p (t d) -> p t d", t=2), xm,
                                          ALU.add).then_inc(k["done"], 1)
                    dve.wait_ge(k["done"], PAIRS)
                    dve.wait_ge(k["gx"], 1)

        HALF_TILES = TILES // 2

        def gelu_experts():
            k = {n: sem("moe_" + n) for n in ("w1a", "w1b", "w2a", "w2b", "hid", "gelu", "y", "sum")}
            w1 = [local(f"moe_w1_{j}", [KB, 2, FF]) for j in range(2)]
            w2 = [local(f"moe_w2_{j}", [P, FC, D]) for j in range(2)]
            hT = big[:].rearrange("p f (h n) -> p h f n", h=2)
            in1, in2 = (k["w1a"], k["w1b"]), (k["w2a"], k["w2b"])
            steps = [(j, half) for j in range(2) for half in range(2)]
            NS = len(steps)
            with nc.Block() as block:
                @block.sync
                def _(sp):
                    with sp.Fori(0, E // 2) as i:
                        for j in range(2):
                            sp.wait_ge(k["y"], i * NS + 2 * j + 1)
                            sp.dma_start(w1[j][:].unsqueeze(1), I["moe_w1"].rearrange("e p c n -> p e c n")[:, bass.ds(i * 2 + j, 1)]).then_inc(in1[j], 16)
                            sp.dma_start(w2[j][:].unsqueeze(1), I["moe_w2"].rearrange("e p c n -> p e c n")[:, bass.ds(i * 2 + j, 1)]).then_inc(in2[j], 16)

                @block.tensor
                def _(pe):
                    pe.sem_inc(k["y"], 3)
                    with pe.Fori(0, E // 2) as i:
                        def hidden(n):
                            j, half = steps[n]
                            if half == 0:
                                pe.wait_ge(in1[j], i * 16 + 16)
                            for f in range(FC):
                                pe.wait_ge(k["gelu"], i * (NS * FC) + n * FC + f + 1)
                                for c in range(2):
                                    last = pe.matmul(PS[:, (n * FC + f) % 4, :], w1[j][:, c, f * P:(f + 1) * P],
                                                     XT[:, c, half * BANK:(half + 1) * BANK], start=(c == 0), stop=(c == 1))
                                last.then_inc(k["hid"], 1)

                        def second(n):
                            j, half = steps[n]
                            if half == 0:
                                pe.wait_ge(in2[j], i * 16 + 16)
                            pe.wait_ge(k["gelu"], i * (NS * FC) + (n + 1) * FC + 4)
                            own(pe, k["sum"], i * (NS * HALF_TILES) + (n + 1) * HALF_TILES)
                            for t in range(HALF_TILES):
                                for f in range(FC):
                                    last = pe.matmul(PS[:, 4 + 2 * half + t // 2, (t % 2) * D:(t % 2 + 1) * D],
                                                     hT[:, half, f, t * P:(t + 1) * P], w2[j][:, f, :],
                                                     start=(f == 0), stop=(f == FC - 1))
                            last.then_inc(k["y"], 1)

                        hidden(0)
                        for n in range(1, NS):
                            hidden(n)
                            second(n - 1)
                        second(NS - 1)

                @block.scalar
                def _(act):
                    act.sem_inc(k["gelu"], 4)
                    with act.Fori(0, E // 2) as i:
                        for n, (j, half) in enumerate(steps):
                            own(act, k["y"], i * NS + n + 2)
                            for f in range(FC):
                                act.wait_ge(k["hid"], i * (NS * FC) + n * FC + f + 1)
                                act.activation(hT[:, half, f, :], PS[:, (n * FC + f) % 4, :], ACT.Gelu).then_inc(k["gelu"], 1)

                @block.vector
                def _(dve):
                    dve.sem_inc(k["sum"], 2 * HALF_TILES)
                    with dve.Fori(0, E // 2) as i:
                        for n, (j, half) in enumerate(steps):
                            dve.wait_ge(k["y"], i * NS + n + 4)
                            own(dve, k["sum"], i * (NS * HALF_TILES) + (n + 2) * HALF_TILES)
                            for t in range(HALF_TILES):
                                xt = X[:, half * HALF_TILES + t, :]
                                dve.scalar_tensor_tensor(xt, PS[:, 4 + 2 * half + t // 2, (t % 2) * D:(t % 2 + 1) * D],
                                                         GX[:, bass.ds(i * 2 + j, 1), half * HALF_TILES + t], xt, ALU.mult,
                                                         ALU.add).then_inc(k["sum"], 1)
                    dve.wait_ge(k["sum"], (E * 2 + 2) * HALF_TILES)

        def silu_experts():
            k = {n: sem("glu_" + n) for n in ("w1a", "w1b", "w2a", "w2b", "hid", "silu", "h", "y", "sum", "gx")}
            gu = [local(f"gu_{j}", [KC, 2, 2 * D]) for j in range(2)]
            dn = [local(f"dn_{j}", [KC, 2, D]) for j in range(2)]
            sg = local("sg", [KC, 2, BANK])
            hT = big[0:KC, 0:4, 0:BANK].rearrange("p (h c) n -> p h c n", h=2)
            in1, in2 = (k["w1a"], k["w1b"]), (k["w2a"], k["w2b"])
            steps = [(j, half) for j in range(2) for half in range(2)]
            NS = len(steps)
            TURNS = H // 2
            with nc.Block() as block:
                @block.sync
                def _(sp):
                    with sp.Fori(0, TURNS) as i:
                        for j in range(2):
                            sp.wait_ge(k["y"], i * NS + 2 * j + 1)
                            sp.dma_start(gu[j][:].unsqueeze(1), I["gu"].rearrange("e p c n -> p e c n")[:, bass.ds(i * 2 + j, 1)]).then_inc(in1[j], 16)
                            sp.dma_start(dn[j][:].unsqueeze(1), I["down"].rearrange("e p c n -> p e c n")[:, bass.ds(i * 2 + j, 1)]).then_inc(in2[j], 16)

                @block.tensor
                def _(pe):
                    pe.sem_inc(k["y"], 3)
                    with pe.Fori(0, TURNS) as i:
                        def hidden(n):
                            j, half = steps[n]
                            if half == 0:
                                pe.wait_ge(in1[j], i * 16 + 16)
                            for u in range(2):
                                pe.wait_ge(k["h"], i * (2 * NS) + 2 * n + u + 1)
                                for which in range(2):
                                    for c in range(2):
                                        last = pe.matmul(PS[0:KC, 2 * u + which, :],
                                                         gu[j][:, c, which * D + u * KC:which * D + (u + 1) * KC],
                                                         XT[0:KC, c, half * BANK:(half + 1) * BANK],
                                                         start=(c == 0), stop=(c == 1))
                                last.then_inc(k["hid"], 1)

                        def second(n):
                            j, half = steps[n]
                            if half == 0:
                                pe.wait_ge(in2[j], i * 16 + 16)
                            pe.wait_ge(k["h"], i * (2 * NS) + 2 * (n + 1) + 2)
                            own(pe, k["sum"], i * (NS * HALF_TILES) + (n + 1) * HALF_TILES)
                            for t in range(HALF_TILES):
                                for c in range(2):
                                    last = pe.matmul(PS[:, 4 + 2 * half + t // 2, (t % 2) * D:(t % 2 + 1) * D],
                                                     hT[:, half, c, t * P:(t + 1) * P], dn[j][:, c, :],
                                                     start=(c == 0), stop=(c == 1))
                            last.then_inc(k["y"], 1)

                        hidden(0)
                        for n in range(1, NS):
                            hidden(n)
                            second(n - 1)
                        second(NS - 1)

                @block.scalar
                def _(act):
                    with act.Fori(0, TURNS) as i:
                        for n in range(NS):
                            for u in range(2):
                                act.wait_ge(k["hid"], i * (2 * NS) + 2 * n + u + 1)
                                act.activation(sg[:, u, :], PS[0:KC, 2 * u, :], ACT.Silu).then_inc(k["silu"], 1)

                @block.vector
                def _(dve):
                    dve.tensor_copy(GX[:].rearrange("p e t -> p t e"), G[:]).then_inc(k["gx"], 1)
                    dve.wait_ge(k["gx"], 1)
                    dve.sem_inc(k["h"], 2)
                    dve.sem_inc(k["sum"], 2 * HALF_TILES)
                    with dve.Fori(0, TURNS) as i:
                        def product(n):
                            j, half = steps[n]
                            dve.wait_ge(k["y"], i * NS + n + 2)
                            for u in range(2):
                                dve.wait_ge(k["silu"], i * (2 * NS) + 2 * n + u + 1)
                                dve.tensor_tensor(hT[:, half, u, :], PS[0:KC, 2 * u + 1, :], sg[:, u, :], ALU.mult).then_inc(k["h"], 1)

                        def add(n):
                            j, half = steps[n]
                            dve.wait_ge(k["y"], i * NS + n + 4)
                            own(dve, k["sum"], i * (NS * HALF_TILES) + (n + 2) * HALF_TILES)
                            for t in range(HALF_TILES):
                                xt = X[:, half * HALF_TILES + t, :]
                                dve.scalar_tensor_tensor(xt, PS[:, 4 + 2 * half + t // 2, (t % 2) * D:(t % 2 + 1) * D],
                                                         GX[:, bass.ds(i * 2 + j, 1), half * HALF_TILES + t], xt, ALU.mult,
                                                         ALU.add).then_inc(k["sum"], 1)

                        product(0)
                        for n in range(1, NS):
                            product(n)
                            add(n - 1)
                        add(NS - 1)
                    dve.wait_ge(k["sum"], (TURNS * NS + 2) * HALF_TILES)

        def store():
            stored = sem("stored")
            with nc.Block() as block:
                @block.sync
                def _(sp):
                    landed(sp, *plan)
                    sp.dma_start(out.rearrange("(t p) d -> p t d", p=P), X[:]).then_inc(stored, 16)
                    sp.wait_ge(stored, 16)

        if stop == 0:
            return store()
        attention("l0", l0_qkv, l0_proj, ("l0_qkv", "l0_proj"), mask_causal, causal_rel=True)
        end_phase()
        norm_and_transpose("n0")
        end_phase()
        if stop == 1:
            return store()
        quantised_ffn()
        end_phase()
        norm_and_transpose("n1")
        end_phase()
        if stop == 2:
            return store()
        attention("l1", l1_qkv, l1_proj, ("l1_qkv", "l1_proj"), mask_block, head_norm=True)
        end_phase()
        norm_and_transpose("n2")
        end_phase()
        if stop == 3:
            return store()
        gates("heads", w_gates, "w_gates", 14, "heads")
        end_phase()
        wide_attention()
        end_phase()
        norm_and_transpose("n3")
        end_phase()
        if stop == 4:
            return store()
        grassmann_attention()
        end_phase()
        norm_and_transpose("n4")
        end_phase()
        if stop == 5:
            return store()
        gates("moe", moe_g, "moe_g", E, "moe")
        end_phase()
        expert_bias()
        end_phase()
        gelu_experts()
        end_phase()
        norm_and_transpose("n5")
        end_phase()
        if stop == 6:
            return store()
        attention("l3", l3_qkv, l3_proj, ("l3_qkv", "l3_proj"), mask_block, quantum=True)
        end_phase()
        norm_and_transpose("n6")
        end_phase()
        if stop == 7:
            return store()
        gates("shared", l3_gates, "l3_gates", E + 1, "shared")
        end_phase()
        silu_experts()
        end_phase()
        norm_and_transpose("n7", transpose=False)
        end_phase()
        return store()


def lay_out(a):
    f = np.float32

    def chunks(w, b=None):
        m = w.shape[1]
        r = np.zeros((KB, 2, m), f)
        r[:KC, 0], r[:KC, 1] = w[:KC], w[KC:]
        if b is not None:
            r[KC, 0] = b
        return r

    def rows(w):
        return np.ascontiguousarray(w.reshape(-1, P, w.shape[1]).transpose(1, 0, 2))

    def every(v):
        return np.ascontiguousarray(np.broadcast_to(np.reshape(v, (1, -1)), (P, np.size(v))))

    x = a["x"].reshape(IMAGES, 4, 16, 4, 16, 3).transpose(0, 1, 3, 2, 4, 5).reshape(TOKENS, FF)
    o = {"patches": rows(np.ascontiguousarray(x.T))}
    o["tok_w"] = rows(a["L0_tok_W"])
    o["pos"] = np.tile(a["L0_tok_pos_emb"], (P // SEQ, 1))
    o["tok_b"] = every(a["L0_tok_b"])
    o["ident"] = np.eye(P, dtype=f)
    n = np.arange(P)[:, None]
    j = np.arange(GROUP)[None, :]
    same = (n % GROUP) // SEQ == j // SEQ
    off = -30000.0
    block = np.where(same, 0.0, off)
    causal = np.where(same & (j % SEQ <= n % SEQ), 0.0, off)
    o["keys_causal"] = causal.astype(f)
    o["keys_block"] = block.astype(f)
    o["block01"] = same.astype(f)
    o["half01"] = np.concatenate([(n % GROUP < SEQ), (n % GROUP >= SEQ)], 1).astype(f)
    o["rel"] = np.tile(np.concatenate([np.zeros((1, HD), f), a["L0_attn_rel_emb"][:SEQ - 1]]), (P // SEQ, 1))
    o["l0_qkv"] = chunks(a["L0_attn_w_attn"], a["L0_attn_b_attn"])
    o["l0_proj"] = chunks(a["L0_attn_w_proj"], a["L0_attn_b_proj"])
    o["ff_w1"] = np.ascontiguousarray(a["L0_ffn_W1"].T.reshape(2, KC, FF).transpose(1, 0, 2))
    o["ff_b1"] = np.ascontiguousarray(a["L0_ffn_b1"].reshape(FC, P).T)
    o["ff_w2"] = rows(np.ascontiguousarray(a["L0_ffn_W2"].T))
    o["ff_b2"] = a["L0_ffn_b2"].reshape(1, D)
    o["ff_s"] = every(np.stack([np.reshape(a["L0_ffn_s_gelu"], ()), np.reshape(a["L0_ffn_s_out"], ())]))
    o["l1_qkv"] = chunks(a["L1_attn_qkv_weight"].T)
    o["l1_proj"] = chunks(a["L1_attn_proj_weight"].T)
    o["w_qkv"] = chunks(a["L1_ffn_qkv_w"], a["L1_ffn_qkv_b"])
    o["w_proj"] = rows(a["L1_ffn_proj_w"])
    o["w_projb"] = a["L1_ffn_proj_b"].reshape(1, D)
    o["w_gates"] = chunks(np.concatenate([a["L1_ffn_wg_w"], a["L1_ffn_wg1_w"], a["L1_ffn_wg0_w"]], 1))
    o["w_affine"] = np.stack([np.tile(a[k].reshape(2, GROUP)[d], NG) for k in (
        "L1_ffn_q_norm_w", "L1_ffn_q_norm_b", "L1_ffn_k_norm_w", "L1_ffn_k_norm_b") for d in range(2)], 1)
    o["iota10"] = np.broadcast_to(np.arange(10, dtype=f), (P, 10))
    o["l2_qkv"] = chunks(a["L2_attn_qkv_w"].T, a["L2_attn_qkv_b"])
    o["l2_proj"] = chunks(a["L2_attn_proj_w"].T, a["L2_attn_proj_b"])
    o["l2_scale"] = np.concatenate([every(a["L2_attn_grassman_scale"]), np.zeros((P, 2), f)], 1)

    def mixing(w, b):
        m = np.zeros((H, SEQ, H, SEQ), f)
        for key in range(SEQ):
            m[:, key, :, key] = w.T
        return chunks(m.reshape(D, D), b)

    o["mix_a"] = mixing(a["L2_attn_conv_w"][:, :H], np.repeat(a["L2_attn_conv_b"], SEQ))
    o["mix_b"] = mixing(a["L2_attn_conv_w"][:, H:], None)
    o["moe_g"] = chunks(a["L2_ffn_Wg"], a["L2_ffn_bg"])
    o["moe_b2"] = a["L2_ffn_b2"]
    o["moe_w1"] = np.stack([chunks(a["L2_ffn_W1"][e], a["L2_ffn_b1"][e]) for e in range(E)])
    o["moe_w2"] = np.stack([rows(a["L2_ffn_W2"][e]) for e in range(E)])
    o["l3_qkv"] = chunks(np.concatenate([a["L3_attn_in_w"].T[:, :2 * D], a["L3_attn_sp_w"].T, a["L3_attn_in_w"].T[:, 2 * D:]], 1),
                         np.concatenate([a["L3_attn_in_b"][:2 * D], a["L3_attn_sp_b"], a["L3_attn_in_b"][2 * D:]]))
    o["l3_proj"] = chunks(a["L3_attn_out_w"].T, a["L3_attn_out_b"])
    o["l3_qw"] = every(a["L3_attn_qw"])
    o["l3_gates"] = chunks(np.concatenate([a["L3_ffn_router_w"], a["L3_ffn_sg_w"]], 1),
                           np.concatenate([np.zeros(E, f), a["L3_ffn_sg_b"]]))
    gate = np.concatenate([a["L3_ffn_w_gate"], a["L3_ffn_ws_gate"].reshape(D, 4, D).transpose(1, 0, 2)])
    up = np.concatenate([a["L3_ffn_w_up"], a["L3_ffn_ws_up"].reshape(D, 4, D).transpose(1, 0, 2)])
    down = np.concatenate([a["L3_ffn_w_down"], a["L3_ffn_ws_down"].reshape(4, D, D)])
    o["gu"] = np.stack([chunks(np.concatenate([gate[e], up[e]], 1))[:KC] for e in range(12)])
    o["down"] = np.stack([chunks(down[e])[:KC] for e in range(12)])
    return {k: np.ascontiguousarray(v) for k, v in o.items()}


STOP = 99


def kernel(**inputs):
    import concourse.bacc as bacc
    from concourse.bass_utils import run_bass_kernel_spmd as run

    nc = bacc.Bacc("TRN2", target_bir_lowering=False, num_devices=1)
    laid = lay_out({k: np.asarray(v) for k, v in inputs.items()})
    arrays = {f"in_{k}": v for k, v in laid.items()}
    aps = {k: nc.dram_tensor(f"in_{k}", v.shape, mybir.dt.from_np(v.dtype), kind="ExternalInput").ap()
           for k, v in laid.items()}
    out = nc.dram_tensor("out_0", (TOKENS, D), FP32, kind="ExternalOutput").ap()
    vit_tower(nc, aps, out, STOP)
    r = run(nc, [arrays], core_ids=[0])
    return r.results[0]["out_0"].reshape(IMAGES, SEQ, D)
```

```python
import concourse.bass as bass
from concourse import mybir
from concourse.alu_op_type import AluOpType as ALU
from contextlib import ExitStack
import numpy as np

FP32 = mybir.dt.float32
FP32R = mybir.dt.float32r
BF16 = mybir.dt.bfloat16
U32 = mybir.dt.uint32
ACT = mybir.ActivationFunctionType
AX = mybir.AxisListType

D = 192
SEQ = 16
IMAGES = 64
TOKENS = IMAGES * SEQ
P = 128
TILES = TOKENS // P
PAIRS = TILES // 2
H = 12
HD = D // H
WD = 64
KC = D // 2
KR = D - P
KB = KC + 1
GROUP = 32
NG = P // GROUP
FF = 768
FC = FF // P
E = 8
LN_EPS = 1e-5
BANK = 512
MAGIC = 1.5 * 2.0 ** 23


class Steps:

    def __init__(self, eng, sem, per=0, index=None):
        self.eng, self.sem, self.per, self.index, self.n = eng, sem, per, index, 0

    def link(self, ins):
        self.n += 1
        ins.then_inc(self.sem, 1)
        self.eng.wait_ge(self.sem, (0 if self.index is None else self.index * self.per) + self.n)

    def end(self):
        assert self.index is None or self.n == self.per, (self.n, self.per)


def spread(ap, n):
    return ap.unsqueeze(ap.ndim).to_broadcast(list(ap.shape) + [n])


def spread_mid(ap, n):
    return ap.unsqueeze(1).to_broadcast([ap.shape[0], n, ap.shape[1]])


ROOT_BITS = float(0x5F3759DF)
ROOT_STEPS = 11


def rsqrt(dve, st, r, v, t):
    ri, vi = r.bitcast(mybir.dt.int32), v.bitcast(mybir.dt.int32)
    st.link(dve.tensor_scalar(ri, vi, 1, None, ALU.arith_shift_right))
    st.link(dve.tensor_scalar(ri, ri, -1.0, ROOT_BITS, ALU.mult, ALU.add))
    for _ in range(3):
        st.link(dve.tensor_tensor(t, r, r, ALU.mult))
        st.link(dve.scalar_tensor_tensor(t, t, -0.5, v, ALU.mult, ALU.mult))
        st.link(dve.scalar_tensor_tensor(r, t, 1.5, r, ALU.add, ALU.mult))


def at_least(eng, s, value):
    if not (isinstance(value, int) and value <= 0):
        eng.wait_ge(s, value)


def pipelined(eng, before, turn, after, two_ahead=False):
    before()
    if two_ahead:
        turn(0, True, 2)
        with eng.Fori(1, TILES - 2) as i:
            turn(i, False, 2)
        turn(TILES - 2, False, 1)
        turn(TILES - 1, False, 0)
    else:
        turn(0, True, False)
        with eng.Fori(1, TILES - 1) as i:
            turn(i, False, False)
        turn(TILES - 1, False, True)
    after()


def reflect(dve, st, dst, vs, tvs, prod, w, j, first, nm):
    n, m = SEQ - j, SEQ - first
    if m == 0:
        return
    d = dst[:, j:SEQ, :, first:SEQ]
    t = prod[:, 0:n, :, 0:m]
    wm = w[:, :, 0:m]
    st.link(dve.tensor_tensor(t, d, spread(vs[:, j:SEQ, :, j], m), ALU.mult))
    st.link(dve.tensor_reduce(wm, t.rearrange("p n c d -> p c d n"), AX.X, ALU.add))
    st.link(dve.tensor_tensor(t, wm.unsqueeze(1).to_broadcast([P, n, nm, m]), spread(tvs[:, j:SEQ, :, j], m), ALU.mult))
    st.link(dve.tensor_tensor(d, d, t, ALU.subtract))


def reflect_on_pool(pool, st, dst, vs, tvs, prod, j, nm):
    n = SEQ - j
    d = dst[:, j:SEQ, :, j:SEQ]
    t = prod[:, 0:n, :, 0:n]
    st.link(pool.tensor_tensor(t, d, spread(vs[:, j:SEQ, :, j], n), ALU.mult))
    left = n
    while left > 1:
        half = left // 2
        st.link(pool.tensor_tensor(t[:, 0:half], t[:, 0:half], t[:, left - half:left], ALU.add))
        left -= half
    sums = prod[:, SEQ, :, 0:n]
    st.link(pool.tensor_copy(sums, t[:, 0]))
    st.link(pool.tensor_tensor(t, sums.unsqueeze(1).to_broadcast([P, n, nm, n]), spread(tvs[:, j:SEQ, :, j], n), ALU.mult))
    st.link(pool.tensor_tensor(d, d, t, ALU.subtract))


def vit_tower(nc, I, out, stop=99):
    ctx = ExitStack()
    with ctx:
        def sb(name, shape, dt=FP32):
            return ctx.enter_context(nc.sbuf_tensor(name, shape, dt))

        scratch = ExitStack()

        def local(name, shape, dt=FP32):
            return scratch.enter_context(nc.sbuf_tensor(name, shape, dt))

        of_phase = []

        def sem(name):
            of_phase.append(nc.alloc_semaphore(name))
            return of_phase[-1]

        def lasting(name):
            return ctx.enter_context(nc.semaphore(name))

        def end_phase():
            nc.clear_and_free_semaphores(list(of_phase))
            of_phase.clear()
            scratch.close()
            nc.all_engine_barrier()

        PS = ctx.enter_context(nc.psum_tensor("PS", [P, 8, BANK], FP32))
        X = sb("X", [P, TILES, D])
        XT = sb("XT", [KB, 2, TOKENS])
        ones = sb("ones", [1, P])
        stats = sb("stats", [P, TILES, 6])
        mv = sb("mv", [P, TILES, 2])
        rstd = sb("rstd", [P, TILES])
        newton = sb("newton", [P, TILES])
        order = lasting("order")

        XTs = sb("XTs", [KB, 2, P])
        XTv = sb("XTv", [KB, 2, P])
        Xs = sb("Xs", [P, D])
        NB = 28
        QK = sb("QK", [P, NB, GROUP])
        QKT = sb("QKT", [P, NB, GROUP])
        SQ = sb("SQ", [P, 2 * H, HD])
        V = sb("V", [P, D])
        S, PT = sb("S", [P, H, GROUP]), sb("PT", [P, H, GROUP])
        smax, rsum, rinv = sb("smax", [P, H]), sb("rsum", [P, H]), sb("rinv", [P, H])
        Y = sb("Y", [P, D])
        YT = sb("YT", [KB, 2, P])
        F = sb("F", [P, 2, GROUP])
        QF, QFT = sb("QF", [P, GROUP]), sb("QFT", [P, GROUP])
        qs = sb("qs", [P, 1])
        mixw = sb("mixw", [P, 2])

        identb = sb("identb", [P, P], BF16)
        mask_causal = sb("mask_causal", [P, H * GROUP], BF16)
        mask_block = sb("mask_block", [P, (H + 2) * GROUP], BF16)

        GL, GA, GB = (sb(n, [P, TILES, 14]) for n in ("GL", "GA", "GB"))
        top8 = sb("top8", [P, TILES, 8])
        topi = sb("topi", [P, TILES, 8], U32)
        topf = sb("topf", [P, TILES, 8])
        G = sb("G", [P, TILES, H])
        gm, gs_ = sb("gm", [P, TILES, 1]), sb("gs", [P, TILES, 1])
        GT = sb("GT", [E, TOKENS])
        GX = sb("GX", [P, H, TILES])

        XH = sb("XH", [P, 2, TOKENS], FP32R)
        XL = sb("XL", [P, TOKENS], FP32R)

        loaded = {}
        plan = []

        early = ExitStack()

        def keep(name, stack=ctx):
            src = I[name]
            loaded[name] = (stack.enter_context(nc.sbuf_tensor("w_" + name, src.shape, src.dtype)), lasting("in_" + name))
            plan.append(name)
            return loaded[name][0]

        ident, iota10, block01 = keep("ident"), keep("iota10"), keep("block01")
        l2_qkv, l2_proj, l2_scale = keep("l2_qkv"), keep("l2_proj"), keep("l2_scale")
        mix_a, mix_b, half01 = keep("mix_a"), keep("mix_b"), keep("half01")
        moe_g, moe_b1, moe_b2 = keep("moe_g"), keep("moe_b1"), keep("moe_b2")
        l3_qkv, l3_proj, l3_qw = keep("l3_qkv"), keep("l3_proj"), keep("l3_qw")
        l3_gates = keep("l3_gates")
        late, plan[:] = list(plan), []
        ctx.callback(early.close)
        tok_w, pos, tok_b = keep("tok_w", early), keep("pos", early), keep("tok_b", early)
        keys_causal, keys_block = keep("keys_causal", early), keep("keys_block", early)
        rel, l0_qkv, l0_proj = keep("rel", early), keep("l0_qkv", early), keep("l0_proj", early)
        ff_w1, ff_b1, ff_w2, ff_b2 = keep("ff_w1", early), keep("ff_b1", early), keep("ff_w2", early), keep("ff_b2", early)
        ff_s = keep("ff_s", early)
        l1_qkv, l1_proj = keep("l1_qkv", early), keep("l1_proj", early)
        w_gates, w_affine = keep("w_gates", early), keep("w_affine", early)
        w_qkv, w_proj, w_projb = keep("w_qkv", early), keep("w_proj", early), keep("w_projb", early)
        plan[3:3] = late[:1]
        plan += late[1:]

        def landed(eng, *names):
            for n in names:
                eng.wait_ge(loaded[n][1], 16)

        def own(eng, s, value):
            if isinstance(value, int):
                at_least(eng, s, value)
                return
            eng.wait_ge(s, value)
            eng.sem_inc(order, 1)

        big = local("patches", [P, FC, TOKENS])
        buf_zero = sem("buf_zero")
        emb_done, emb_added, xt_ones, pos_ready = sem("emb_done"), sem("emb_added"), sem("xt_ones"), sem("pos_ready")
        in_patches = [sem(f"in_patches_{m}") for m in range(PAIRS)]

        def load_patches(eng, m):
            cols = slice(m * 2 * P, (m + 1) * 2 * P)
            eng.dma_start(big[:, :, cols], I["patches"][:, :, cols]).then_inc(in_patches[m], 16)

        with nc.Block() as block:
            @block.sync
            def _(sp):
                sp.dma_start(loaded["tok_w"][0][:], I["tok_w"]).then_inc(loaded["tok_w"][1], 16)
                load_patches(sp, 1)
                for n in plan[1:3]:
                    sp.dma_start(loaded[n][0][:], I[n]).then_inc(loaded[n][1], 16)
                load_patches(sp, 3)
                for n in plan[3:]:
                    sp.dma_start(loaded[n][0][:], I[n]).then_inc(loaded[n][1], 16)

            @block.scalar
            def _(act):
                load_patches(act, 0)
                load_patches(act, 2)

            @block.gpsimd
            def _(pool):
                pool.memset(XT[KC:KB, :, :], 1.0).then_inc(xt_ones, 1)
                pool.wait_ge(xt_ones, 1)
                pool.memset(ones[:], 1.0).then_inc(xt_ones, 1)
                pool.wait_ge(xt_ones, 2)
                pool.memset(QK[:], 0.0).then_inc(buf_zero, 1)
                pool.wait_ge(buf_zero, 1)
                pool.memset(YT[KC:KB, :, :], 1.0).then_inc(buf_zero, 1)
                pool.wait_ge(buf_zero, 2)
                pool.memset(mask_block[:], 0.0).then_inc(buf_zero, 1)
                pool.wait_ge(buf_zero, 3)
                landed(pool, "ident", "keys_causal", "keys_block")
                pool.tensor_copy(identb[:], ident[:]).then_inc(buf_zero, 1)
                pool.wait_ge(buf_zero, 4)
                for mask, keys in ((mask_causal, keys_causal), (mask_block, keys_block)):
                    pool.tensor_copy(mask[:, 0:H * GROUP].rearrange("p (h j) -> p h j", h=H),
                                     spread_mid(keys[:], H)).then_inc(buf_zero, 1)
                pool.wait_ge(buf_zero, 6)

            @block.tensor
            def _(pe):
                landed(pe, "tok_w")
                for t in range(TILES):
                    if t % 2 == 0:
                        pe.wait_ge(in_patches[t // 2], 16)
                    for c in range(FC):
                        last = pe.matmul(PS[:, t // 2, (t % 2) * D:(t % 2 + 1) * D], big[:, c, t * P:(t + 1) * P],
                                         tok_w[:, c, :], start=(c == 0), stop=(c == FC - 1))
                    last.then_inc(emb_done, 1)

            @block.vector
            def _(dve):
                landed(dve, "pos", "tok_b")
                dve.tensor_tensor(pos[:], pos[:], tok_b[:], ALU.add).then_inc(pos_ready, 1)
                dve.wait_ge(pos_ready, 1)
                for m in range(PAIRS):
                    dve.wait_ge(emb_done, 2 * m + 2)
                    dve.tensor_tensor(X[:, 2 * m:2 * m + 2, :], PS[:, m, 0:2 * D].rearrange("p (t d) -> p t d", t=2),
                                      spread_mid(pos[:], 2), ALU.add).then_inc(emb_added, 1)
                dve.wait_ge(emb_added, PAIRS)

        def norm_and_transpose(name, norm=True, transpose=True, split=None):
            dve_step = sem(name + "_dve")
            wide, split_done = (sem(name + "_wide"), sem(name + "_split")) if split else (None, None)
            normed, turned, copied = sem(name + "_normed"), sem(name + "_turned"), sem(name + "_copied")
            with nc.Block() as block:
                @block.sync
                def _(sp):
                    if split:
                        for j in range(2):
                            load_set(sp, j, j, split)

                @block.vector
                def _(dve):
                    if not norm:
                        return
                    steps = Steps(dve, dve_step)
                    for t in range(TILES):
                        dve.bn_stats(stats[:, t, :], X[:, t, :]).then_inc(dve_step, 1)
                    steps.n = TILES
                    dve.wait_ge(dve_step, TILES)
                    for t in range(TILES):
                        dve.bn_aggr(mv[:, t, :], stats[:, t, :]).then_inc(dve_step, 1)
                    steps.n = 2 * TILES
                    dve.wait_ge(dve_step, 2 * TILES)
                    steps.link(dve.tensor_scalar(mv[:, :, 1], mv[:, :, 1], LN_EPS, None, ALU.add))
                    rsqrt(dve, steps, rstd[:], mv[:, :, 1], newton[:])
                    for t in range(TILES):
                        dve.tensor_scalar(X[:, t, :], X[:, t, :], mv[:, t, 0:1], rstd[:, t:t + 1],
                                          ALU.subtract, ALU.mult).then_inc(normed, 1)
                    dve.wait_ge(normed, TILES)
                    if split:
                        for m in range(PAIRS):
                            cols = slice(m * 2 * P, (m + 1) * 2 * P)
                            dve.wait_ge(wide, m + 1)
                            turned_m = PS[:, 4 + m, :].rearrange("p (c n) -> p c n", c=2)
                            dve.tensor_copy(XH[:, :, cols], turned_m).then_inc(split_done, 1)
                            dve.wait_ge(split_done, 3 * m + 1)
                            dve.tensor_tensor(XL[:, cols], turned_m[:, 0, :], XH[:, 0, cols], ALU.subtract).then_inc(split_done, 1)
                            dve.tensor_tensor(XH[KR:P, 1, cols], turned_m[KR:P, 1, :], XH[KR:P, 1, cols],
                                              ALU.subtract).then_inc(split_done, 1)
                        dve.wait_ge(split_done, 3 * PAIRS)

                @block.scalar
                def _(act):
                    if transpose:
                        for m in range(PAIRS):
                            act.wait_ge(turned, m + 1)
                            act.activation(XT[0:KC, :, m * 2 * P:(m + 1) * 2 * P],
                                           PS[0:KC, m, :].rearrange("p (c n) -> p c n", c=2), ACT.Copy).then_inc(copied, 1)
                        act.wait_ge(copied, PAIRS)

                @block.tensor
                def _(pe):
                    if not transpose:
                        return
                    landed(pe, "ident")
                    for m in range(PAIRS):
                        if norm:
                            pe.wait_ge(normed, 2 * m + 2)
                        for t in range(2):
                            for c in range(2):
                                last = pe.transpose(PS[0:KC, m, c * 2 * P + t * P:c * 2 * P + (t + 1) * P],
                                                    X[:, 2 * m + t, c * KC:(c + 1) * KC], ident[:])
                        last.then_inc(turned, 1)
                        if split:
                            for t in range(2):
                                pe.transpose(PS[:, 4 + m, t * P:(t + 1) * P], X[:, 2 * m + t, 0:P], ident[:])
                                dst = slice(2 * P + t * P, 2 * P + (t + 1) * P)
                                pe.transpose(PS[:, 4 + m, dst], X[:, 2 * m + t, KR:D], ident[:])
                                last = pe.transpose(PS[0:KR, 4 + m, dst], X[:, 2 * m + t, P:D], ident[:])
                            last.then_inc(wide, 1)

        end_phase()
        norm_and_transpose("tok", norm=False)
        end_phase()

        def attention(name, wqkv, wproj, w_names, mask, causal_rel=False, head_norm=False, quantum=False):
            s = {k: sem(f"{name}_{k}") for k in (
                "xtq", "xtv", "xs", "qk", "v", "front", "sp", "batch", "state", "wh", "wl", "vcopy", "qcopy",
                "cent", "sqd", "qkt", "score", "expin", "expd",
                "pt", "pv", "yn", "yt", "ytc", "proj", "added", "prep", "soft", "fsq", "fin", "fexp", "qft", "qv",
                "qw", "qadd", "left", "take")}
            nh = H + 2 if quantum else H
            nb = 2 * nh
            wv = 2 * D + (HD if quantum else 0)
            QKV, VB, SB, QVB, YB, TB, OB = range(7)
            nq = 2 if quantum else 1

            if head_norm:
                CNA, SQA = local("CNA", [P, TILES, 2 * H, HD]), local("SQA", [P, TILES, 2 * H, HD])
                hma, hva, hra, hta = (local(n, [P, TILES, 2 * H]) for n in ("hma", "hva", "hra", "hta"))
                with nc.Block() as block:
                    @block.tensor
                    def _(pe):
                        landed(pe, *w_names)
                        for t in range(TILES):
                            for c in range(2):
                                last = pe.matmul(PS[:, t, 0:2 * D], XT[:, c, t * P:(t + 1) * P], wqkv[:, c, 0:2 * D],
                                                 start=(c == 0), stop=(c == 1))
                            last.then_inc(s["sp"], 1)

                    @block.scalar
                    def _(act):
                        for t in range(TILES):
                            act.wait_ge(s["cent"], t + 1)
                            act.activation(SQA[:, t], CNA[:, t], ACT.Square).then_inc(s["sqd"], 1)
                            if t < 2:
                                landed(act, "w_qkv")
                                act.activation(w_qkvh[:, t], w_qkv[:, t], ACT.Copy).then_inc(s["wh"], 1)

                    @block.gpsimd
                    def _(pool):
                        for c in range(2):
                            pool.wait_ge(s["wh"], c + 1)
                            pool.tensor_tensor(w_qkvl[:, c], w_qkv[:, c], w_qkvh[:, c], ALU.subtract).then_inc(s["wl"], 1)
                            pool.wait_ge(s["wl"], c + 1)

                    @block.vector
                    def _(dve):
                        st = Steps(dve, s["batch"])
                        for t in range(TILES):
                            qk = PS[:, t, 0:2 * D].rearrange("p (h d) -> p h d", d=HD)
                            dve.wait_ge(s["sp"], t + 1)
                            st.link(dve.tensor_reduce(hma[:, t, :], qk, AX.X, ALU.add))
                            st.link(dve.tensor_scalar(hma[:, t, :], hma[:, t, :], 1.0 / HD, None, ALU.mult))
                            dve.tensor_tensor(CNA[:, t], qk, spread(hma[:, t, :], HD), ALU.subtract).then_inc(s["cent"], 1)
                        for half in range(2):
                            ts = slice(half * TILES // 2, (half + 1) * TILES // 2)
                            dve.wait_ge(s["sqd"], ts.stop)
                            st.link(dve.tensor_reduce(hva[:, ts, :], SQA[:, ts], AX.X, ALU.add))
                        st.link(dve.tensor_scalar(hva[:], hva[:], 1.0 / HD, LN_EPS, ALU.mult, ALU.add))
                        rsqrt(dve, st, hra[:], hva[:], hta[:])
                        dve.wait_ge(s["cent"], TILES)
                        for half in range(2):
                            ts = slice(half * TILES // 2, (half + 1) * TILES // 2)
                            dve.tensor_tensor(CNA[:, ts], CNA[:, ts], spread(hra[:, ts, :], HD), ALU.mult).then_inc(s["prep"], 1)

            if quantum:
                SPA, SPQ = local("SPA", [P, TILES, HD]), local("SPQ", [P, TILES, HD])
                SPB = local("SPB", [P, TILES, 4, HD])
                sp2, spr, spt = (local(n, [P, TILES]) for n in ("sp2", "spr", "spt"))
                with nc.Block() as block:
                    @block.tensor
                    def _(pe):
                        landed(pe, *w_names)
                        for t in range(TILES):
                            for c in range(2):
                                last = pe.matmul(PS[:, QKV, t * HD:(t + 1) * HD], XT[:, c, t * P:(t + 1) * P],
                                                 wqkv[:, c, 2 * D:wv], start=(c == 0), stop=(c == 1), skip_group_check=True)
                        last.then_inc(s["sp"], 1)

                    @block.scalar
                    def _(act):
                        landed(act, "l3_qw")
                        act.activation(mixw[:, 0:1], l3_qw[:], ACT.Exp, scale=-1.0).then_inc(s["qw"], 1)

                    @block.vector
                    def _(dve):
                        st = Steps(dve, s["batch"])
                        dve.wait_ge(s["qw"], 1)
                        st.link(dve.tensor_scalar(mixw[:, 1:2], mixw[:, 0:1], 1.0, None, ALU.add))
                        st.link(dve.reciprocal(mixw[:, 0:1], mixw[:, 1:2]))
                        st.link(dve.tensor_scalar(mixw[:, 1:2], mixw[:, 0:1], -1.0, 1.0, ALU.mult, ALU.add))
                        dve.wait_ge(s["sp"], 1)
                        st.link(dve.tensor_copy(SPA[:], PS[:, QKV, 0:TILES * HD].rearrange("p (t d) -> p t d", t=TILES)))
                        st.link(dve.tensor_tensor(SPQ[:], SPA[:], SPA[:], ALU.mult))
                        st.link(dve.tensor_reduce(sp2[:], SPQ[:], AX.X, ALU.add))
                        st.link(dve.tensor_scalar(sp2[:], sp2[:], 2.0 ** -64, None, ALU.max))
                        rsqrt(dve, st, spr[:], sp2[:], spt[:])
                        st.link(dve.tensor_tensor(spt[:], spr[:], sp2[:], ALU.mult))
                        st.link(dve.tensor_scalar(spt[:], spt[:], 1e-8, None, ALU.add))
                        st.link(dve.reciprocal(spr[:], spt[:]))
                        half = HD // 2
                        st.link(dve.tensor_tensor(SPA[:], SPA[:], spread(spr[:], HD), ALU.mult))
                        for j in range(3):
                            st.link(dve.tensor_copy(SPB[:, :, j, :], SPA[:]))
                        st.link(dve.tensor_copy(SPB[:, :, 3, 0:half], SPA[:, :, half:HD]))
                        st.link(dve.tensor_scalar(SPB[:, :, 3, half:HD], SPA[:, :, 0:half], -1.0, None, ALU.mult))

            with nc.Block() as block:
                @block.gpsimd
                def _(pool):
                    def stage_heads(i):
                        if head_norm:
                            return
                        own(pool, s["qk"], i)
                        pool.tensor_copy(XTs[:], XT[:, :, bass.ds(i * P, P)]).then_inc(s["xtq"], 1)
                        own(pool, s["xtq"], i + 1)

                    def stage_values(i):
                        own(pool, s["v"], i)
                        pool.tensor_copy(XTv[:], XT[:, :, bass.ds(i * P, P)]).then_inc(s["xtv"], 1)
                        own(pool, s["xtv"], i + 1)

                    def stage_tokens(i):
                        if quantum:
                            own(pool, s["qv"], i)
                            pool.tensor_copy(Xs[:].unsqueeze(1), X[:, bass.ds(i, 1), :]).then_inc(s["xs"], 1)
                            own(pool, s["xs"], i + 1)

                    stage_heads(0)
                    stage_values(0)
                    stage_heads(1)
                    stage_tokens(0)
                    with pool.Fori(1, TILES - 1) as i:
                        stage_values(i)
                        stage_heads(i + 1)
                        stage_tokens(i)
                    stage_values(TILES - 1)
                    stage_tokens(TILES - 1)

                @block.tensor
                def _(pe):
                    landed(pe, "ident", *w_names)

                    def project_heads(i):
                        if head_norm:
                            return
                        own(pe, s["xtq"], i + 1)
                        own(pe, s["left"], i)
                        for c in range(2):
                            last = pe.matmul(PS[:, QKV, 0:2 * D], XTs[:, c, :], wqkv[:, c, 0:2 * D], start=(c == 0), stop=(c == 1))
                        last.then_inc(s["qk"], 1)

                    def project_values(i):
                        own(pe, s["xtv"], i + 1)
                        own(pe, s["vcopy"], i)
                        for c in range(2):
                            last = pe.matmul(PS[:, VB, 0:D], XTv[:, c, :], wqkv[:, c, wv:wv + D], start=(c == 0), stop=(c == 1))
                        last.then_inc(s["v"], 1)

                    def turn_output(i):
                        own(pe, s["yn"], i + 1)
                        for c in range(2):
                            last = pe.transpose(PS[0:KC, TB, c * P:(c + 1) * P], Y[:, c * KC:(c + 1) * KC], ident[:])
                        last.then_inc(s["yt"], 1)

                    def project_output(i):
                        own(pe, s["ytc"], i + 1)
                        own(pe, s["added"], i)
                        for c in range(2):
                            last = pe.matmul(PS[:, OB, 0:D], YT[:, c, :], wproj[:, c, :], start=(c == 0), stop=(c == 1))
                        last.then_inc(s["proj"], 1)

                    def score(i):
                        own(pe, s["qkt"], i + 1)
                        own(pe, s["expin"], i)
                        pe.matmul(PS[:, SB, 0:nh * GROUP], identb[:], mask[:, 0:nh * GROUP], start=True, stop=False,
                                  skip_group_check=True)
                        for h in range(nh):
                            for g in range(NG):
                                r = slice(g * GROUP, g * GROUP + HD)
                                last = pe.matmul(PS[g * GROUP:(g + 1) * GROUP, SB, h * GROUP:(h + 1) * GROUP],
                                                 QKT[r, h, :], QKT[r, nh + h, :], start=False, stop=True,
                                                 skip_group_check=True)
                        last.then_inc(s["score"], 1)

                    def turn(i, first, ahead):
                        if ahead > 0:
                            score(i + 1)
                        if not first:
                            turn_output(i - 1)
                        if ahead > 0:
                            project_values(i + 1)
                        if ahead > 1:
                            project_heads(i + 2)
                        if not first:
                            project_output(i - 1)
                        own(pe, s["pt"], i + 1)
                        own(pe, s["vcopy"], i + 1)
                        for h in range(H):
                            for g in range(NG):
                                r = slice(g * GROUP, (g + 1) * GROUP)
                                last = pe.matmul(PS[r, YB, h * HD:(h + 1) * HD], PT[r, h, :], V[r, h * HD:(h + 1) * HD],
                                                 start=True, stop=True, skip_group_check=True)
                        last.then_inc(s["pv"], 1)
                        if quantum:
                            own(pe, s["qft"], i + 1)
                            own(pe, s["xs"], i + 1)
                            own(pe, s["qadd"], i)
                            for g in range(NG):
                                r = slice(g * GROUP, (g + 1) * GROUP)
                                last = pe.matmul(PS[r, QVB, 0:D], QFT[r, :], Xs[r, :], start=True, stop=True,
                                                 skip_group_check=True)
                            last.then_inc(s["qv"], 1)

                    def before():
                        project_heads(0)
                        project_values(0)
                        score(0)
                        project_heads(1)

                    def after():
                        turn_output(TILES - 1)
                        project_output(TILES - 1)

                    pipelined(pe, before, turn, after, two_ahead=True)

                @block.scalar
                def _(act):
                    def heads_out(i):
                        if head_norm:
                            act.wait_ge(s["prep"], 2)
                        else:
                            act.wait_ge(s["qk"], i + 1)
                        at_least(act, s["qkt"], i)
                        if head_norm:
                            act.activation(QK[:, 0:2 * H, 0:HD].unsqueeze(1), CNA[:, bass.ds(i, 1)],
                                           ACT.Copy).then_inc(s["qcopy"], 1)
                            return
                        if not quantum:
                            n = H if causal_rel else 2 * H
                            act.activation(QK[:, 0:n, 0:HD], PS[:, QKV, 0:n * HD].rearrange(
                                "p (h d) -> p h d", d=HD), ACT.Copy).then_inc(s["qcopy"], 1)
                            return
                        for j in range(2):
                            act.activation(QK[:, j * nh:j * nh + H, 0:HD],
                                           PS[:, QKV, j * D:(j + 1) * D].rearrange("p (h d) -> p h d", d=HD),
                                           ACT.Copy).then_inc(s["qcopy"], 1)

                    def values_out(i):
                        at_least(act, s["v"], i + 1)
                        at_least(act, s["pv"], i)
                        act.activation(V[:], PS[:, VB, 0:D], ACT.Copy).then_inc(s["vcopy"], 1)

                    def output_out(i):
                        act.wait_ge(s["yt"], i + 1)
                        at_least(act, s["proj"], i)
                        act.activation(YT[0:KC, :, :], PS[0:KC, TB, 0:2 * P].rearrange("p (c n) -> p c n", c=2),
                                       ACT.Copy).then_inc(s["ytc"], 1)

                    def exponents(i):
                        if quantum:
                            act.wait_ge(s["score"], i + 1)
                            act.activation(F[:], PS[:, SB, H * GROUP:nh * GROUP].rearrange(
                                "p (h j) -> p h j", j=GROUP), ACT.Square).then_inc(s["fsq"], 1)
                            act.wait_ge(s["fin"], i + 1)
                            act.activation(QF[:], QF[:], ACT.Exp).then_inc(s["fexp"], 1)
                        act.wait_ge(s["expin"], i + 1)
                        act.activation(S[:], S[:], ACT.Exp, scale=HD ** -0.5).then_inc(s["expd"], 1)

                    def turn(i, first, ahead):
                        if not first:
                            output_out(i - 1)
                        if ahead > 0:
                            exponents(i + 1)
                        if ahead > 1:
                            heads_out(i + 2)
                        if ahead > 0:
                            values_out(i + 1)

                    def before():
                        heads_out(0)
                        values_out(0)
                        exponents(0)
                        heads_out(1)

                    pipelined(act, before, turn, lambda: output_out(TILES - 1), two_ahead=True)

                @block.vector
                def _(dve):
                    if causal_rel:
                        landed(dve, "rel")
                    if quantum:
                        landed(dve, "block01")

                    def take(i):
                        st = Steps(dve, s["take"], 1 if causal_rel else 0, i)
                        if not head_norm:
                            dve.wait_ge(s["qk"], i + 1)
                        dve.wait_ge(s["qcopy"], i * nq + nq)
                        if causal_rel:
                            st.link(dve.tensor_tensor(QK[:, H:2 * H, 0:HD],
                                                      PS[:, QKV, D:2 * D].rearrange("p (h d) -> p h d", d=HD),
                                                      spread_mid(rel[:], H), ALU.add))
                            dve.sem_inc(s["left"], 1)
                        if quantum:
                            dve.sem_inc(s["left"], 1)
                        st.end()

                    def prepare(i):
                        st = Steps(dve, s["state"], 1 if quantum else 0, i)
                        if quantum:
                            st.link(dve.tensor_copy(QK[:, 0:nb, 0:HD].rearrange("p (a h) d -> p a h d", a=2)[:, :, H:nh, :],
                                                    SPB[:, bass.ds(i, 1)].rearrange("p t (a h) d -> p (t a) h d", a=2)))
                        st.end()
                        at_least(dve, s["score"], i)
                        dve.transpose(QKT[:, 0:nb, :], QK[:, 0:nb, :]).then_inc(s["qkt"], 1)

                    def add_output(i):
                        dve.wait_ge(s["proj"], i + 1)
                        xi, o = X[:, bass.ds(i, 1), :], PS[:, OB:OB + 1, 0:D]
                        if quantum:
                            dve.scalar_tensor_tensor(xi, o, mixw[:, 1:2], xi, ALU.mult, ALU.add).then_inc(s["added"], 1)
                        else:
                            dve.tensor_tensor(xi, o, xi, ALU.add).then_inc(s["added"], 1)

                    def less_maximum(i):
                        st = Steps(dve, s["front"], 1, i)
                        sc_ps = PS[:, SB, 0:H * GROUP].rearrange("p (h j) -> p h j", j=GROUP)
                        dve.wait_ge(s["score"], i + 1)
                        if quantum:
                            dve.wait_ge(s["fsq"], i + 1)
                            dve.tensor_tensor(QF[:], F[:, 0, :], F[:, 1, :], ALU.add).then_inc(s["fin"], 1)
                        st.link(dve.tensor_reduce(smax[:], sc_ps, AX.X, ALU.max))
                        at_least(dve, s["pt"], i)
                        dve.tensor_tensor(S[:], sc_ps, spread(smax[:], GROUP), ALU.subtract).then_inc(s["expin"], 1)
                        st.end()

                    def turn(i, first, ahead):
                        st = Steps(dve, s["soft"], 6 if quantum else 2, i)
                        if quantum:
                            dve.wait_ge(s["fexp"], i + 1)
                            st.link(dve.tensor_tensor(QF[:], QF[:], block01[:], ALU.mult))
                            dve.transpose(QFT[:], QF[:]).then_inc(s["qft"], 1)
                            st.link(dve.tensor_reduce(qs[:], QF[:], AX.X, ALU.add))
                            st.link(dve.reciprocal(qs[:], qs[:]))
                            st.link(dve.tensor_tensor(qs[:], qs[:], mixw[:, 0:1], ALU.mult))
                        dve.wait_ge(s["expd"], i + 1)
                        dve.transpose(PT[:], S[:]).then_inc(s["pt"], 1)
                        st.link(dve.tensor_reduce(rsum[:], S[:], AX.X, ALU.add))
                        st.link(dve.reciprocal(rinv[:], rsum[:]))
                        st.end()
                        if ahead > 0:
                            less_maximum(i + 1)
                        if ahead > 1:
                            take(i + 2)
                            prepare(i + 2)
                        if not first:
                            add_output(i - 1)
                        dve.wait_ge(s["pv"], i + 1)
                        at_least(dve, s["yt"], i)
                        dve.tensor_tensor(Y[:].rearrange("p (h d) -> p h d", d=HD),
                                          PS[:, YB, 0:D].rearrange("p (h d) -> p h d", d=HD),
                                          spread(rinv[:], HD), ALU.mult).then_inc(s["yn"], 1)
                        if quantum:
                            dve.wait_ge(s["qv"], i + 1)
                            xi = X[:, bass.ds(i, 1), :]
                            dve.scalar_tensor_tensor(xi, PS[:, QVB:QVB + 1, 0:D], qs[:], xi, ALU.mult, ALU.add).then_inc(s["qadd"], 1)
                            dve.wait_ge(s["qadd"], i + 1)

                    def after():
                        add_output(TILES - 1)
                        dve.wait_ge(s["added"], TILES)

                    def before():
                        take(0)
                        prepare(0)
                        less_maximum(0)
                        take(1)
                        prepare(1)

                    pipelined(dve, before, turn, after, two_ahead=True)

        def wide_attention():
            WB = 2 * H * 2
            CW = local("CW", [P, 2 * H, WD])
            SW = local("SW", [P, 2 * H * WD])
            QKW = local("QKW", [P, WB, GROUP])
            KW = local("KW", [P, WB, GROUP])
            VW = local("VW", [P, H * WD])
            YW = local("YW", [P, H * WD])
            YTW = local("YTW", [P, 6, P])
            xq, xv = ([local(f"{n}_{p}", [KB, 2, P], FP32R) for p in ("high", "low")] for n in ("xq", "xv"))
            wr, wv, wt, wm, wi = (local(n, [P, 2 * H]) for n in ("wr", "wv", "wt", "wm", "wi"))
            k = {n: sem("wide_" + n) for n in ("xts", "xtv", "qk", "v", "vcopy", "cent", "sq", "turned", "affine", "score",
                                               "expin", "expd", "pt", "pv", "yn", "yt", "ytc", "proj", "added",
                                               "prep", "soft", "take")}
            HB = H * WD // 2

            with nc.Block() as block:
                @block.gpsimd
                def _(pool):
                    def stage_parts(i, parts, used, done):
                        own(pool, used, i)
                        tile = XT[:, :, bass.ds(i * P, P)]
                        pool.tensor_copy(parts[0][:], tile).then_inc(done, 1)
                        own(pool, done, i * 2 + 1)
                        pool.tensor_tensor(parts[1][:], tile, parts[0][:], ALU.subtract).then_inc(done, 1)
                        own(pool, done, i * 2 + 2)

                    def stage(i):
                        stage_parts(i, xq, k["qk"], k["xts"])
                        stage_parts(i, xv, k["v"], k["xtv"])

                    stage(0)
                    with pool.Fori(1, TILES) as i:
                        stage(i)

                @block.tensor
                def _(pe):
                    landed(pe, "w_proj", "w_projb")

                    def product(bank, x, block):
                        terms = [(c, u, v) for c in range(2) for u, v in ((x[0], w_qkvh), (x[1], w_qkvh), (x[0], w_qkvl))]
                        for m, (c, u, v) in enumerate(terms):
                            last = pe.matmul(PS[:, bank, 0:HB], u[:, c, :], v[:, c, block * HB:(block + 1) * HB],
                                             start=(m == 0), stop=(m == len(terms) - 1))
                        return last

                    def project(i):
                        own(pe, k["xts"], i * 2 + 2)
                        own(pe, k["cent"], i)
                        for b in range(4):
                            last = product(b, xq, b)
                        last.then_inc(k["qk"], 1)

                    def project_values(i):
                        own(pe, k["xtv"], i * 2 + 2)
                        own(pe, k["expin"], i)
                        own(pe, k["added"], i - 1)
                        for b in range(2):
                            last = product(6 + b, xv, 4 + b)
                        last.then_inc(k["v"], 1)

                    def turn_output(i):
                        own(pe, k["yn"], i + 1)
                        for j in range(6):
                            last = pe.transpose(PS[:, 4 + j // 3, (j % 3) * P:(j % 3 + 1) * P], YW[:, j * P:(j + 1) * P], ident[:])
                        last.then_inc(k["yt"], 1)

                    def project_output(i):
                        own(pe, k["ytc"], i + 1)
                        own(pe, k["vcopy"], i + 1)
                        for j in range(6):
                            pe.matmul(PS[:, 7, 0:D], YTW[:, j, :], w_proj[:, j, :], start=(j == 0), stop=False)
                        pe.matmul(PS[:, 7, 0:D], ones[:], w_projb[:], start=False, stop=True).then_inc(k["proj"], 1)

                    def turn(i, first, last_turn):
                        if not last_turn:
                            project(i + 1)
                        own(pe, k["affine"], i * 4 + 4)
                        own(pe, k["vcopy"], i + 1)
                        pe.matmul(PS[:, 6, 0:H * GROUP], identb[:], mask_block[:, 0:H * GROUP], start=True, stop=False,
                                  skip_group_check=True)
                        for h in range(H):
                            for g in range(NG):
                                r = slice(g * GROUP, (g + 1) * GROUP)
                                for d in range(2):
                                    last = pe.matmul(PS[r, 6, h * GROUP:(h + 1) * GROUP], KW[r, 2 * h + d, :],
                                                     KW[r, 2 * H + 2 * h + d, :], start=False, stop=True,
                                                     skip_group_check=True)
                        last.then_inc(k["score"], 1)
                        if not first:
                            turn_output(i - 1)
                            project_output(i - 1)
                        own(pe, k["pt"], i + 1)
                        for h in range(H):
                            for g in range(NG):
                                r = slice(g * GROUP, (g + 1) * GROUP)
                                last = pe.matmul(PS[r, 4 + h // 6, (h % 6) * WD:(h % 6 + 1) * WD], PT[r, h, :],
                                                 VW[r, h * WD:(h + 1) * WD], start=True, stop=True, skip_group_check=True)
                        last.then_inc(k["pv"], 1)
                        if not last_turn:
                            project_values(i + 1)

                    def before():
                        project(0)
                        project_values(0)

                    def after():
                        turn_output(TILES - 1)
                        project_output(TILES - 1)

                    pipelined(pe, before, turn, after)

                @block.scalar
                def _(act):
                    landed(act, "w_affine")

                    def square(i):
                        act.wait_ge(k["cent"], i + 1)
                        act.activation(SW[:], CW[:].rearrange("p h d -> p (h d)"), ACT.Square).then_inc(k["sq"], 1)

                    def affine(i):
                        at_least(act, k["score"], i)
                        act.wait_ge(k["turned"], i + 1)
                        for j in range(2):
                            for d in range(2):
                                v = KW[:].rearrange("p (j h d) n -> p j h d n", j=2, d=2)[:, j, :, d, :]
                                act.activation(v, v, ACT.Identity, scale=w_affine[:, 4 * j + d:4 * j + d + 1],
                                               bias=w_affine[:, 4 * j + 2 + d:4 * j + 3 + d]).then_inc(k["affine"], 1)

                    def values_out(i):
                        act.wait_ge(k["v"], i + 1)
                        at_least(act, k["pv"], i)
                        act.activation(VW[:].rearrange("p (b n) -> p b n", b=2), PS[:, 6:8, 0:HB], ACT.Copy).then_inc(k["vcopy"], 1)

                    def output_out(i):
                        act.wait_ge(k["yt"], i + 1)
                        at_least(act, k["proj"], i)
                        act.activation(YTW[:].rearrange("p (b j) n -> p b (j n)", b=2), PS[:, 4:6, 0:3 * P],
                                       ACT.Copy).then_inc(k["ytc"], 1)

                    def turn(i, first, last_turn):
                        if not last_turn:
                            square(i + 1)
                        if not first:
                            output_out(i - 1)
                        act.wait_ge(k["expin"], i + 1)
                        act.activation(S[:], S[:], ACT.Exp, scale=WD ** -0.5).then_inc(k["expd"], 1)
                        if not last_turn:
                            affine(i + 1)
                            values_out(i + 1)

                    def before():
                        square(0)
                        affine(0)
                        values_out(0)

                    pipelined(act, before, turn, lambda: output_out(TILES - 1))

                @block.vector
                def _(dve):
                    def take(i):
                        st = Steps(dve, k["take"], 2, i)
                        dve.wait_ge(k["qk"], i + 1)
                        qk = PS[:, 0:4, 0:HB].rearrange("p b (h d) -> p b h d", d=WD)
                        cw = CW[:].rearrange("p (b h) d -> p b h d", b=4)
                        mean = wm[:].rearrange("p (b h) -> p b h", b=4)
                        st.link(dve.tensor_reduce(mean, qk, AX.X, ALU.add))
                        st.link(dve.tensor_scalar(wm[:], wm[:], 1.0 / WD, None, ALU.mult))
                        dve.tensor_tensor(cw, qk, spread(mean, WD), ALU.subtract).then_inc(k["cent"], 1)
                        st.end()

                    def prepare(i, adding=False):
                        st = Steps(dve, k["prep"], 3 + ROOT_STEPS, i)
                        dve.wait_ge(k["sq"], i + 1)
                        st.link(dve.tensor_reduce(wv[:], SW[:].rearrange("p (h d) -> p h d", d=WD), AX.X, ALU.add))
                        if adding:
                            add_output(i - 2)
                        st.link(dve.tensor_scalar(wv[:], wv[:], 1.0 / WD, LN_EPS, ALU.mult, ALU.add))
                        rsqrt(dve, st, wr[:], wv[:], wt[:])
                        st.link(dve.tensor_tensor(QKW[:].rearrange("p (h d) n -> p h (d n)", d=2), CW[:], spread(wr[:], WD), ALU.mult))
                        at_least(dve, k["score"], i)
                        dve.transpose(KW[:], QKW[:]).then_inc(k["turned"], 1)
                        st.end()

                    def add_output(i):
                        dve.wait_ge(k["proj"], i + 1)
                        xi = X[:, bass.ds(i, 1), :]
                        dve.tensor_tensor(xi, PS[:, 7:8, 0:D], xi, ALU.add).then_inc(k["added"], 1)

                    def turn(i, first, last_turn):
                        if not last_turn:
                            take(i + 1)
                        st = Steps(dve, k["soft"], 4, i)
                        dve.wait_ge(k["score"], i + 1)
                        sc_ps = PS[:, 6, 0:H * GROUP].rearrange("p (h j) -> p h j", j=GROUP)
                        st.link(dve.tensor_reduce(smax[:], sc_ps, AX.X, ALU.max))
                        at_least(dve, k["pt"], i)
                        dve.tensor_tensor(S[:], sc_ps, spread(smax[:], GROUP), ALU.subtract).then_inc(k["expin"], 1)
                        dve.wait_ge(k["expd"], i + 1)
                        dve.transpose(PT[:], S[:]).then_inc(k["pt"], 1)
                        st.link(dve.tensor_reduce(rsum[:], S[:], AX.X, ALU.add))
                        st.link(dve.reciprocal(rinv[:], rsum[:]))
                        st.link(dve.tensor_tensor(wi[:, 0:H].unsqueeze(1), rinv[:].unsqueeze(1), G[:, bass.ds(i, 1), :], ALU.mult))
                        st.end()
                        if not last_turn:
                            prepare(i + 1, adding=not first)
                        elif not first:
                            add_output(i - 1)
                        dve.wait_ge(k["pv"], i + 1)
                        at_least(dve, k["yt"], i)
                        dve.tensor_tensor(YW[:].rearrange("p (b h d) -> p b h d", b=2, d=WD),
                                          PS[:, 4:6, 0:HB].rearrange("p b (h d) -> p b h d", d=WD),
                                          spread(wi[:, 0:H].rearrange("p (b h) -> p b h", b=2), WD), ALU.mult).then_inc(k["yn"], 1)

                    def after():
                        add_output(TILES - 1)
                        dve.wait_ge(k["added"], TILES)

                    def before():
                        take(0)
                        prepare(0)

                    pipelined(dve, before, turn, after)

        def grassmann_attention():
            k = {n: sem("gr_" + n) for n in ("qk", "qkc", "v", "vc", "to", "a", "q", "qo", "qb", "dve", "mixsum",
                                             "xts", "pad", "qkt", "score", "sq", "dc", "dt", "dtc", "mixed", "expin",
                                             "expd", "pt", "pv", "yn", "yt", "ytc", "proj", "added", "dve2", "sc2", "prep", "ss", "root", "tri", "qpool")}
            there = nc.dram_tensor("heads_there", (TOKENS, 2 * D), FP32).ap()
            back = nc.dram_tensor("heads_back", (TOKENS, 2 * D), FP32).ap()
            NM = 2 * (H // 2)
            M = SEQ
            VA = local("VA", [P, TILES, D])
            QT_ = local("qr_work", [P, 6144])[:]
            tok = QT_[:, 0:TILES * 2 * D].rearrange("p (t n) -> p t n", t=TILES)
            A = QT_[:, 3072:6144].rearrange("p (n c d) -> p n c d", n=M, c=NM)
            Q = local("QM", [P, M, NM, M])
            T = QT_[:, 0:3072].rearrange("p (n c d) -> p n c d", n=M, c=NM)
            col = local("qr_col", [P, M, NM])
            w = local("qr_w", [P, NM, M])
            tail, nrm, v0, tau, tmp = (local("qr_" + n, [P, NM]) for n in ("tail", "nrm", "v0", "tau", "tmp"))
            TV = local("qr_tv", [P, M, NM, M])
            NV = NM - NM // 4
            pool_prod = local("qr_pool", [P, M + 1, NM - NV, M])

            def half_rows(ap, half, which):
                o = which * D + half * KC
                return ap.rearrange("(b n) c -> b n c", n=SEQ)[:, :, o:o + KC]

            def matrices(which, buf, half):
                return buf[half * 64:(half + 1) * 64, :, which * 6:(which + 1) * 6, :].rearrange("b n c d -> b n (c d)")

            def load_heads(eng, which):
                eng.wait_ge(k["to"], 16)
                for half in range(2):
                    eng.dma_start(matrices(which, A, half), half_rows(there, half, which)).then_inc(k["a"], 16)

            def store_heads(eng, which):
                eng.wait_ge(k["q"], 2)
                for half in range(2):
                    eng.dma_start(half_rows(back, half, which), matrices(which, Q, half)).then_inc(k["qo"], 16)

            with nc.Block() as block:
                @block.tensor
                def _(pe):
                    landed(pe, "l2_qkv")
                    for t in range(TILES):
                        for c in range(2):
                            last = pe.matmul(PS[:, t, 0:2 * D], XT[:, c, t * P:(t + 1) * P], l2_qkv[:, c, 0:2 * D],
                                             start=(c == 0), stop=(c == 1))
                        last.then_inc(k["qk"], 1)
                    for t in range(TILES):
                        pe.wait_ge(k["qkc"], t + 1)
                        for c in range(2):
                            last = pe.matmul(PS[:, t, 0:D], XT[:, c, t * P:(t + 1) * P], l2_qkv[:, c, 2 * D:],
                                             start=(c == 0), stop=(c == 1))
                        last.then_inc(k["v"], 1)

                @block.scalar
                def _(act):
                    for t in range(TILES):
                        act.wait_ge(k["qk"], t + 1)
                        act.activation(tok[:, t, :], PS[:, t, 0:2 * D], ACT.Copy).then_inc(k["qkc"], 1)
                    for t in range(TILES):
                        act.wait_ge(k["v"], t + 1)
                        act.activation(VA[:, t, :], PS[:, t, 0:D], ACT.Copy).then_inc(k["vc"], 1)
                    act.wait_ge(k["vc"], TILES)
                    load_heads(act, 1)
                    for j in range(M - 1):
                        act.wait_ge(k["ss"], j + 1)
                        act.activation(tmp[:], nrm[:], ACT.Sqrt).then_inc(k["root"], 1)
                    store_heads(act, 1)

                @block.gpsimd
                def _(pool):
                    landed(pool, "mix_a", "mix_b", "half01", "l2_scale")
                    pool.tensor_tensor(mix_a[:], mix_a[:], mix_b[:], ALU.add).then_inc(k["mixsum"], 1)
                    pool.wait_ge(k["mixsum"], 1)
                    pool.tensor_tensor(l2_scale[:, 1:3], half01[:], l2_scale[:, 0:1].to_broadcast([P, 2]), ALU.mult).then_inc(k["mixsum"], 1)
                    pool.wait_ge(k["mixsum"], 2)
                    st = Steps(pool, k["qpool"])
                    pool.wait_ge(k["tri"], 1)
                    for j in reversed(range(M - 1)):
                        reflect_on_pool(pool, st, Q[:, :, NV:NM, :], A[:, :, NV:NM, :], TV[:, :, NV:NM, :], pool_prod, j, NM - NV)
                    pool.sem_inc(k["q"], 1)

                @block.sync
                def _(sp):
                    sp.wait_ge(k["qkc"], TILES)
                    sp.dma_start(there.rearrange("(t p) c -> p t c", p=P), tok).then_inc(k["to"], 16)
                    load_heads(sp, 0)
                    store_heads(sp, 0)
                    sp.wait_ge(k["qo"], 64)
                    sp.dma_start(tok, back.rearrange("(t p) c -> p t c", p=P)).then_inc(k["qb"], 16)
                    sp.wait_ge(k["qb"], 16)

                @block.vector
                def _(dve):
                    st = Steps(dve, k["dve"])
                    st.link(dve.memset(Q[:], 0.0))
                    for n in range(M):
                        dve.memset(Q[:, n, :, n], 1.0).then_inc(k["dve"], 1)
                    st.n += M
                    dve.wait_ge(k["dve"], st.n)
                    dve.wait_ge(k["a"], 64)
                    for j in range(M - 1):
                        m = M - j
                        x = A[:, j:M, :, j]
                        cj = col[:, 0:m, :]
                        st.link(dve.tensor_tensor(cj, x, x, ALU.mult))
                        st.link(dve.tensor_reduce(tail[:], cj[:, 1:m, :].rearrange("p n c -> p c n"), AX.X, ALU.add))
                        st.link(dve.tensor_tensor(nrm[:], tail[:], cj[:, 0, :], ALU.add))
                        dve.tensor_scalar(nrm[:], nrm[:], 1e-37, None, ALU.max).then_inc(k["ss"], 1)
                        st.link(dve.tensor_scalar(v0[:], A[:, j, :, j], 0.0, 2.0, ALU.is_ge, ALU.mult))
                        st.link(dve.tensor_scalar(tail[:], tail[:], 0.0, None, ALU.is_gt))
                        dve.wait_ge(k["root"], j + 1)
                        st.link(dve.reciprocal(tau[:], tmp[:]))
                        st.link(dve.tensor_tensor(tau[:], tau[:], nrm[:], ALU.mult))
                        st.link(dve.tensor_tensor(tau[:], tau[:], tmp[:], ALU.add))
                        st.link(dve.tensor_scalar(nrm[:], tau[:], 0.5, None, ALU.mult))
                        st.link(dve.scalar_tensor_tensor(v0[:], v0[:], 1.0, nrm[:], ALU.subtract, ALU.mult))
                        st.link(dve.tensor_tensor(A[:, j, :, j], A[:, j, :, j], v0[:], ALU.add))
                        st.link(dve.tensor_tensor(v0[:], v0[:], A[:, j, :, j], ALU.mult))
                        st.link(dve.reciprocal(tau[:], v0[:]))
                        st.link(dve.tensor_tensor(tau[:], tau[:], tail[:], ALU.mult))
                        st.link(dve.tensor_tensor(TV[:, j:M, :, j], A[:, j:M, :, j], tau[:].unsqueeze(1).to_broadcast([P, m, NM]), ALU.mult))
                        reflect(dve, st, A, A, TV, T, w, j, j + 1, NM)
                    dve.sem_inc(k["tri"], 1)
                    for j in reversed(range(M - 1)):
                        reflect(dve, st, Q[:, :, 0:NV, :], A[:, :, 0:NV, :], TV[:, :, 0:NV, :], T[:, :, 0:NV, :], w[:, 0:NV, :],
                                j, j, NV)
                    dve.sem_inc(k["q"], 1)

            SB, DB, MB, YB, TB, OB = range(6)
            DC = local("DC", [P, D])
            DT = local("DT", [KB, 2, P])
            MX = local("MX", [P, H, SEQ])
            with nc.Block() as block:
                @block.gpsimd
                def _(pool):
                    def stage_heads(i):
                        own(pool, k["qkt"], i)
                        pool.tensor_copy(QK[:, 0:2 * H, 0:HD].unsqueeze(1), tok[:, bass.ds(i, 1), :].rearrange(
                            "p t (h d) -> p t h d", d=HD)).then_inc(k["pad"], 1)
                        own(pool, k["pad"], i + 1)

                    def stage_values(i):
                        own(pool, k["pv"], i)
                        pool.tensor_copy(V[:].unsqueeze(1), VA[:, bass.ds(i, 1), :]).then_inc(k["xts"], 1)
                        own(pool, k["xts"], i + 1)

                    pool.memset(DT[KC:KB, :, :], 1.0).then_inc(k["prep"], 1)
                    pool.wait_ge(k["prep"], 1)
                    stage_heads(0)
                    stage_values(0)
                    stage_heads(1)
                    with pool.Fori(1, TILES - 1) as i:
                        stage_heads(i + 1)
                        stage_values(i)
                    stage_values(TILES - 1)

                @block.tensor
                def _(pe):
                    landed(pe, "l2_proj", "ident", "mix_a")

                    def score(i):
                        own(pe, k["qkt"], i + 1)
                        own(pe, k["sq"], i)
                        for h in range(H):
                            for g in range(NG):
                                r = slice(g * GROUP, g * GROUP + HD)
                                last = pe.matmul(PS[g * GROUP:(g + 1) * GROUP, SB, h * GROUP:(h + 1) * GROUP],
                                                 QKT[r, h, :], QKT[r, H + h, :], start=True, stop=True,
                                                 skip_group_check=True)
                        last.then_inc(k["score"], 1)

                    def turn_scores(i):
                        own(pe, k["dc"], i + 1)
                        for c in range(2):
                            last = pe.transpose(PS[0:KC, DB, c * P:(c + 1) * P], DC[:, c * KC:(c + 1) * KC], ident[:])
                        last.then_inc(k["dt"], 1)

                    def mix(i):
                        own(pe, k["dtc"], i + 1)
                        own(pe, k["expin"], i)
                        for c in range(2):
                            last = pe.matmul(PS[:, MB, 0:D], DT[:, c, :], mix_a[:, c, :], start=(c == 0), stop=(c == 1))
                        last.then_inc(k["mixed"], 1)

                    def turn_output(i):
                        own(pe, k["yn"], i + 1)
                        for c in range(2):
                            last = pe.transpose(PS[0:KC, TB, c * P:(c + 1) * P], Y[:, c * KC:(c + 1) * KC], ident[:])
                        last.then_inc(k["yt"], 1)

                    def project_output(i):
                        own(pe, k["ytc"], i + 1)
                        own(pe, k["added"], i)
                        for c in range(2):
                            last = pe.matmul(PS[:, OB, 0:D], YT[:, c, :], l2_proj[:, c, :], start=(c == 0), stop=(c == 1))
                        last.then_inc(k["proj"], 1)

                    def turn(i, first, last_turn):
                        if not first:
                            turn_output(i - 1)
                        if not last_turn:
                            score(i + 1)
                        if not first:
                            project_output(i - 1)
                        if not last_turn:
                            turn_scores(i + 1)
                            mix(i + 1)
                        own(pe, k["pt"], i + 1)
                        own(pe, k["xts"], i + 1)
                        for h in range(H):
                            for g in range(NG):
                                r = slice(g * GROUP, (g + 1) * GROUP)
                                last = pe.matmul(PS[r, YB, h * HD:(h + 1) * HD], PT[r, h, :], V[r, h * HD:(h + 1) * HD],
                                                 start=True, stop=True, skip_group_check=True)
                        last.then_inc(k["pv"], 1)

                    def before():
                        score(0)
                        turn_scores(0)
                        mix(0)

                    def after():
                        turn_output(TILES - 1)
                        project_output(TILES - 1)

                    pipelined(pe, before, turn, after)

                @block.scalar
                def _(act):
                    def square(i):
                        act.wait_ge(k["score"], i + 1)
                        at_least(act, k["dc"], i)
                        act.activation(SQ[:].rearrange("p (h a) j -> p h (a j)", a=2), PS[:, SB, 0:H * GROUP].rearrange(
                            "p (h j) -> p h j", j=GROUP), ACT.Square).then_inc(k["sq"], 1)

                    def scores_out(i):
                        act.wait_ge(k["dt"], i + 1)
                        act.activation(DT[0:KC, :, :], PS[0:KC, DB, 0:2 * P].rearrange("p (c n) -> p c n", c=2),
                                       ACT.Copy).then_inc(k["dtc"], 1)

                    def output_out(i):
                        act.wait_ge(k["yt"], i + 1)
                        act.activation(YT[0:KC, :, :], PS[0:KC, TB, 0:2 * P].rearrange("p (c n) -> p c n", c=2),
                                       ACT.Copy).then_inc(k["ytc"], 1)

                    def turn(i, first, last_turn):
                        act.wait_ge(k["expin"], i + 1)
                        act.activation(MX[:], MX[:], ACT.Exp).then_inc(k["expd"], 1)
                        if not first:
                            output_out(i - 1)
                        if not last_turn:
                            square(i + 1)
                            scores_out(i + 1)

                    def before():
                        square(0)
                        scores_out(0)

                    pipelined(act, before, turn, lambda: output_out(TILES - 1))

                @block.vector
                def _(dve):
                    def turn_heads(i):
                        dve.wait_ge(k["pad"], i + 1)
                        at_least(dve, k["score"], i)
                        dve.transpose(QKT[:, 0:2 * H, :], QK[:, 0:2 * H, :]).then_inc(k["qkt"], 1)

                    def compact(i):
                        st = Steps(dve, k["sc2"], 1, i)
                        dve.wait_ge(k["sq"], i + 1)
                        at_least(dve, k["dt"], i)
                        dc = DC[:].rearrange("p (h j) -> p h j", j=SEQ)
                        sq = SQ[:].rearrange("p (h a) j -> p h a j", a=2)
                        st.link(dve.tensor_scalar(dc, sq[:, :, 0, :], l2_scale[:, 1:2], None, ALU.mult))
                        dve.scalar_tensor_tensor(dc, sq[:, :, 1, :], l2_scale[:, 2:3], dc, ALU.mult, ALU.add).then_inc(k["dc"], 1)
                        st.end()

                    def add_output(i):
                        dve.wait_ge(k["proj"], i + 1)
                        xi = X[:, bass.ds(i, 1), :]
                        dve.tensor_tensor(xi, PS[:, OB:OB + 1, 0:D], xi, ALU.add).then_inc(k["added"], 1)

                    def turn(i, first, last_turn):
                        if not last_turn:
                            turn_heads(i + 1)
                        st = Steps(dve, k["dve2"], 5, i)
                        dve.wait_ge(k["mixed"], i + 1)
                        mx = PS[:, MB, 0:D].rearrange("p (h j) -> p h j", j=SEQ)
                        st.link(dve.tensor_reduce(smax[:], mx, AX.X, ALU.max))
                        dve.tensor_tensor(MX[:], mx, spread(smax[:], SEQ), ALU.subtract).then_inc(k["expin"], 1)
                        dve.wait_ge(k["expd"], i + 1)
                        at_least(dve, k["pt"], i)
                        st.link(dve.tensor_scalar(S[:, :, 0:SEQ], MX[:], half01[:, 0:1], None, ALU.mult))
                        st.link(dve.tensor_scalar(S[:, :, SEQ:GROUP], MX[:], half01[:, 1:2], None, ALU.mult))
                        dve.transpose(PT[:], S[:]).then_inc(k["pt"], 1)
                        if not last_turn:
                            compact(i + 1)
                        st.link(dve.tensor_reduce(rsum[:], MX[:], AX.X, ALU.add))
                        st.link(dve.reciprocal(rinv[:], rsum[:]))
                        if not first:
                            add_output(i - 1)
                        dve.wait_ge(k["pv"], i + 1)
                        at_least(dve, k["yt"], i)
                        dve.tensor_tensor(Y[:].rearrange("p (h d) -> p h d", d=HD),
                                          PS[:, YB, 0:D].rearrange("p (h d) -> p h d", d=HD),
                                          spread(rinv[:], HD), ALU.mult).then_inc(k["yn"], 1)
                        st.end()

                    def before():
                        turn_heads(0)
                        compact(0)

                    def after():
                        add_output(TILES - 1)
                        dve.wait_ge(k["added"], TILES)

                    pipelined(dve, before, turn, after)

        def quantised_ffn():
            big = local("hidden", [P, FC, TOKENS])
            am, amt, diag, sc = local("am", [P, 2]), local("amt", [2, 1]), local("diag", [2, 2]), local("wscale", [P, 4])
            inv, both = local("wscale_inv", [P, 4]), local("wscale_both", [P, 1])
            w1q = local("ff_w1q", [KC, 2, FF], FP32R)
            w2q = local("ff_w2q", [P, FC, D], BF16)
            hq = local("ff_hq", [P, FC, TOKENS], BF16)
            xh, xl = local("ff_xh", [KC, 2, TOKENS], FP32R), local("ff_xl", [KC, 2, TOKENS], FP32R)
            ones2 = local("ones2", [2, P])
            fy = local("fy", [P, PAIRS, 2 * D])
            k = {n: sem("ff_" + n) for n in ("dve", "am", "amt", "diag", "scales", "w1b", "w1q", "w2b", "w2q", "hid", "gelu",
                                             "hb", "hq", "y", "yb", "yq", "zero", "xh", "xl", "done")}
            with nc.Block() as block:
                @block.gpsimd
                def _(pool):
                    pool.memset(am[:], 0.0).then_inc(k["zero"], 1)
                    pool.wait_ge(k["zero"], 1)
                    pool.memset(ones2[:], 1.0).then_inc(k["zero"], 1)
                    pool.wait_ge(k["zero"], 2)
                    pool.wait_ge(k["xh"], 1)
                    pool.tensor_tensor(xl[:], XT[0:KC, :, :], xh[:], ALU.subtract).then_inc(k["xl"], 1)
                    pool.wait_ge(k["xl"], 1)

                @block.tensor
                def _(pe):
                    landed(pe, "ident")
                    pe.wait_ge(k["am"], 2)
                    pe.transpose(PS[0:2, 7, 0:P], am[:], ident[:]).then_inc(k["amt"], 1)
                    pe.wait_ge(k["diag"], 1)
                    pe.matmul(PS[:, 6, 0:2], ones2[:], diag[:], start=True, stop=True).then_inc(k["scales"], 1)
                    pe.wait_ge(k["w1q"], 1)
                    pe.wait_ge(k["xl"], 1)
                    n = 0
                    for f in range(FC):
                        for half in range(2):
                            if n >= 4:
                                pe.wait_ge(k["gelu"], n - 3)
                            terms = [(c, x) for x in (xh, xl) for c in range(2)]
                            for m, (c, x) in enumerate(terms):
                                last = pe.matmul(PS[:, n % 4, :], w1q[:, c, f * P:(f + 1) * P],
                                                 x[:, c, half * BANK:(half + 1) * BANK],
                                                 start=(m == 0), stop=(m == len(terms) - 1))
                            last.then_inc(k["hid"], 1)
                            n += 1
                    pe.wait_ge(k["w2q"], 1)
                    pe.wait_ge(k["hq"], 2 * FC)
                    for m in range(PAIRS):
                        for t in range(2):
                            for f in range(FC):
                                last = pe.matmul(PS[:, 4 + m, t * D:(t + 1) * D], hq[:, f, (2 * m + t) * P:(2 * m + t + 1) * P],
                                                 w2q[:, f, :], start=(f == 0), stop=(f == FC - 1))
                        last.then_inc(k["y"], 1)

                @block.scalar
                def _(act):
                    landed(act, "ff_b1")
                    act.activation(xh[:], XT[0:KC, :, :], ACT.Copy).then_inc(k["xh"], 1)

                    def less_magic(dst, src, ready, count, done):
                        act.wait_ge(ready, count)
                        act.activation(dst, src, ACT.Copy, bias=-MAGIC).then_inc(done, 1)

                    def hidden_chunk(n):
                        return slice(None), n // 2, slice(n % 2 * BANK, (n % 2 + 1) * BANK)

                    less_magic(w1q[:], ff_w1[:], k["w1b"], 1, k["w1q"])
                    for n in range(2 * FC):
                        act.wait_ge(k["hid"], n + 1)
                        f = n // 2
                        act.activation(big[hidden_chunk(n)], PS[:, n % 4, :], ACT.Gelu,
                                       bias=ff_b1[:, f:f + 1], scale=sc[:, 0:1]).then_inc(k["gelu"], 1)
                        if n == 0:
                            less_magic(w2q[:], ff_w2[:], k["w2b"], 1, k["w2q"])
                        else:
                            less_magic(hq[hidden_chunk(n - 1)], big[hidden_chunk(n - 1)], k["hb"], n, k["hq"])
                    less_magic(hq[hidden_chunk(n)], big[hidden_chunk(n)], k["hb"], n + 1, k["hq"])
                    for m in range(PAIRS):
                        less_magic(fy[:, m, :], fy[:, m, :], k["yb"], m + 1, k["yq"])

                @block.vector
                def _(dve):
                    st = Steps(dve, k["dve"])
                    landed(dve, "ff_w1", "ff_w2", "ff_s", "ff_b2", "ident")
                    dve.wait_ge(k["zero"], 2)
                    dve.tensor_reduce(am[0:KC, 0:1], ff_w1[:], AX.XY, ALU.max, apply_absolute_value=True).then_inc(k["am"], 1)
                    dve.tensor_reduce(am[:, 1:2], ff_w2[:], AX.XY, ALU.max, apply_absolute_value=True).then_inc(k["am"], 1)
                    dve.wait_ge(k["amt"], 1)
                    st.link(dve.tensor_reduce(amt[:], PS[0:2, 7, 0:P], AX.X, ALU.max))
                    dve.tensor_scalar(diag[:], ident[0:2, 0:2], amt[:], None, ALU.mult).then_inc(k["diag"], 1)
                    dve.wait_ge(k["scales"], 1)
                    st.link(dve.tensor_scalar(sc[:, 0:2], PS[:, 6, 0:2], 1.0 / 127.0, None, ALU.mult))
                    st.link(dve.tensor_copy(sc[:, 2:4], ff_s[:]))
                    st.link(dve.reciprocal(inv[:], sc[:]))

                    def rounded(dst, src, n, low, done):
                        st.link(dve.tensor_scalar(dst, src, inv[0:dst.shape[0], n:n + 1], 127.0, ALU.mult, ALU.min))
                        dve.tensor_scalar(dst, dst, low, MAGIC, ALU.max, ALU.add).then_inc(done, 1)

                    rounded(ff_w1[:], ff_w1[:], 0, -127.0, k["w1b"])
                    rounded(ff_w2[:], ff_w2[:], 1, -127.0, k["w2b"])
                    st.link(dve.tensor_tensor(both[:], sc[:, 1:2], sc[:, 2:3], ALU.mult))
                    for n in range(2 * FC):
                        dve.wait_ge(k["gelu"], n + 1)
                        h = big[:, n // 2, n % 2 * BANK:(n % 2 + 1) * BANK]
                        rounded(h, h, 2, -128.0, k["hb"])

                    def add(m):
                        dve.wait_ge(k["yq"], m + 1)
                        xm = X[:, 2 * m:2 * m + 2, :]
                        dve.scalar_tensor_tensor(xm, fy[:, m, :].rearrange("p (t d) -> p t d", t=2), sc[:, 3:4], xm,
                                                 ALU.mult, ALU.add).then_inc(k["done"], 1)

                    for m in range(PAIRS):
                        dve.wait_ge(k["y"], m + 1)
                        y = fy[:, m, :].rearrange("p (t d) -> p t d", t=2)
                        st.link(dve.scalar_tensor_tensor(y, PS[:, 4 + m, 0:2 * D].rearrange("p (t d) -> p t d", t=2), both[:],
                                                         spread_mid(ff_b2[:], 2), ALU.mult, ALU.add))
                        rounded(fy[:, m, :], fy[:, m, :], 3, -128.0, k["yb"])
                        if m > 0:
                            add(m - 1)
                    add(PAIRS - 1)
                    dve.wait_ge(k["done"], PAIRS)

        def gates(name, wg, wname, ncol, kind):
            k = {n: sem(f"{name}_{n}") for n in ("dve", "logits", "less", "exp")}
            soft = {"heads": ((0, 10), (10, 12), (12, 14)), "moe": ((0, E),), "shared": ((0, E),)}[kind]
            ne = soft[0][1]
            with nc.Block() as block:
                @block.tensor
                def _(pe):
                    landed(pe, wname)
                    for t in range(TILES):
                        for c in range(2):
                            last = pe.matmul(PS[:, 7, t * ncol:(t + 1) * ncol], XT[:, c, t * P:(t + 1) * P], wg[:, c, :],
                                             start=(c == 0), stop=(c == 1), skip_group_check=True)
                    last.then_inc(k["logits"], 1)

                @block.scalar
                def _(act):
                    act.wait_ge(k["less"], 1)
                    act.activation(GA[:, :, 0:ncol], GL[:, :, 0:ncol], ACT.Exp).then_inc(k["exp"], 1)

                @block.vector
                def _(dve):
                    landed(dve, "iota10")
                    st = Steps(dve, k["dve"])
                    dve.wait_ge(k["logits"], 1)
                    st.link(dve.tensor_copy(GL[:, :, 0:ncol], PS[:, 7, 0:TILES * ncol].rearrange("p (t e) -> p t e", t=TILES)))
                    for a, b in soft:
                        st.link(dve.tensor_reduce(gm[:, :, 0], GL[:, :, a:b], AX.X, ALU.max))
                        st.link(dve.tensor_tensor(GL[:, :, a:b], GL[:, :, a:b], spread(gm[:, :, 0], b - a), ALU.subtract))
                    if kind == "shared":
                        st.link(dve.tensor_scalar(GL[:, :, E], GL[:, :, E], -1.0, None, ALU.mult))
                    st.link(dve.tensor_scalar(GB[:, :, 0:1], GL[:, :, 0:1], 1.0, None, ALU.mult))
                    dve.sem_inc(k["less"], 1)
                    dve.wait_ge(k["exp"], 1)
                    for a, b in soft:
                        st.link(dve.tensor_reduce(gs_[:, :, 0], GA[:, :, a:b], AX.X, ALU.add))
                        st.link(dve.reciprocal(gm[:], gs_[:]))
                        st.link(dve.tensor_tensor(GA[:, :, a:b], GA[:, :, a:b], spread(gm[:, :, 0], b - a), ALU.mult))
                    for t in range(TILES):
                        dve.max(top8[:, t, :], GA[:, t, 0:ne]).then_inc(k["dve"], 1)
                    st.n += TILES
                    dve.wait_ge(k["dve"], st.n)
                    for t in range(TILES):
                        dve.max_index(topi[:, t, :], top8[:, t, :], GA[:, t, 0:ne]).then_inc(k["dve"], 1)
                    st.n += TILES
                    dve.wait_ge(k["dve"], st.n)
                    st.link(dve.tensor_copy(topf[:], topi[:]))
                    for t in range(TILES):
                        dve.scalar_tensor_tensor(GL[:, t, 0:ne], iota10[:, 0:ne], topf[:, t, 0:1], GA[:, t, 0:ne],
                                                 ALU.is_equal, ALU.mult).then_inc(k["dve"], 1)
                        dve.scalar_tensor_tensor(GB[:, t, 0:ne], iota10[:, 0:ne], topf[:, t, 1:2], GA[:, t, 0:ne],
                                                 ALU.is_equal, ALU.mult).then_inc(k["dve"], 1)
                    st.n += 2 * TILES
                    dve.wait_ge(k["dve"], st.n)
                    st.link(dve.tensor_tensor(GL[:, :, 0:ne], GL[:, :, 0:ne], GB[:, :, 0:ne], ALU.add))
                    if kind == "moe":
                        st.link(dve.tensor_copy(G[:, :, 0:E], GL[:, :, 0:E]))
                        return
                    st.link(dve.tensor_reduce(gs_[:, :, 0], GL[:, :, 0:ne], AX.X, ALU.add))
                    if kind == "heads":
                        eps = float(np.finfo(np.float32).eps)
                        st.link(dve.tensor_scalar(gs_[:], gs_[:], eps, None, ALU.max))
                    st.link(dve.reciprocal(gm[:], gs_[:]))
                    if kind == "heads":
                        st.link(dve.tensor_scalar(GA[:, :, 12:14], GA[:, :, 12:14], 4.0, None, ALU.mult))
                        st.link(dve.tensor_tensor(gm[:, :, 0], gm[:, :, 0], GA[:, :, 13], ALU.mult))
                        st.link(dve.tensor_tensor(G[:, :, 2:H], GL[:, :, 0:10], spread(gm[:, :, 0], 10), ALU.mult))
                        st.link(dve.tensor_tensor(G[:, :, 0:2], GA[:, :, 10:12], spread(GA[:, :, 12], 2), ALU.mult))
                    else:
                        st.link(dve.tensor_scalar(gs_[:, :, 0], GA[:, :, E], 1.0, None, ALU.add))
                        st.link(dve.reciprocal(GB[:, :, 0:1], gs_[:]))
                        st.link(dve.tensor_copy(G[:, :, E:H], spread(GB[:, :, 0], H - E)))
                        st.link(dve.tensor_scalar(GB[:, :, 1], GB[:, :, 0], -1.0, 1.0, ALU.mult, ALU.add))
                        st.link(dve.tensor_tensor(gm[:, :, 0], gm[:, :, 0], GB[:, :, 1], ALU.mult))
                        st.link(dve.tensor_tensor(G[:, :, 0:E], GL[:, :, 0:E], spread(gm[:, :, 0], E), ALU.mult))

        def expert_bias():
            k = {n: sem("eb_" + n) for n in ("gx", "gt", "gtc", "b", "done")}
            with nc.Block() as block:
                @block.tensor
                def _(pe):
                    landed(pe, "ident", "moe_b2")
                    for t in range(TILES):
                        last = pe.transpose(PS[0:E, t // 4, (t % 4) * P:(t % 4 + 1) * P], G[:, t, 0:E], ident[:])
                    last.then_inc(k["gt"], 1)
                    pe.wait_ge(k["gtc"], 2)
                    for t in range(TILES):
                        last = pe.matmul(PS[:, 2 + t // 2, (t % 2) * D:(t % 2 + 1) * D], GT[:, t * P:(t + 1) * P], moe_b2[:],
                                         start=True, stop=True)
                    last.then_inc(k["b"], 1)

                @block.scalar
                def _(act):
                    act.wait_ge(k["gt"], 1)
                    for b in range(2):
                        act.activation(GT[:, b * BANK:(b + 1) * BANK], PS[0:E, b, :], ACT.Copy).then_inc(k["gtc"], 1)
                    act.wait_ge(k["gtc"], 2)

                @block.vector
                def _(dve):
                    dve.tensor_copy(GX[:, 0:E, :].rearrange("p e t -> p t e"), G[:, :, 0:E]).then_inc(k["gx"], 1)
                    dve.wait_ge(k["b"], 1)
                    for m in range(PAIRS):
                        xm = X[:, 2 * m:2 * m + 2, :]
                        dve.tensor_tensor(xm, PS[:, 2 + m, 0:2 * D].rearrange("p (t d) -> p t d", t=2), xm,
                                          ALU.add).then_inc(k["done"], 1)
                    dve.wait_ge(k["done"], PAIRS)
                    dve.wait_ge(k["gx"], 1)

        HALF_TILES = TILES // 2

        def hidden_product(pe, bank, wh, wl, columns, half):
            n = slice(half * BANK, (half + 1) * BANK)
            pe.matmul(PS[:, bank, :], wh[:, 0, columns], XH[:, 0, n], start=True, stop=False)
            pe.matmul(PS[:, bank, :], wh[:, 0, columns], XL[:, n], start=False, stop=False)
            pe.matmul(PS[:, bank, :], wh[:, 1, columns], XH[:, 1, n], start=False, stop=False)
            pe.matmul(PS[:, bank, :], wl[:, 0, columns], XH[:, 0, n], start=False, stop=False)
            return pe.matmul(PS[:, bank, :], wl[0:KR, 1, columns], XH[0:KR, 1, n], start=False, stop=True)

        def load_set(sp, e, j, base):
            w1, w2 = base["names"]
            sp.dma_start(raw1[j][:].unsqueeze(1), I[w1].rearrange("e p n -> p e n")[:, bass.ds(e, 1)]).then_inc(in1[j], 16)
            n = base["second"]
            sp.dma_start(raw2[j][:, 0:n].unsqueeze(1), I[w2].rearrange("e p n -> p e n")[:, bass.ds(e, 1)]).then_inc(in2[j], 16)

        def load_weights(sp, base, k):
            with sp.Fori(1, base["sets"] // 2) as i:
                for j in range(2):
                    sp.wait_ge(k["low_w"], i * 4 + 2 * j - 2)
                    load_set(sp, i * 2 + j, j, base)

        def leading_parts(act, i, j, k, parts, base):
            wh1, _, wh2, _ = parts[j]
            own(act, in1[j], (i + 1) * 16 + base["in"])
            act.activation(wh1[:].rearrange("p c n -> p (c n)"), raw1[j][:], ACT.Copy).then_inc(k["high_w"], 1)
            own(act, in2[j], (i + 1) * 16 + base["in"])
            act.activation(wh2[:].rearrange("p c n -> p (c n)"), raw2[j][:, 0:base["second"]], ACT.Copy).then_inc(k["high_w"], 1)

        def split_weights(pool, base, k, parts):
            with pool.Fori(0, base["sets"] // 2) as i:
                for j in range(2):
                    wh1, wl1, wh2, wl2 = parts[j]
                    own(pool, k["high_w"], i * 4 + 2 * j + 1)
                    pool.tensor_tensor(wl1[:].rearrange("p c n -> p (c n)"), raw1[j][:], wh1[:].rearrange("p c n -> p (c n)"),
                                       ALU.subtract).then_inc(k["low_w"], 1)
                    own(pool, k["low_w"], i * 4 + 2 * j + 1)
                    own(pool, k["high_w"], i * 4 + 2 * j + 2)
                    pool.tensor_tensor(wl2[:].rearrange("p c n -> p (c n)"), raw2[j][:, 0:base["second"]],
                                       wh2[:].rearrange("p c n -> p (c n)"), ALU.subtract).then_inc(k["low_w"], 1)
                    own(pool, k["low_w"], i * 4 + 2 * j + 2)

        def gelu_experts():
            k = {n: sem("moe_" + n) for n in ("high_w", "low_w", "hid", "gelu", "low", "y", "sum")}
            parts = [(local(f"moe_wh1_{j}", [P, 2, FF], FP32R), local(f"moe_wl1_{j}", [P, 2, FF], FP32R),
                      local(f"moe_wh2_{j}", [P, FC, D], FP32R), local(f"moe_wl2_{j}", [P, FC, D], FP32R)) for j in range(2)]
            hF = local("moe_hf", [P, 2, BANK])
            hH, hL = (local(n, [P, 2, FC, BANK], FP32R) for n in ("moe_hh", "moe_hl"))
            steps = [(j, half) for j in range(2) for half in range(2)]
            NS = len(steps)
            with nc.Block() as block:
                @block.sync
                def _(sp):
                    load_weights(sp, moe, k)

                @block.gpsimd
                def _(pool):
                    split_weights(pool, moe, k, parts)

                @block.tensor
                def _(pe):
                    pe.sem_inc(k["y"], 3)
                    with pe.Fori(0, E // 2) as i:
                        def hidden(n):
                            j, half = steps[n]
                            if half == 0:
                                own(pe, k["low_w"], i * 4 + j * 2 + 1)
                            for f in range(FC):
                                own(pe, k["gelu"], (i * (NS * FC) + n * FC + f + 1) * 2)
                                hidden_product(pe, (n * FC + f) % 4, parts[j][0], parts[j][1],
                                               slice(f * P, (f + 1) * P), half).then_inc(k["hid"], 1)

                        def second(n):
                            j, half = steps[n]
                            if half == 0:
                                own(pe, k["low_w"], i * 4 + j * 2 + 2)
                            own(pe, k["low"], i * (NS * FC) + (n + 1) * FC + 2)
                            own(pe, k["sum"], i * (NS * HALF_TILES) + (n + 1) * HALF_TILES)
                            for t in range(HALF_TILES):
                                terms = [(h, w, f) for f in range(FC) for h, w in (
                                    (hH, parts[j][2]), (hH, parts[j][3]), (hL, parts[j][2]))]
                                for m, (h, w, f) in enumerate(terms):
                                    last = pe.matmul(PS[:, 4 + 2 * half + t // 2, (t % 2) * D:(t % 2 + 1) * D],
                                                     h[:, half, f, t * P:(t + 1) * P], w[:, f, :],
                                                     start=(m == 0), stop=(m == len(terms) - 1))
                            last.then_inc(k["y"], 1)

                        hidden(0)
                        for n in range(1, NS):
                            hidden(n)
                            second(n - 1)
                        second(NS - 1)

                @block.scalar
                def _(act):
                    landed(act, "moe_b1")
                    act.sem_inc(k["gelu"], 8)

                    def turn(i, last_turn):
                        for n, (j, half) in enumerate(steps):
                            own(act, k["y"], i * NS + n + 2)
                            if half == 1 and not (last_turn and j == 1):
                                leading_parts(act, i + j, 1 - j, k, parts, moe)
                            for f in range(FC):
                                act.wait_ge(k["hid"], i * (NS * FC) + n * FC + f + 1)
                                own(act, k["low"], i * (NS * FC) + n * FC + f + 1)
                                for dst in (hF[:, f % 2, :], hH[:, half, f, :]):
                                    act.activation(dst, PS[:, (n * FC + f) % 4, :], ACT.Gelu,
                                                   bias=moe_b1[:, bass.ds(i * 2 + j, 1), f]).then_inc(k["gelu"], 1)

                    leading_parts(act, 0, 0, k, parts, moe)
                    with act.Fori(0, E // 2 - 1) as i:
                        turn(i, False)
                    turn(E // 2 - 1, True)

                @block.vector
                def _(dve):
                    dve.sem_inc(k["sum"], 2 * HALF_TILES)
                    dve.sem_inc(k["low"], 2)
                    with dve.Fori(0, E // 2) as i:
                        def low(n):
                            half = steps[n][1]
                            for f in range(FC):
                                dve.wait_ge(k["gelu"], (i * (NS * FC) + n * FC + f + 5) * 2)
                                dve.tensor_tensor(hL[:, half, f, :], hF[:, f % 2, :], hH[:, half, f, :],
                                                  ALU.subtract).then_inc(k["low"], 1)

                        def add(n):
                            j, half = steps[n]
                            dve.wait_ge(k["y"], i * NS + n + 4)
                            own(dve, k["sum"], i * (NS * HALF_TILES) + (n + 2) * HALF_TILES)
                            for t in range(HALF_TILES):
                                xt = X[:, half * HALF_TILES + t, :]
                                dve.scalar_tensor_tensor(xt, PS[:, 4 + 2 * half + t // 2, (t % 2) * D:(t % 2 + 1) * D],
                                                         GX[:, bass.ds(i * 2 + j, 1), half * HALF_TILES + t], xt, ALU.mult,
                                                         ALU.add).then_inc(k["sum"], 1)

                        low(0)
                        for n in range(1, NS):
                            low(n)
                            add(n - 1)
                        add(NS - 1)
                    dve.wait_ge(k["sum"], (E * 2 + 2) * HALF_TILES)

        def silu_experts():
            k = {n: sem("glu_" + n) for n in ("high_w", "low_w", "hid", "silu", "h", "y", "sum", "gx")}
            PAIRED = glu["sets"]
            NT = 3
            parts = [(local(f"glu_wh1_{j}", [P, 2, FF], FP32R), local(f"glu_wl1_{j}", [P, 2, FF], FP32R),
                      local(f"glu_wh2_{j}", [P, NT, D], FP32R), local(f"glu_wl2_{j}", [P, NT, D], FP32R)) for j in range(2)]
            sg = local("glu_sg", [P, 2, BANK])
            hF = local("glu_hf", [P, 2, BANK])
            hH, hL = (local(n, [P, 2, NT, BANK], FP32R) for n in ("glu_hh", "glu_hl"))
            steps = [(j, half) for j in range(2) for half in range(2)]
            NS = len(steps)
            rows_of = [((0, slice(0, P)), (2, slice(0, KR))), ((1, slice(0, P)), (2, slice(KR, P)))]
            SUMS = 2 * HALF_TILES
            with nc.Block() as block:
                @block.sync
                def _(sp):
                    load_weights(sp, glu, k)

                @block.gpsimd
                def _(pool):
                    split_weights(pool, glu, k, parts)

                @block.tensor
                def _(pe):
                    pe.sem_inc(k["y"], 3)
                    with pe.Fori(0, PAIRED // 2) as i:
                        def hidden(n):
                            j, half = steps[n]
                            if half == 0:
                                own(pe, k["low_w"], i * 4 + j * 2 + 1)
                            for u in range(NT):
                                own(pe, k["h"], (i * (NS * NT) + n * NT + u + 1) * 3)
                                for which in range(2):
                                    last = hidden_product(pe, 2 * ((n * NT + u) % 2) + which, parts[j][0], parts[j][1],
                                                          slice((2 * u + which) * P, (2 * u + which + 1) * P), half)
                                last.then_inc(k["hid"], 1)

                        def second(n):
                            j, half = steps[n]
                            if half == 0:
                                own(pe, k["low_w"], i * 4 + j * 2 + 2)
                            own(pe, k["h"], (i * (NS * NT) + (n + 1) * NT + 2) * 3)
                            for e in range(2):
                                terms = [(h, w, b) for b in rows_of[e] for h, w in (
                                    (hH, parts[j][2]), (hH, parts[j][3]), (hL, parts[j][2]))]
                                for t in range(HALF_TILES):
                                    if t % 2 == 0:
                                        own(pe, k["sum"], i * (NS * SUMS) + n * SUMS + e * HALF_TILES + t + 2)
                                    for m, (h, w, (b, r)) in enumerate(terms):
                                        last = pe.matmul(PS[:, 4 + 2 * e + t // 2, (t % 2) * D:(t % 2 + 1) * D],
                                                         h[r, half, b, t * P:(t + 1) * P], w[r, b, :],
                                                         start=(m == 0), stop=(m == len(terms) - 1))
                            last.then_inc(k["y"], 1)

                        hidden(0)
                        for n in range(1, NS):
                            hidden(n)
                            second(n - 1)
                        second(NS - 1)

                @block.scalar
                def _(act):
                    def turn(i, last_turn):
                        for n, (j, half) in enumerate(steps):
                            if half == 1 and not (last_turn and j == 1):
                                own(act, k["y"], i * NS + n + 2)
                                leading_parts(act, i + j, 1 - j, k, parts, glu)
                            for u in range(NT):
                                act.wait_ge(k["hid"], i * (NS * NT) + n * NT + u + 1)
                                b = (n * NT + u) % 2
                                act.activation(sg[:, b, :], PS[:, 2 * b, :], ACT.Silu).then_inc(k["silu"], 1)

                    leading_parts(act, 0, 0, k, parts, glu)
                    with act.Fori(0, PAIRED // 2 - 1) as i:
                        turn(i, False)
                    turn(PAIRED // 2 - 1, True)

                @block.vector
                def _(dve):
                    dve.tensor_copy(GX[:].rearrange("p e t -> p t e"), G[:]).then_inc(k["gx"], 1)
                    dve.wait_ge(k["gx"], 1)
                    dve.sem_inc(k["h"], 6)
                    dve.sem_inc(k["sum"], SUMS)
                    with dve.Fori(0, PAIRED // 2) as i:
                        def product(n):
                            half = steps[n][1]
                            dve.wait_ge(k["y"], i * NS + n + 2)
                            for u in range(NT):
                                b = (n * NT + u) % 2
                                c = i * (NS * NT) + n * NT + u
                                dve.wait_ge(k["silu"], c + 1)
                                up = PS[:, 2 * b + 1, :]
                                dve.tensor_tensor(hF[:, b, :], up, sg[:, b, :], ALU.mult).then_inc(k["h"], 1)
                                dve.tensor_tensor(hH[:, half, u, :], up, sg[:, b, :], ALU.mult).then_inc(k["h"], 1)
                                dve.wait_ge(k["h"], c * 3 + 8)
                                dve.tensor_tensor(hL[:, half, u, :], hF[:, b, :], hH[:, half, u, :],
                                                  ALU.subtract).then_inc(k["h"], 1)

                        def add(n):
                            j, half = steps[n]
                            dve.wait_ge(k["y"], i * NS + n + 4)
                            for e in range(2):
                                if e == 0:
                                    own(dve, k["sum"], i * (NS * SUMS) + (n + 1) * SUMS)
                                else:
                                    own(dve, k["sum"], i * (NS * SUMS) + (n + 1) * SUMS + HALF_TILES)
                                for t in range(HALF_TILES):
                                    xt = X[:, half * HALF_TILES + t, :]
                                    dve.scalar_tensor_tensor(xt, PS[:, 4 + 2 * e + t // 2, (t % 2) * D:(t % 2 + 1) * D],
                                                             GX[:, bass.ds(i * 4 + j * 2 + e, 1), half * HALF_TILES + t], xt,
                                                             ALU.mult, ALU.add).then_inc(k["sum"], 1)

                        product(0)
                        for n in range(1, NS):
                            product(n)
                            add(n - 1)
                        add(NS - 1)
                    dve.wait_ge(k["sum"], SUMS * (2 * PAIRED + 1))

        def store():
            stored = sem("stored")
            with nc.Block() as block:
                @block.sync
                def _(sp):
                    landed(sp, *plan)
                    sp.dma_start(out.rearrange("(t p) d -> p t d", p=P), X[:]).then_inc(stored, 16)
                    sp.wait_ge(stored, 16)

        if stop == 0:
            return store()
        attention("l0", l0_qkv, l0_proj, ("l0_qkv", "l0_proj"), mask_causal, causal_rel=True)
        end_phase()
        norm_and_transpose("n0")
        end_phase()
        if stop == 1:
            return store()
        quantised_ffn()
        end_phase()
        norm_and_transpose("n1")
        end_phase()
        if stop == 2:
            return store()
        w_qkvh, w_qkvl = (early.enter_context(nc.sbuf_tensor(n, [KB, 2, 3 * H * WD], FP32R)) for n in ("w_qkvh", "w_qkvl"))
        attention("l1", l1_qkv, l1_proj, ("l1_qkv", "l1_proj"), mask_block, head_norm=True)
        end_phase()
        norm_and_transpose("n2")
        end_phase()
        if stop == 3:
            return store()
        gates("heads", w_gates, "w_gates", 14, "heads")
        end_phase()
        wide_attention()
        end_phase()
        early.close()
        raw1 = [sb(f"raw1_{j}", [P, 2 * FF]) for j in range(2)]
        raw2 = [sb(f"raw2_{j}", [P, FC * D]) for j in range(2)]
        in1, in2 = ([lasting(f"in_raw{n}_{j}") for j in range(2)] for n in (1, 2))
        moe = dict(names=("moe_w1", "moe_w2"), sets=E, second=FC * D)
        moe["in"] = 0
        glu = dict(names=("gu", "down"), sets=H // 2, second=3 * D)
        glu["in"] = moe["sets"] // 2 * 16
        norm_and_transpose("n3")
        end_phase()
        if stop == 4:
            return store()
        grassmann_attention()
        end_phase()
        norm_and_transpose("n4", split=moe)
        end_phase()
        if stop == 5:
            return store()
        gates("moe", moe_g, "moe_g", E, "moe")
        end_phase()
        expert_bias()
        end_phase()
        gelu_experts()
        end_phase()
        norm_and_transpose("n5")
        end_phase()
        if stop == 6:
            return store()
        attention("l3", l3_qkv, l3_proj, ("l3_qkv", "l3_proj"), mask_block, quantum=True)
        end_phase()
        norm_and_transpose("n6", split=glu)
        end_phase()
        if stop == 7:
            return store()
        gates("shared", l3_gates, "l3_gates", E + 1, "shared")
        end_phase()
        silu_experts()
        end_phase()
        norm_and_transpose("n7", transpose=False)
        end_phase()
        return store()


def lay_out(a):
    f = np.float32

    def chunks(w, b=None):
        m = w.shape[1]
        r = np.zeros((KB, 2, m), f)
        r[:KC, 0], r[:KC, 1] = w[:KC], w[KC:]
        if b is not None:
            r[KC, 0] = b
        return r

    def rows(w):
        return np.ascontiguousarray(w.reshape(-1, P, w.shape[1]).transpose(1, 0, 2))

    def every(v):
        return np.ascontiguousarray(np.broadcast_to(np.reshape(v, (1, -1)), (P, np.size(v))))

    x = a["x"].reshape(IMAGES, 4, 16, 4, 16, 3).transpose(0, 1, 3, 2, 4, 5).reshape(TOKENS, FF)
    o = {"patches": rows(np.ascontiguousarray(x.T))}
    o["tok_w"] = rows(a["L0_tok_W"])
    o["pos"] = np.tile(a["L0_tok_pos_emb"], (P // SEQ, 1))
    o["tok_b"] = every(a["L0_tok_b"])
    o["ident"] = np.eye(P, dtype=f)
    n = np.arange(P)[:, None]
    j = np.arange(GROUP)[None, :]
    same = (n % GROUP) // SEQ == j // SEQ
    off = -30000.0
    block = np.where(same, 0.0, off)
    causal = np.where(same & (j % SEQ <= n % SEQ), 0.0, off)
    o["keys_causal"] = causal.astype(f)
    o["keys_block"] = block.astype(f)
    o["block01"] = same.astype(f)
    o["half01"] = np.concatenate([(n % GROUP < SEQ), (n % GROUP >= SEQ)], 1).astype(f)
    o["rel"] = np.tile(np.concatenate([np.zeros((1, HD), f), a["L0_attn_rel_emb"][:SEQ - 1]]), (P // SEQ, 1))
    o["l0_qkv"] = chunks(a["L0_attn_w_attn"], a["L0_attn_b_attn"])
    o["l0_proj"] = chunks(a["L0_attn_w_proj"], a["L0_attn_b_proj"])
    o["ff_w1"] = np.ascontiguousarray(a["L0_ffn_W1"].T.reshape(2, KC, FF).transpose(1, 0, 2))
    o["ff_b1"] = np.ascontiguousarray(a["L0_ffn_b1"].reshape(FC, P).T)
    o["ff_w2"] = rows(np.ascontiguousarray(a["L0_ffn_W2"].T))
    o["ff_b2"] = every(a["L0_ffn_b2"])
    o["ff_s"] = every(np.stack([np.reshape(a["L0_ffn_s_gelu"], ()), np.reshape(a["L0_ffn_s_out"], ())]))
    o["l1_qkv"] = chunks(a["L1_attn_qkv_weight"].T)
    o["l1_proj"] = chunks(a["L1_attn_proj_weight"].T)
    o["w_qkv"] = chunks(a["L1_ffn_qkv_w"], a["L1_ffn_qkv_b"])
    o["w_proj"] = rows(a["L1_ffn_proj_w"])
    o["w_projb"] = a["L1_ffn_proj_b"].reshape(1, D)
    o["w_gates"] = chunks(np.concatenate([a["L1_ffn_wg_w"], a["L1_ffn_wg1_w"], a["L1_ffn_wg0_w"]], 1))
    o["w_affine"] = np.stack([np.tile(a[k].reshape(2, GROUP)[d], NG) for k in (
        "L1_ffn_q_norm_w", "L1_ffn_q_norm_b", "L1_ffn_k_norm_w", "L1_ffn_k_norm_b") for d in range(2)], 1)
    o["iota10"] = np.broadcast_to(np.arange(10, dtype=f), (P, 10))
    o["l2_qkv"] = chunks(a["L2_attn_qkv_w"].T, a["L2_attn_qkv_b"])
    o["l2_proj"] = chunks(a["L2_attn_proj_w"].T, a["L2_attn_proj_b"])
    o["l2_scale"] = np.concatenate([every(a["L2_attn_grassman_scale"]), np.zeros((P, 2), f)], 1)

    def mixing(w, b):
        m = np.zeros((H, SEQ, H, SEQ), f)
        for key in range(SEQ):
            m[:, key, :, key] = w.T
        return chunks(m.reshape(D, D), b)

    o["mix_a"] = mixing(a["L2_attn_conv_w"][:, :H], np.repeat(a["L2_attn_conv_b"], SEQ))
    o["mix_b"] = mixing(a["L2_attn_conv_w"][:, H:], None)
    o["moe_g"] = chunks(a["L2_ffn_Wg"], a["L2_ffn_bg"])
    o["moe_b2"] = a["L2_ffn_b2"]

    def first_weights(w):
        return np.concatenate([w[:P], np.concatenate([w[P:], w[P:]])], 1)

    o["moe_w1"] = np.stack([first_weights(a["L2_ffn_W1"][e]) for e in range(E)])
    o["moe_b1"] = a["L2_ffn_b1"].reshape(E, FC, P).transpose(2, 0, 1)
    o["moe_w2"] = np.stack([rows(a["L2_ffn_W2"][e]).reshape(P, FC * D) for e in range(E)])
    o["l3_qkv"] = chunks(np.concatenate([a["L3_attn_in_w"].T[:, :2 * D], a["L3_attn_sp_w"].T, a["L3_attn_in_w"].T[:, 2 * D:]], 1),
                         np.concatenate([a["L3_attn_in_b"][:2 * D], a["L3_attn_sp_b"], a["L3_attn_in_b"][2 * D:]]))
    o["l3_proj"] = chunks(a["L3_attn_out_w"].T, a["L3_attn_out_b"])
    o["l3_qw"] = every(a["L3_attn_qw"])
    o["l3_gates"] = chunks(np.concatenate([a["L3_ffn_router_w"], a["L3_ffn_sg_w"]], 1),
                           np.concatenate([np.zeros(E, f), a["L3_ffn_sg_b"]]))
    gate = np.concatenate([a["L3_ffn_w_gate"], a["L3_ffn_ws_gate"].reshape(D, 4, D).transpose(1, 0, 2)])
    up = np.concatenate([a["L3_ffn_w_up"], a["L3_ffn_ws_up"].reshape(D, 4, D).transpose(1, 0, 2)])
    down = np.concatenate([a["L3_ffn_w_down"], a["L3_ffn_ws_down"].reshape(4, D, D)])
    pairs = [(e, e + 1) for e in range(0, H, 2)]
    o["gu"] = np.stack([first_weights(np.concatenate(
        [m[e][:, :P] for e in (c, d) for m in (gate, up)] + [m[e][:, P:] for m in (gate, up) for e in (c, d)], 1))
        for c, d in pairs])
    o["down"] = np.stack([rows(np.concatenate([down[c][:P], down[d][:P], down[c][P:], down[d][P:]])).reshape(P, 3 * D) for c, d in pairs])
    return {k: np.ascontiguousarray(v) for k, v in o.items()}


STOP = 99


def kernel(**inputs):
    import concourse.bacc as bacc
    from concourse.bass_utils import run_bass_kernel_spmd as run

    nc = bacc.Bacc("TRN2", target_bir_lowering=False, num_devices=1)
    laid = lay_out({k: np.asarray(v) for k, v in inputs.items()})
    arrays = {f"in_{k}": v for k, v in laid.items()}
    aps = {k: nc.dram_tensor(f"in_{k}", v.shape, mybir.dt.from_np(v.dtype), kind="ExternalInput").ap()
           for k, v in laid.items()}
    out = nc.dram_tensor("out_0", (TOKENS, D), FP32, kind="ExternalOutput").ap()
    vit_tower(nc, aps, out, STOP)
    r = run(nc, [arrays], core_ids=[0])
    return r.results[0]["out_0"].reshape(IMAGES, SEQ, D)
```
